# Optimizing a Trainium2 kernel written in Bass

```python
import numpy as np
import jax
import jax.numpy as jnp

def _softmax(x, axis=-1):
    return jax.nn.softmax(x, axis=axis)

def _gelu(x):
    return jax.nn.gelu(x, approximate=True)

def _silu(x):
    return jax.nn.silu(x)

def _sigmoid(x):
    return jax.nn.sigmoid(x)

def _layernorm(x, axis=-1, eps=1e-05):
    m = jnp.mean(x, axis=axis, keepdims=True)
    v = jnp.var(x, axis=axis, keepdims=True)
    return (x - m) / jnp.sqrt(v + eps)

def _scatter_add(tgt, idx, src, axis=0):
    return tgt.at[idx].add(src)

def _segment_sum(src, seg, n):
    return jax.ops.segment_sum(src, seg, n)
kernel_name = 'mk_audio_tower_d1_tok_audfeat512_r4_d92cd5'

def setup_inputs(seed: int=0):
    np.random.seed(seed)
    _w = jnp.asarray

    def _rec_inputs():
        import jax
        import jax.numpy as jnp
        _rk = jax.random.key(seed)
        x = -0.000392918 + 0.999932 * jax.random.normal(jax.random.fold_in(_rk, 1), (16, 750, 128), jnp.float32)
        return x
    x = _rec_inputs()

    def _L0_tok_setup():
        import jax, jax.numpy as jnp
        import numpy as np
        B, T, C = (8, 1024, 128)
        D = 512
        FACTOR = 2
        TEMP = 1e-05
        key = jax.random.key(seed)
        k = jax.random.split(key, 7)
        s = lambda fan: 1.0 / np.sqrt(fan)
        return {'features': jax.random.normal(k[0], (B, T, C), jnp.float32), 'W1': jax.random.normal(k[1], (C, D), jnp.float32) * s(C), 'b1': jnp.zeros((D,), jnp.float32), 'W2': jax.random.normal(k[2], (D, D), jnp.float32) * s(D), 'b2': jnp.zeros((D,), jnp.float32), 'W3': jax.random.normal(k[3], (D, 1), jnp.float32) * s(D), 'b3': jnp.zeros((1,), jnp.float32), 'factor': FACTOR}
    _L0_tok_all = _L0_tok_setup()
    _L0_tok_in = {k: v for k, v in _L0_tok_all.items() if k in ('W1', 'b1', 'W2', 'b2', 'W3', 'b3')}
    del _L0_tok_all

    def _L0_attn_setup():
        import jax, jax.numpy as jnp
        import numpy as np
        import math
        DIM = 128
        HEADS = 8
        DIM_HEAD = 64
        INNER = HEADS * DIM_HEAD
        B = 2
        N = 512

        def _alibi_slopes(heads):

            def pow2(n):
                start = 2 ** (-2 ** (-(math.log2(n) - 3)))
                return [start * start ** i for i in range(n)]
            if math.log2(heads).is_integer():
                return pow2(heads)
            cp2 = 2 ** math.floor(math.log2(heads))
            return pow2(cp2) + pow2(2 * cp2)[0::2][:heads - cp2]

        def _proj(xp, w1, wd):
            y = jnp.einsum('ed,bdn->ben', w1, xp)
            y = wd[None, :, 0:1] * y[..., :-2] + wd[None, :, 1:2] * y[..., 1:-1] + wd[None, :, 2:3] * y[..., 2:]
            return y

        def _split_heads(y, b, n):
            return y.reshape(b, HEADS, DIM_HEAD, n).transpose(0, 1, 3, 2)
        key = jax.random.key(seed)
        ks = jax.random.split(key, 9)
        s = 0.02
        return {'x': jax.random.normal(ks[0], (B, N, DIM), dtype=jnp.float32), 'gamma': jnp.ones((DIM,), jnp.float32), 'beta': jnp.zeros((DIM,), jnp.float32), 'wq1': jax.random.normal(ks[1], (INNER, DIM), jnp.float32) * s, 'wqd': jax.random.normal(ks[2], (INNER, 3), jnp.float32) * s, 'wk1': jax.random.normal(ks[3], (INNER, DIM), jnp.float32) * s, 'wkd': jax.random.normal(ks[4], (INNER, 3), jnp.float32) * s, 'wv1': jax.random.normal(ks[5], (INNER, DIM), jnp.float32) * s, 'wvd': jax.random.normal(ks[6], (INNER, 3), jnp.float32) * s, 'wout': jax.random.normal(ks[7], (DIM, INNER), jnp.float32) * s}
    _L0_attn_all = _L0_attn_setup()
    _L0_attn_in = {k: v for k, v in _L0_attn_all.items() if k in ('gamma', 'beta', 'wq1', 'wqd', 'wk1', 'wkd', 'wv1', 'wvd', 'wout')}
    del _L0_attn_all

    def _L0_ffn_setup():
        import jax, jax.numpy as jnp
        import numpy as np
        D, H, E, B, S = (128, 512, 16, 8, 2048)
        MAX_GROUP_SIZE = 1024
        MIN_CAPACITY = 8
        CAPACITY_FACTOR = 1.0

        def _group_dims(num_tokens, num_experts):
            num_groups = -(-num_tokens // MAX_GROUP_SIZE)
            while num_tokens % num_groups != 0 or num_groups % num_experts != 0:
                num_groups += 1
            return (num_tokens // num_groups, num_groups)
        key = jax.random.key(seed)
        ks = jax.random.split(key, 6)
        s = 0.02
        return {'x': jax.random.normal(ks[0], (B, S, D), jnp.float32), 'gate_w': jax.random.normal(ks[1], (D, E), jnp.float32) * s, 'w1': jax.random.normal(ks[2], (E, D, H), jnp.float32) * s, 'b1': jnp.zeros((E, H), jnp.float32), 'w2': jax.random.normal(ks[3], (E, H, D), jnp.float32) * s, 'b2': jnp.zeros((E, D), jnp.float32), 'sw1': jax.random.normal(ks[4], (D, H), jnp.float32) * s, 'sb1': jnp.zeros((H,), jnp.float32), 'sw2': jax.random.normal(ks[5], (H, D), jnp.float32) * s, 'sb2': jnp.zeros((D,), jnp.float32)}
    _L0_ffn_all = _L0_ffn_setup()
    _L0_ffn_in = {k: v for k, v in _L0_ffn_all.items() if k in ('gate_w', 'w1', 'b1', 'w2', 'b2', 'sw1', 'sb1', 'sw2', 'sb2')}
    del _L0_ffn_all
    return {'x': x, 'L0_tok_W1': _L0_tok_in['W1'], 'L0_tok_b1': _L0_tok_in['b1'], 'L0_tok_W2': _L0_tok_in['W2'], 'L0_tok_b2': _L0_tok_in['b2'], 'L0_tok_W3': _L0_tok_in['W3'], 'L0_tok_b3': _L0_tok_in['b3'], 'L0_attn_gamma': _L0_attn_in['gamma'], 'L0_attn_beta': _L0_attn_in['beta'], 'L0_attn_wq1': _L0_attn_in['wq1'], 'L0_attn_wqd': _L0_attn_in['wqd'], 'L0_attn_wk1': _L0_attn_in['wk1'], 'L0_attn_wkd': _L0_attn_in['wkd'], 'L0_attn_wv1': _L0_attn_in['wv1'], 'L0_attn_wvd': _L0_attn_in['wvd'], 'L0_attn_wout': _L0_attn_in['wout'], 'L0_ffn_gate_w': _L0_ffn_in['gate_w'], 'L0_ffn_w1': _L0_ffn_in['w1'], 'L0_ffn_b1': _L0_ffn_in['b1'], 'L0_ffn_w2': _L0_ffn_in['w2'], 'L0_ffn_b2': _L0_ffn_in['b2'], 'L0_ffn_sw1': _L0_ffn_in['sw1'], 'L0_ffn_sb1': _L0_ffn_in['sb1'], 'L0_ffn_sw2': _L0_ffn_in['sw2'], 'L0_ffn_sb2': _L0_ffn_in['sb2']}

def reference(x, L0_tok_W1, L0_tok_b1, L0_tok_W2, L0_tok_b2, L0_tok_W3, L0_tok_b3, L0_attn_gamma, L0_attn_beta, L0_attn_wq1, L0_attn_wqd, L0_attn_wk1, L0_attn_wkd, L0_attn_wv1, L0_attn_wvd, L0_attn_wout, L0_ffn_gate_w, L0_ffn_w1, L0_ffn_b1, L0_ffn_w2, L0_ffn_b2, L0_ffn_sw1, L0_ffn_sb1, L0_ffn_sw2, L0_ffn_sb2):
    import jax
    import jax.numpy as jnp

    def _L0_tok_ref(features, W1, b1, W2, b2, W3, b3, factor):
        import jax, jax.numpy as jnp
        import numpy as np
        B, T, C = (8, 1024, 128)
        D = 512
        FACTOR = 2
        TEMP = 1e-05
        Bv, Tv, Cv = features.shape
        Tnew = Tv // factor
        h = jax.nn.gelu(features @ W1 + b1, approximate=False)
        h = jax.nn.gelu(h @ W2 + b2, approximate=False)
        imp = jax.nn.sigmoid((h @ W3 + b3)[..., 0]) + TEMP
        imp = imp / imp.sum(axis=1, keepdims=True) * (Tv / factor)
        cs = jnp.cumsum(imp, axis=1)
        grid = jnp.arange(Tnew, dtype=cs.dtype)
        pc = jnp.maximum(cs[:, :, None] - grid[None, None, :], 0.0)
        Pp = jnp.pad(pc, ((0, 0), (1, 0), (0, 1)))
        Wt = Pp[:, 1:, :-1] - Pp[:, 1:, 1:] - (Pp[:, :-1, :-1] - Pp[:, :-1, 1:])
        Xnew = jnp.einsum('btn,btc->bnc', Wt, features)
        return Xnew

    def _L0_attn_ref(x, gamma, beta, wq1, wqd, wk1, wkd, wv1, wvd, wout):
        import jax, jax.numpy as jnp
        import numpy as np
        import math
        DIM = 128
        HEADS = 8
        DIM_HEAD = 64
        INNER = HEADS * DIM_HEAD
        B = 2
        N = 512

        def _alibi_slopes(heads):

            def pow2(n):
                start = 2 ** (-2 ** (-(math.log2(n) - 3)))
                return [start * start ** i for i in range(n)]
            if math.log2(heads).is_integer():
                return pow2(heads)
            cp2 = 2 ** math.floor(math.log2(heads))
            return pow2(cp2) + pow2(2 * cp2)[0::2][:heads - cp2]

        def _proj(xp, w1, wd):
            y = jnp.einsum('ed,bdn->ben', w1, xp)
            y = wd[None, :, 0:1] * y[..., :-2] + wd[None, :, 1:2] * y[..., 1:-1] + wd[None, :, 2:3] * y[..., 2:]
            return y

        def _split_heads(y, b, n):
            return y.reshape(b, HEADS, DIM_HEAD, n).transpose(0, 1, 3, 2)
        b, n, d = x.shape
        scale = DIM_HEAD ** (-0.5)
        mu = jnp.mean(x, axis=-1, keepdims=True)
        var = jnp.var(x, axis=-1, keepdims=True)
        xn = (x - mu) / jnp.sqrt(var + 1e-05) * gamma + beta
        xp = jnp.pad(xn.transpose(0, 2, 1), ((0, 0), (0, 0), (2, 0)))
        q = _split_heads(_proj(xp, wq1, wqd), b, n) * scale
        k = _split_heads(_proj(xp, wk1, wkd), b, n)
        v = _split_heads(_proj(xp, wv1, wvd), b, n)
        sim = jnp.einsum('bhid,bhjd->bhij', q, k)
        slopes = jnp.asarray(_alibi_slopes(HEADS), dtype=sim.dtype)
        idx = jnp.arange(n)
        bias = -jnp.abs(idx[None, :] - idx[:, None]).astype(sim.dtype)
        sim = sim + bias[None, None] * slopes[None, :, None, None]
        causal = jnp.triu(jnp.ones((n, n), bool), 1)
        sim = jnp.where(causal[None, None], -jnp.finfo(sim.dtype).max, sim)
        attn = jax.nn.softmax(sim, axis=-1)
        out = jnp.einsum('bhij,bhjd->bhid', attn, v)
        out = out.transpose(0, 2, 1, 3).reshape(b, n, INNER)
        return out @ wout.T

    def _L0_ffn_ref(x, gate_w, w1, b1, w2, b2, sw1, sb1, sw2, sb2):
        import jax, jax.numpy as jnp
        import numpy as np
        D, H, E, B, S = (128, 512, 16, 8, 2048)
        MAX_GROUP_SIZE = 1024
        MIN_CAPACITY = 8
        CAPACITY_FACTOR = 1.0

        def _group_dims(num_tokens, num_experts):
            num_groups = -(-num_tokens // MAX_GROUP_SIZE)
            while num_tokens % num_groups != 0 or num_groups % num_experts != 0:
                num_groups += 1
            return (num_tokens // num_groups, num_groups)
        Bn, Sn, Dn = x.shape
        En = gate_w.shape[1]
        T = Bn * Sn
        group_size, num_groups = _group_dims(T, En)
        cap = max(int(round(CAPACITY_FACTOR * group_size * num_groups / En)), MIN_CAPACITY)
        xg = x.reshape(num_groups, group_size, Dn)
        logits = jnp.einsum('gsd,de->gse', xg, gate_w)
        probs = jax.nn.softmax(logits, axis=-1)
        flat_probs = probs.transpose(2, 0, 1).reshape(En, T)
        scores, tok_idx = jax.lax.top_k(flat_probs, cap)
        xf = x.reshape(T, Dn)
        toks = xf[tok_idx]
        h = jax.nn.gelu(jnp.einsum('ecd,edh->ech', toks, w1) + b1[:, None, :])
        y = jnp.einsum('ech,ehd->ecd', h, w2) + b2[:, None, :]
        y = y * scores[..., None]
        routed = jnp.zeros_like(xf).at[tok_idx.reshape(-1)].add(y.reshape(-1, Dn))
        shared = jax.nn.gelu(xf @ sw1 + sb1) @ sw2 + sb2
        out = (routed + shared).reshape(Bn, Sn, Dn)
        return out
    h = _L0_tok_ref(x, L0_tok_W1, L0_tok_b1, L0_tok_W2, L0_tok_b2, L0_tok_W3, L0_tok_b3, 2)
    h = h + _L0_attn_ref(_layernorm(h, axis=-1), L0_attn_gamma, L0_attn_beta, L0_attn_wq1, L0_attn_wqd, L0_attn_wk1, L0_attn_wkd, L0_attn_wv1, L0_attn_wvd, L0_attn_wout)
    h = h + _L0_ffn_ref(_layernorm(h, axis=-1), L0_ffn_gate_w, L0_ffn_w1, L0_ffn_b1, L0_ffn_w2, L0_ffn_b2, L0_ffn_sw1, L0_ffn_sb1, L0_ffn_sw2, L0_ffn_sb2)
    return h

_drawn_inputs = setup_inputs


def setup_inputs(seed=0):
    import zlib

    import numpy as np

    out = dict(_drawn_inputs(seed))
    spreads = {'L0_tok_b1': (0.0, 0.1),
     'L0_tok_b2': (0.0, 0.1),
     'L0_attn_gamma': (1.0, 0.6),
     'L0_attn_beta': (0.0, 0.8),
     'L0_ffn_b1': (0.0, 0.8),
     'L0_ffn_b2': (0.0, 0.555),
     'L0_ffn_sb1': (0.0, 0.624),
     'L0_ffn_sb2': (0.0, 0.1)}
    factors = {'L0_attn_wq1': 8.0,
     'L0_attn_wqd': 8.0,
     'L0_attn_wk1': 8.0,
     'L0_attn_wkd': 8.0,
     'L0_attn_wv1': 8.0,
     'L0_attn_wvd': 8.0,
     'L0_attn_wout': 8.0,
     'L0_ffn_gate_w': 3.493,
     'L0_ffn_w1': 7.403,
     'L0_ffn_w2': 6.708}
    for name, (base, spread) in spreads.items():
        noise = np.random.default_rng([zlib.crc32(name.encode()), seed]).standard_normal(out[name].shape)
        drawn = base * np.exp(spread * noise) if base else spread * noise
        out[name] = jnp.asarray(drawn.astype(out[name].dtype))
    for name, factor in factors.items():
        out[name] = (out[name] * factor).astype(out[name].dtype)
    return out
```

```python
import concourse.bass as bass
from concourse import mybir
from contextlib import ExitStack

F32 = mybir.dt.float32
I32 = mybir.dt.int32
U32 = mybir.dt.uint32
BF16 = mybir.dt.bfloat16
ALU = mybir.AluOpType
ACT = mybir.ActivationFunctionType
AX_X = mybir.AxisListType.X

B, T, C = 16, 750, 128
N = T // 2
PT_ = 125
TT_, NT = T // PT_, N // PT_
D = 512
DC = D // 128
HEADS, DH = 8, 64
E = 16
TOK = B * N
CAP = TOK // E
ROW = C + E
TEMP, EPS = 1e-5, 1e-5
MASKED = 3.4028234663852886e38


def slopes(heads):
    return [2.0 ** (-8.0 * (h + 1) / heads) for h in range(heads)]


def wait(eng, sem, value):
    if isinstance(value, int) and value <= 0:
        return
    eng.wait_ge(sem, value)


def wait_apart(eng, sem, value, passed):
    wait(eng, sem, value)
    if not isinstance(value, int):
        eng.sem_inc(passed, 1)


def cap(value, most):
    return min(value, most) if isinstance(value, int) else value


def valid(m):
    return not isinstance(m, int) or 0 <= m < B


def build(nc, x, tW1, tb1, tW2, tb2, tW3, tb3, gamma, beta, wq1, wqd, wk1, wkd, wv1, wvd, wout,
          gate_w, ew1, eb1, ew2, eb2, sw1, sb1, sw2, sb2, out):
    ctx = ExitStack()
    with ctx:
        ctx.enter_context(nc.allow_non_contiguous_dma(reason="short vectors, once"))

        def sb(name, shape, dt=F32):
            return ctx.enter_context(nc.sbuf_tensor(name, shape, dt))

        mid = ctx.enter_context(ExitStack())

        def sbm(name, shape, dt=F32):
            return mid.enter_context(nc.sbuf_tensor(name, shape, dt))

        def sem(name):
            return ctx.enter_context(nc.semaphore(name))

        z_dram = nc.dram_tensor("z_scratch", (B, DC, T), F32, kind="Internal").ap()
        table = nc.dram_tensor("token_table", (TOK, ROW), F32, kind="Internal").ap()
        probs_dram = nc.dram_tensor("probs_scratch", (B, E, N), F32, kind="Internal").ap()
        table_b = table.rearrange("(b n) c -> b n c", n=N)

        bank = [ctx.enter_context(nc.psum_tensor(f"bank{i}", [128, 512], F32)) for i in range(8)]

        ident = sb("ident", [128, 128])
        gammac = sb("gammac", [128, 1])
        betac = sb("betac", [128, 1])
        sb1c = sb("sb1c", [128, DC])
        mhalf = sb("mhalf", [PT_, NT])
        probsT = sb("probsT", [128, 2 * N])
        idx = sb("idx", [PT_, E, NT], U32)
        thr = sb("thr", [128, 1], I32)
        cnt = sb("cnt", [128, 4])
        same = sb("same", [128, 128])
        before = sb("before", [128, 128])

        qkd = sbm("qkd", [128, 2, DC, 3])
        vd = sbm("vd", [128, DC, 3])
        WQKT = sbm("WQKT", [128, 2, D])
        WVT = sbm("WVT", [128, 3, D])
        WOT = sbm("WOT", [128, DC, 128])
        gate = sbm("gate", [128, E])
        SW1 = sbm("SW1", [128, D])
        SW2 = sbm("SW2", [128, DC, 128])
        sb2b = sbm("sb2b", [PT_, C])
        nbias = sbm("nbias", [PT_, HEADS, N])
        grid0 = sbm("grid0", [PT_, N])
        grid1 = sbm("grid1", [PT_, N])

        csT = sbm("csT", [PT_, 2 * TT_, B])

        Hall = sbm("Hall", [PT_, B, NT, C])
        tTall = sbm("tTall", [128, TOK])

        out_rows = out.rearrange("b n c -> (b n) c")

        with ExitStack() as one:
            def sb_(name, shape, dt=F32):
                return one.enter_context(nc.sbuf_tensor(name, shape, dt))

            def sem(name):
                return one.enter_context(nc.semaphore(name))

            W1 = sb_("W1", [128, D])
            W2 = sb_("W2", [128, DC, D])
            w3c = sb_("w3c", [128, DC])
            w3rep = sb_("w3rep", [128, DC, 32])
            b1c = sb_("b1c", [128, DC])
            b2c = sb_("b2c", [128, DC])
            b3c = sb_("b3c", [B, 1])
            wraw = sb_("wraw", [128, 3, DC, 128])
            wvtap = sb_("wvtap", [128, 3, DC, 128])
            woraw = sb_("woraw", [128, D])
            dist = sb_("dist", [PT_, N])
            zrow = sb_("zrow", [B, DC, T])
            imp = sb_("imp", [B, T])
            isum = sb_("isum", [B, 2])
            ones_t = sb_("ones_t", [B, T])
            cs = sb_("cs", [B, T + 1])
            X = sb_("X", [PT_, 2, TT_, C])
            xT = sb_("xT", [128, 2, N])
            h1 = sb_("h1", [128, 2, DC, N])
            h2 = sb_("h2", [128, 2, DC, N])
            zsb = sb_("zsb", [128, 2, N])

            s_w = sem("s_tok_weights")
            s_w2 = sem("s_other_weights")
            s_pool = sem("s_pool_consts")
            s_id = sem("s_identity")
            s_w3 = sem("s_w3_replicated")
            s_prep = sem("s_scaled_weights")
            s_wt = sem("s_weights_transposed")
            s_wc = sem("s_weights_copied")
            s_x = [sem(f"s_x_loaded{u}") for u in range(2)]
            s_xp = sem("s_xT_in_psum")
            s_xt = sem("s_xT_ready")
            s_h1 = sem("s_h1_in_psum")
            s_g1 = sem("s_h1_ready")
            s_h2 = sem("s_h2_in_psum")
            s_g2 = sem("s_h2_ready")
            s_z = sem("s_z_in_psum")
            s_zc = sem("s_z_copied")
            s_zs = [sem(f"s_z_stored{u}") for u in range(2)]
            s_zl = sem("s_z_loaded")
            s_zsum = sem("s_z_steps")
            s_sig = sem("s_sigmoid_ready")
            s_cp = sem("s_cs_in_psum")

            block = one.enter_context(nc.Block())
            TOK_W, OTHER_W = 6, 14

            @block.sync
            def _(sp):
                sp.dma_start(X[:, 0], x[0].rearrange("(k p) c -> p k c", p=PT_)).then_inc(s_x[0], 16)
                sp.dma_start(W1[:], tW1).then_inc(s_w, 16)
                sp.dma_start(b1c[:], tb1.rearrange("(m p) -> p m", p=128)).then_inc(s_w, 16)
                sp.dma_start(W2[:], tW2.rearrange("(k p) n -> p k n", p=128)).then_inc(s_w, 16)
                sp.dma_start(b2c[:], tb2.rearrange("(m p) -> p m", p=128)).then_inc(s_w, 16)
                sp.dma_start(w3c[:], tW3.rearrange("(m p) o -> p (m o)", p=128)).then_inc(s_w, 16)
                sp.dma_start(b3c[:], tb3.rearrange("(o n) -> o n", o=1).broadcast_to([B, 1])).then_inc(s_w, 16)
                for n, w in enumerate((wq1, wk1, wv1)):
                    sp.dma_start(wraw[:, n], w.rearrange("(m p) d -> p m d", p=128)).then_inc(s_w2, 16)
                for n, w in enumerate((wqd, wkd)):
                    sp.dma_start(qkd[:, n], w.rearrange("(m p) a -> p m a", p=128)).then_inc(s_w2, 16)
                sp.dma_start(vd[:], wvd.rearrange("(m p) a -> p m a", p=128)).then_inc(s_w2, 16)
                sp.dma_start(woraw[:], wout).then_inc(s_w2, 16)
                sp.dma_start(gammac[:], gamma.rearrange("(p o) -> p o", o=1)).then_inc(s_w2, 16)
                sp.dma_start(betac[:], beta.rearrange("(p o) -> p o", o=1)).then_inc(s_w2, 16)
                sp.dma_start(gate[:], gate_w).then_inc(s_w2, 16)
                sp.dma_start(SW1[:], sw1).then_inc(s_w2, 16)
                sp.dma_start(SW2[:], sw2.rearrange("(k p) n -> p k n", p=128)).then_inc(s_w2, 16)
                sp.dma_start(sb1c[:], sb1.rearrange("(m p) -> p m", p=128)).then_inc(s_w2, 16)
                sp.dma_start(sb2b[:], sb2.rearrange("(o n) -> o n", o=1).broadcast_to([PT_, C])).then_inc(s_w2, 16)
                sp.dma_start(X[:, 1], x[1].rearrange("(k p) c -> p k c", p=PT_)).then_inc(s_x[1], 16)
                with sp.Fori(0, B // 2) as i:
                    for u in range(2):
                        for half in range(2):
                            sp.wait_ge(s_zc, 4 * i + 2 * u + half + 1)
                            sp.dma_start(z_dram[2 * i + u, :, half * N:(half + 1) * N],
                                         zsb[0:128:32, half]).then_inc(s_zs[half], 16)
                        sp.wait_ge(s_xp, 4 * i + 2 * u + 2)
                        nxt = (2 * i + u + 2) % B
                        sp.dma_start(X[:, u], x[nxt].rearrange("(k p) c -> p k c", p=PT_)).then_inc(s_x[u], 16)
                for half in range(2):
                    sp.wait_ge(s_zs[half], 16 * B)
                for u in range(2):
                    sp.wait_ge(s_x[u], 16 * (B // 2 + 1))
                sp.dma_start(zrow[:], z_dram).then_inc(s_zl, 16)
                sp.wait_ge(s_zl, 16)

            @block.gpsimd
            def _(pool):
                nc.gpsimd.memset(ident[:], 0.0).then_inc(s_pool, 1)
                pool.wait_ge(s_pool, 1)
                nc.gpsimd.affine_select(out=ident[:], in_=ident[:], compare_op=ALU.not_equal, fill=1.0, base=0,
                                        pattern=[[-1, 128]], channel_multiplier=1).then_inc(s_id, 1)
                nc.gpsimd.iota(dist[:], pattern=[[-1, N]], base=N - PT_, channel_multiplier=1,
                               allow_small_or_imprecise_dtypes=True).then_inc(s_pool, 1)
                nc.gpsimd.iota(grid0[:], pattern=[[1, N]], base=0, channel_multiplier=0,
                               allow_small_or_imprecise_dtypes=True).then_inc(s_pool, 1)
                nc.gpsimd.iota(grid1[:], pattern=[[1, N]], base=1, channel_multiplier=0,
                               allow_small_or_imprecise_dtypes=True).then_inc(s_pool, 1)
                pool.wait_ge(s_pool, 4)
                nc.gpsimd.memset(grid1[:, N - 1:N], 1e30).then_inc(s_pool, 1)
                nc.gpsimd.memset(mhalf[:], -0.5).then_inc(s_pool, 1)
                nc.gpsimd.memset(ones_t[:], 1.0).then_inc(s_pool, 1)
                nc.gpsimd.memset(cs[:, 0:1], 0.0).then_inc(s_pool, 1)
                for h, slope in enumerate(slopes(HEADS)):
                    nc.gpsimd.tensor_scalar(nbias[:, h], dist[:], slope, None, ALU.mult).then_inc(s_pool, 1)
                    pool.wait_ge(s_pool, 9 + 2 * h)
                    nc.gpsimd.affine_select(out=nbias[:, h], in_=nbias[:, h], compare_op=ALU.is_ge, fill=MASKED,
                                            base=N - PT_, pattern=[[-1, N]], channel_multiplier=1).then_inc(s_pool, 1)
                pool.wait_ge(s_w2, 16 * OTHER_W)
                nc.gpsimd.tensor_scalar(qkd[:, 0], qkd[:, 0], -(DH ** -0.5), None, ALU.mult).then_inc(s_prep, 1)
                for a in range(3):
                    for m in range(DC):
                        nc.gpsimd.tensor_scalar(wvtap[:, a, m], wraw[:, 2, m], vd[:, m, a:a + 1], None,
                                                ALU.mult).then_inc(s_prep, 1)

            jobs = [(wraw[:, n, m], WQKT[:, n, m * 128:(m + 1) * 128]) for n in range(2) for m in range(DC)]
            jobs += [(wvtap[:, a, m], WVT[:, a, m * 128:(m + 1) * 128]) for a in range(3) for m in range(DC)]
            jobs += [(woraw[:, m * 128:(m + 1) * 128], WOT[:, m]) for m in range(DC)]

            @block.tensor
            def _(pe):
                def layer1(g, p):
                    pe.wait_ge(s_xt, g + 1)
                    for m in range(DC):
                        wait(pe, s_g1, 4 * g + m - 1)
                        nc.tensor.matmul(bank[2 + m % 2][:, :N], W1[:, m * 128:(m + 1) * 128], xT[:, p],
                                         start=True, stop=True).then_inc(s_h1, 1)

                def layer2(g, p, ms):
                    pe.wait_ge(s_g1, 4 * g + 4)
                    for m in ms:
                        wait(pe, s_g2, 4 * g + m - 1)
                        for k in range(DC):
                            last = nc.tensor.matmul(bank[4 + m % 2][:, :N], W2[:, k, m * 128:(m + 1) * 128],
                                                    h1[:, p, k], start=(k == 0), stop=(k == DC - 1))
                        last.then_inc(s_h2, 1)

                def layer3(g, p):
                    pe.wait_ge(s_g2, 4 * g + 4)
                    wait(pe, s_zc, g - 1)
                    for c in range(DC):
                        last = nc.tensor.matmul(bank[6 + p][32 * c:32 * c + 32, :N], w3rep[:, c], h2[:, p, c],
                                                start=True, stop=True)
                    last.then_inc(s_z, 1)

                pe.wait_ge(s_id, 1)
                pe.wait_ge(s_w, 16 * TOK_W)
                pe.wait_ge(s_w3, 1)
                pe.wait_ge(s_x[0], 16)
                for k in range(3):
                    last = nc.tensor.transpose(bank[0][:, k * PT_:(k + 1) * PT_], X[:, 0, k], ident[:PT_, :PT_])
                last.then_inc(s_xp, 1)
                layer1(0, 0)

                def two_batches(i):
                    for s in range(4):
                        g = 4 * i + s
                        p, nxt = s % 2, (s + 1) % 4
                        if nxt % 2 == 0:
                            pe.wait_ge(s_x[nxt // 2], 16 * (i + 1 + (nxt == 0)))
                        wait(pe, s_xt, g)
                        for k in range(3):
                            last = nc.tensor.transpose(bank[1 - p][:, k * PT_:(k + 1) * PT_],
                                                       X[:, nxt // 2, 3 * (nxt % 2) + k], ident[:PT_, :PT_])
                        last.then_inc(s_xp, 1)
                        layer2(g, p, (0, 1))
                        layer1(g + 1, 1 - p)
                        layer2(g, p, (2, 3))
                        layer3(g, p)

                two_batches(0)
                with pe.Fori(1, B // 2) as i:
                    two_batches(i)
                pe.wait_ge(s_g1, 4 * (2 * B + 1))
                pe.wait_ge(s_w2, 16 * OTHER_W)
                pe.wait_ge(s_prep, 13)
                for n, (src, _) in enumerate(jobs):
                    wait(pe, s_wc, n - 3)
                    nc.tensor.transpose(bank[n % 4][:, 0:128], src, ident[:]).then_inc(s_wt, 1)
                pe.wait_ge(s_zsum, 8)
                for n in range(2):
                    for k in range(TT_):
                        col = (n * TT_ + k) * B
                        last = nc.tensor.transpose(bank[4][:PT_, col:col + B],
                                                   cs[:, 1 - n + k * PT_:1 - n + (k + 1) * PT_], ident[:B, :B])
                last.then_inc(s_cp, 1)

            @block.scalar
            def _(act):
                def gelu1(g, p):
                    for m in range(DC):
                        act.wait_ge(s_h1, 4 * g + m + 1)
                        if m == 0:
                            wait(act, s_h2, 4 * g - 4)
                        nc.scalar.activation(h1[:, p, m], bank[2 + m % 2][:, :N], ACT.Gelu,
                                             bias=b1c[:, m:m + 1]).then_inc(s_g1, 1)

                def gelu2(g, p, ms):
                    for m in ms:
                        act.wait_ge(s_h2, 4 * g + m + 1)
                        if m == 0:
                            wait(act, s_z, g - 1)
                        nc.scalar.activation(h2[:, p, m], bank[4 + m % 2][:, :N], ACT.Gelu,
                                             bias=b2c[:, m:m + 1]).then_inc(s_g2, 1)

                act.wait_ge(s_w, 16 * TOK_W)
                gelu1(0, 0)

                def two_batches(i):
                    for s in range(4):
                        g, p = 4 * i + s, s % 2
                        gelu2(g, p, (0, 1))
                        gelu1(g + 1, 1 - p)
                        gelu2(g, p, (2, 3))

                two_batches(0)
                with act.Fori(1, B // 2) as i:
                    two_batches(i)
                act.wait_ge(s_zsum, 3)
                nc.scalar.activation(imp[:], zrow[:, 0], ACT.Sigmoid, bias=b3c[:, 0:1]).then_inc(s_sig, 1)

            @block.vector
            def _(dve):
                def copy_x(g, p):
                    dve.wait_ge(s_xp, g + 1)
                    wait(dve, s_h1, 4 * g - 4)
                    nc.vector.tensor_copy(xT[:, p], bank[p][:, :N]).then_inc(s_xt, 1)

                dve.wait_ge(s_w, 16 * TOK_W)
                nc.vector.tensor_copy(w3rep[:], w3c[:, :, None].broadcast_to([128, DC, 32])).then_inc(s_w3, 1)
                copy_x(0, 0)
                with dve.Fori(0, B // 2) as i:
                    for s in range(4):
                        g, p = 4 * i + s, s % 2
                        copy_x(g + 1, 1 - p)
                        dve.wait_ge(s_z, g + 1)
                        if s < 2:
                            dve.wait_ge(s_zs[p], 16 * (2 * i))
                        else:
                            dve.wait_ge(s_zs[p], 16 * (2 * i + 1))
                        nc.vector.tensor_copy(zsb[:, p], bank[6 + p][:, :N]).then_inc(s_zc, 1)
                for n, (_, dst) in enumerate(jobs):
                    dve.wait_ge(s_wt, n + 1)
                    nc.vector.tensor_copy(dst, bank[n % 4][:, 0:128]).then_inc(s_wc, 1)
                dve.wait_ge(s_zl, 16)
                for c in range(1, DC):
                    nc.vector.tensor_tensor(zrow[:, 0], zrow[:, 0], zrow[:, c], ALU.add).then_inc(s_zsum, 1)
                    dve.wait_ge(s_zsum, c)
                dve.wait_ge(s_sig, 1)
                nc.vector.tensor_scalar(imp[:], imp[:], TEMP, None, ALU.add).then_inc(s_zsum, 1)
                dve.wait_ge(s_zsum, 4)
                nc.vector.reduce_sum(isum[:, 0:1], imp[:], AX_X).then_inc(s_zsum, 1)
                dve.wait_ge(s_zsum, 5)
                nc.vector.reciprocal(isum[:, 1:2], isum[:, 0:1]).then_inc(s_zsum, 1)
                dve.wait_ge(s_zsum, 6)
                nc.vector.tensor_scalar(imp[:], imp[:], isum[:, 1:2], float(N), ALU.mult, ALU.mult).then_inc(s_zsum, 1)
                dve.wait_ge(s_zsum, 7)
                dve.wait_ge(s_pool, 8)
                nc.vector.tensor_tensor_scan(cs[:, 1:T + 1], ones_t[:], imp[:], 0.0, ALU.mult,
                                             ALU.add).then_inc(s_zsum, 1)
                dve.wait_ge(s_cp, 1)
                nc.vector.tensor_copy(csT[:].rearrange("p k b -> p (k b)"), bank[4][:PT_, :2 * TT_ * B])

        with ExitStack() as two:
            def sb_(name, shape, dt=F32):
                return two.enter_context(nc.sbuf_tensor(name, shape, dt))

            def sem(name):
                return two.enter_context(nc.semaphore(name))

            FIRST, LAST = -3, B + 1
            LOOP0, LOOP1 = 3, 13
            XPAD = N + 2
            SEG = (0, N, N + PT_)
            ORDER = (2, 0, 1)
            LN = 9

            X2 = sb_("X2", [PT_, 2, TT_, C])
            csb = sb_("csb", [PT_, 2 * TT_])
            cellmax = sb_("cellmax", [PT_, N])
            overlap = sb_("overlap", [PT_, 2, N])
            Wt = sb_("Wt", [PT_, TT_, N])
            lnstat = sb_("lnstat", [PT_, NT, 6])
            lnmv = sb_("lnmv", [PT_, NT, 2])
            lnve = sb_("lnve", [PT_, NT])
            lnr = sb_("lnr", [PT_, NT])
            gstat = sb_("gstat", [PT_, NT, 6])
            gmv = sb_("gmv", [PT_, NT, 2])
            gve = sb_("gve", [PT_, NT])
            gr = sb_("gr", [PT_, NT])
            n1 = sb_("n1", [PT_, NT, C])
            n2 = sb_("n2", [PT_, NT, C])
            xnT = sb_("xnT", [128, 2, XPAD + 1])
            tap0 = sb_("tap0", [128, 2, N])
            tap1 = sb_("tap1", [128, 2, N])
            QK = sb_("QK", [128, 2, DC, N])
            V = sb_("V", [PT_, 2, NT, D])
            P = sb_("P", [PT_, 4, 2 * N])
            nmax = sb_("nmax", [PT_, 4, NT])
            psum_ = sb_("psum_", [PT_, 4, NT])
            prec = sb_("prec", [PT_, 4, NT])
            PT = sb_("PT", [PT_, 4, 2 * N])
            OT = sb_("OT", [128, DC, N])
            row = sb_("row", [PT_, NT, ROW])
            tT = sb_("tT", [128, N])
            lg = sb_("lg", [PT_, NT, E])
            lmax = sb_("lmax", [PT_, NT])
            lsum = sb_("lsum", [PT_, NT])
            lrec = sb_("lrec", [PT_, NT])
            pTs = sb_("pTs", [E, N])

            bS, bT, bO = (bank[0], bank[1]), (bank[2], bank[3]), bank[4]
            G0, G1, G2 = bank[5], bank[6], bank[7]

            s_x2 = [sem(f"s_x2_loaded{u}") for u in range(2)]
            s_csb = sem("s_cs_of_batch")
            s_cm = sem("s_cellmax_ready")
            s_ov = sem("s_overlap_ready")
            s_wt = sem("s_pool_weights_ready")
            s_ein = sem("s_pooled_in_psum")
            s_lnd = sem("s_ln_dve_steps")
            s_lnp = sem("s_ln_rsqrt_steps")
            s_xtp = sem("s_xnT_in_psum")
            s_xt = sem("s_xnT_ready")
            s_pad = sem("s_xnT_padded")
            s_qkp = sem("s_qk_in_psum")
            s_t0 = sem("s_tap0_ready")
            s_t1 = sem("s_tap1_ready")
            s_qk = sem("s_qk_ready")
            s_vp = sem("s_v_in_psum")
            s_v = sem("s_v_ready")
            s_sp = sem("s_scores_in_psum")
            s_s = sem("s_scores_ready")
            s_ex = sem("s_exp_ready")
            s_rc = sem("s_recip_ready")
            s_pn = sem("s_probs_normalised")
            s_tp = sem("s_probs_transposed_in_psum")
            s_pt0 = sem("s_probsT0_ready")
            s_pt1 = sem("s_probsT1_ready")
            s_pv = sem("s_pv_in_psum")
            s_o = sem("s_attended_ready")
            s_wo = sem("s_projected_in_psum")
            s_g = sem("s_residual_and_gate_steps")
            s_gp = sem("s_gate_ln_rsqrt_steps")
            s_ttp = sem("s_tT_in_psum")
            s_tt = sem("s_tT_ready")
            s_lp = sem("s_logits_in_psum")
            s_lm = sem("s_logits_shifted")
            s_le = sem("s_logits_exp")
            s_lf = sem("s_probabilities_steps")
            s_pp = sem("s_probsT_in_psum")
            s_pc = sem("s_probsT_copied")
            s_tab = sem("s_table_stored")
            s_tts = sem("s_tT_stored")
            s_ps = sem("s_probsT_stored")
            s_pl = sem("s_probsT_loaded")

            s_on = [sem(f"s_waits_passed{n}") for n in range(2)]

            block = two.enter_context(nc.Block())

            def parity(b, k):
                return (b + k) % 2

            def bodies(eng, body):
                for b in range(FIRST, LOOP0):
                    body(b, b % 2)
                with eng.Fori(LOOP0, LOOP1 - 1, 2) as i:
                    body(i, LOOP0 % 2)
                    body(i + 1, (LOOP0 + 1) % 2)
                for b in range(LOOP1, LAST + 1):
                    body(b, b % 2)

            @block.sync
            def _(sp):
                def body(b, u):
                    if valid(b + 3):
                        wait(sp, s_ein, b + 2)
                        sp.dma_start(X2[:, (u + 1) % 2], x[b + 3].rearrange("(k p) c -> p k c", p=PT_)
                                     ).then_inc(s_x2[(u + 1) % 2], 16)
                    m = b - 2
                    if valid(m):
                        sp.wait_ge(s_lf, 3 * m + 3)
                        sp.dma_start(table_b[m].rearrange("(t p) c -> p t c", p=PT_), row[:]
                                     ).then_inc(s_tab, 16)
                        sp.wait_ge(s_pc, m + 1)
                        sp.dma_start(probs_dram[m], pTs[:]).then_inc(s_ps, 16)
                    m = b - 1
                    if valid(m):
                        sp.wait_ge(s_tt, m + 1)
                        sp.dma_start(tTall[:, bass.ds(m * N, N)], tT[:]).then_inc(s_tts, 16)

                bodies(sp, body)
                sp.wait_ge(s_tab, 16 * B)
                sp.wait_ge(s_ps, 16 * B)
                for pair in range(B // 2):
                    sp.dma_start(probsT[pair * E:(pair + 1) * E].rearrange("e (u n) -> e u n", u=2),
                                 probs_dram[2 * pair:2 * pair + 2].rearrange("u e n -> e u n")
                                 ).then_inc(s_pl, 16)
                sp.wait_ge(s_pl, 16 * (B // 2))
                sp.wait_ge(s_tts, 16 * B)

            @block.tensor
            def _(pe):
                def scores(b, h):
                    c, r = h // 2, DH * (h % 2)
                    pe.wait_ge(s_qk, 8 * b + 2 * c + 2)
                    for unit, tiles in enumerate(((2,), (0, 1))):
                        wait(pe, s_s, 3 * (8 * b + h) - 2 + 2 * unit)
                        for i in tiles:
                            w, at = (i + 1) * PT_, 0 if i != 1 else PT_
                            last = nc.tensor.matmul(bS[unit][:PT_, at:at + w],
                                                    QK[r:r + DH, 0, c, i * PT_:(i + 1) * PT_],
                                                    QK[r:r + DH, 1, c, :w], start=True, stop=True)
                        last.then_inc(s_sp, 1)

                def transpose_probs(b, h):
                    n = 8 * b + h
                    pe.wait_ge(s_pn, 3 * n + 3)
                    wait(pe, s_pt0, n)
                    for i in range(NT):
                        last = nc.tensor.transpose(bT[0][:PT_, i * PT_:(i + 1) * PT_],
                                                   P[:, h % 4, SEG[ORDER.index(i)]:SEG[ORDER.index(i)] + PT_],
                                                   ident[:PT_, :PT_])
                    last.then_inc(s_tp, 1)
                    wait(pe, s_pt1, n)
                    for at, (i, j) in enumerate(((1, 1), (2, 1), (2, 2))):
                        f = SEG[ORDER.index(i)] + j * PT_
                        last = nc.tensor.transpose(bT[1][:PT_, at * PT_:(at + 1) * PT_], P[:, h % 4, f:f + PT_],
                                                   ident[:PT_, :PT_])
                    last.then_inc(s_tp, 1)

                def attend(b, c, u):
                    pe.wait_ge(s_pt0, 8 * b + 2 * c + 2)
                    pe.wait_ge(s_pt1, 8 * b + 2 * c + 2)
                    pe.wait_ge(s_v, 3 * b + 3)
                    wait(pe, s_o, 4 * b + c)
                    for j, at in enumerate((0, N, 2 * N - PT_)):
                        for h in (2 * c, 2 * c + 1):
                            r, w = DH * (h % 2), N - j * PT_
                            last = nc.tensor.matmul(bO[r:r + DH, j * PT_:N], V[:, u, j, h * DH:(h + 1) * DH],
                                                    PT[:, h % 4, at:at + w], start=(j == 0), stop=(j == NT - 1))
                    last.then_inc(s_pv, 1)

                def project_qk(m, c, u):
                    pe.wait_ge(s_xt, m + 1)
                    for n, g in enumerate((G0, G1)):
                        if n == 0 and c > 0:
                            wait(pe, s_v, 3 * m + c)
                        elif n == 0:
                            wait(pe, s_qk, 8 * m - 1)
                        else:
                            wait(pe, s_qk, 8 * m + 2 * c)
                            if c == 0:
                                wait(pe, s_pc, m - 2)
                            if c == 3:
                                wait(pe, s_lm, 2 * (m - 1))
                        nc.tensor.matmul(g[:, :XPAD], WQKT[:, n, c * 128:(c + 1) * 128], xnT[:, u, :XPAD],
                                         start=True, stop=True).then_inc(s_qkp, 1)

                def project_v(m, t, u):
                    pe.wait_ge(s_qk, 8 * m + 2 * t + 1)
                    for a in range(3):
                        last = nc.tensor.matmul(G0[:PT_, :], xnT[:, u, t * PT_ + a:(t + 1) * PT_ + a], WVT[:, a],
                                                start=(a == 0), stop=(a == 2))
                    last.then_inc(s_vp, 1)

                def pool_tokens(m, u):
                    pe.wait_ge(s_wt, 6 * m + 6)
                    pe.wait_ge(s_x2[u], (m - u) * 8 + 16)
                    wait(pe, s_xt, m)
                    wait(pe, s_tt, m - 3)
                    for t in range(NT):
                        for k in range(TT_):
                            last = nc.tensor.matmul(G2[:PT_, t * C:(t + 1) * C], Wt[:, k, t * PT_:(t + 1) * PT_],
                                                    X2[:, u, k], start=(k == 0), stop=(k == TT_ - 1))
                    last.then_inc(s_ein, 1)

                def transpose_tokens(src, done):
                    for t in range(NT):
                        last = nc.tensor.transpose(G2[:, t * PT_:(t + 1) * PT_], src[:, t, 0:C], ident[:PT_, :PT_])
                    last.then_inc(done, 1)

                def body(b, u):
                    v_ = 1 - u
                    for h in range(HEADS):
                        if valid(b):
                            scores(b, h)
                        if h < 2 and valid(b - 1):
                            transpose_probs(b - 1, HEADS - 2 + h)
                        if h >= 2 and valid(b):
                            transpose_probs(b, h - 2)
                        if h == 0 and valid(b):
                            project_qk(b, 3, u)
                        if h in (2, 4, 6) and valid(b + 1):
                            project_qk(b + 1, h // 2 - 1, v_)
                        if h in (3, 5, 7) and valid(b + 1):
                            project_v(b + 1, (h - 3) // 2, v_)
                        if h == 1 and valid(b + 2):
                            pool_tokens(b + 2, u)
                        if h == 1 and valid(b - 2):
                            m = b - 2
                            pe.wait_ge(s_qk, cap(8 * b + 8, 8 * B))
                            pe.wait_ge(s_lf, 3 * m + 3)
                            for t in range(NT):
                                last = nc.tensor.transpose(G1[:E, t * PT_:(t + 1) * PT_], row[:, t, C:ROW],
                                                           ident[:PT_, :PT_])
                            last.then_inc(s_pp, 1)
                        if h in (0, 2) and valid(b - 1):
                            attend(b - 1, 2 + h // 2, v_)
                        if h in (4, 6) and valid(b):
                            attend(b, h // 2 - 2, u)
                        if h == 3 and valid(b - 1):
                            m = b - 1
                            pe.wait_ge(s_o, 4 * m + 4)
                            pe.wait_ge(s_lnd, cap((2 * LN + 1) * (b + 2) + 1, (2 * LN + 1) * B))
                            for t in range(NT):
                                for c in range(DC):
                                    last = nc.tensor.matmul(G2[:PT_, t * C:(t + 1) * C],
                                                            OT[:, c, t * PT_:(t + 1) * PT_], WOT[:, c],
                                                            start=(c == 0), stop=(c == DC - 1))
                            last.then_inc(s_wo, 1)
                        if h == 4 and valid(b + 2):
                            m = b + 2
                            pe.wait_ge(s_lnd, (2 * LN + 1) * (m + 1))
                            wait(pe, s_g, (LN + 1) * (m - 3) + 1)
                            transpose_tokens(n2, s_xtp)
                        if h == 6 and valid(b - 1):
                            m = b - 1
                            pe.wait_ge(s_g, (LN + 1) * (m + 1))
                            pe.wait_ge(s_xt, cap(b + 3, B))
                            transpose_tokens(row, s_ttp)
                        if h == 7 and valid(b - 1):
                            m = b - 1
                            pe.wait_ge(s_tt, m + 1)
                            pe.wait_ge(s_qk, cap(8 * (b + 1) + 6, 8 * B))
                            wait(pe, s_pc, cap(m, B))
                            for t in range(NT):
                                last = nc.tensor.matmul(G1[:PT_, t * E:(t + 1) * E], tT[:, t * PT_:(t + 1) * PT_],
                                                        gate[:], start=True, stop=True)
                            last.then_inc(s_lp, 1)

                bodies(pe, body)

            @block.scalar
            def _(act):
                def body(b, u):
                    for h in range(HEADS):
                        if valid(b):
                            n = 8 * b + h
                            for q, i in enumerate(ORDER):
                                w = (i + 1) * PT_
                                act.wait_ge(s_s, 3 * n + q + 1)
                                nc.scalar.activation(P[:, h % 4, SEG[q]:SEG[q] + w], P[:, h % 4, SEG[q]:SEG[q] + w],
                                                     ACT.Exp, bias=nmax[:, h % 4, q:q + 1], scale=-1.0,
                                                     accum_out=psum_[:, h % 4, q:q + 1]).then_inc(s_ex, 1)
                        m = b if h >= 2 else b - 1
                        if valid(m):
                            n, hh = 8 * m + (h - 2) % 8, (h - 2) % 4
                            act.wait_ge(s_tp, 2 * n + 2)
                            wait(act, s_pv, 4 * m + ((h - 2) % 8) // 2 - 1)
                            nc.scalar.copy(PT[:, hh, N:2 * N], bT[1][:PT_, :N]).then_inc(s_pt1, 1)
                        m, c = (b, 3) if h == 0 else (b + 1, h // 2 - 1)
                        if h % 2 == 0 and valid(m):
                            for q in range(2):
                                n = 8 * m + 2 * c + q
                                act.wait_ge(s_qkp, n + 1)
                                wait(act, s_t1, n - 1)
                                nc.scalar.activation(tap0[:, q], (G0, G1)[q][:, 0:N], ACT.Copy,
                                                     scale=qkd[:, q, c, 0:1]).then_inc(s_t0, 1)
                        m, c = (b, h // 2 - 2) if h >= 4 else (b - 1, h // 2 + 2)
                        if h % 2 == 0 and valid(m):
                            act.wait_ge(s_pv, 4 * m + c + 1)
                            wait(act, s_wo, m)
                            nc.scalar.copy(OT[:, c], bO[:, :N]).then_inc(s_o, 1)
                        if h >= 2 and valid(b + 3):
                            m, k = b + 3, h - 2
                            act.wait_ge(s_ov, 6 * m + k + 1)
                            wait(act, s_ein, m)
                            nc.scalar.activation(Wt[:, k], overlap[:, k % 2], ACT.Relu).then_inc(s_wt, 1)
                        if h in (3, 5, 7) and valid(b + 1):
                            m, t = b + 1, (h - 3) // 2
                            act.wait_ge(s_vp, 3 * m + t + 1)
                            wait(act, s_pv, 4 * (m - 1))
                            nc.scalar.copy(V[:, 1 - u, t], G0[:PT_, :]).then_inc(s_v, 1)
                        if h == 4 and valid(b + 2):
                            m = b + 2
                            act.wait_ge(s_xtp, m + 1)
                            act.wait_ge(s_pad, 1)
                            nc.scalar.activation(xnT[:, u, 2:XPAD], G2[:, :N], ACT.Identity, bias=betac[:, 0:1],
                                                 scale=gammac[:, 0:1]).then_inc(s_xt, 1)
                        if h == 6 and valid(b - 1):
                            m = b - 1
                            act.wait_ge(s_ttp, m + 1)
                            wait(act, s_tts, 16 * m)
                            wait(act, s_lp, m)
                            nc.scalar.copy(tT[:], G2[:, :N]).then_inc(s_tt, 1)
                        if h == 7 and valid(b - 1):
                            m = b - 1
                            act.wait_ge(s_lm, 2 * m + 2)
                            nc.scalar.activation(lg[:], lg[:], ACT.Exp).then_inc(s_le, 1)

                bodies(act, body)

            @block.gpsimd
            def _(pool):
                nc.gpsimd.memset(xnT[:, :, 0:2], 0.0).then_inc(s_pad, 1)

                def rsqrt(ve, r, mv, sem_, n, dve_sem, dve_n):
                    wait_apart(pool, dve_sem, dve_n, s_on[1])
                    nc.gpsimd.tensor_scalar(ve[:], mv[:, :, 1], EPS, None, ALU.add).then_inc(sem_, 1)
                    pool.wait_ge(sem_, n + 1)
                    nc.gpsimd.tensor_tensor(r[:], ve[:], mhalf[:], ALU.pow).then_inc(sem_, 1)

                def body(b, u):
                    for h in range(HEADS):
                        if valid(b + 2):
                            m, base = b + 2, (2 * LN + 1) * (b + 2)
                            if h == 1:
                                rsqrt(lnve, lnr, lnmv, s_lnp, 4 * m, s_lnd, base + 7)
                            if h == 2:
                                rsqrt(lnve, lnr, lnmv, s_lnp, 4 * m + 2, s_lnd, base + LN + 7)
                        if h == 4 and valid(b - 1):
                            m = b - 1
                            rsqrt(gve, gr, gmv, s_gp, 2 * m, s_g, (LN + 1) * m + 7)

                bodies(pool, body)

            @block.vector
            def _(dve):
                def ln_stats(src, stat, mv, s, n):
                    for t in range(NT):
                        nc.vector.bn_stats(stat[:, t], src(t)).then_inc(s, 1)
                    for t in range(NT):
                        wait_apart(dve, s, n + t + 1, s_on[0])
                        nc.vector.bn_aggr(mv[:, t], stat[:, t]).then_inc(s, 1)

                def ln_apply(dst, src, mv, r, s):
                    for t in range(NT):
                        nc.vector.tensor_scalar(dst[:, t, 0:C], src(t), mv[:, t, 0:1], r[:, t:t + 1],
                                                ALU.subtract, ALU.mult).then_inc(s, 1)

                def body(b, u):
                    for h in range(HEADS):
                        m = b if h else b - 1
                        if valid(m):
                            n, hh = 8 * m + (h - 1) % 8, (h - 1) % 4
                            dve.wait_ge(s_ex, 3 * n + 3)
                            nc.vector.reciprocal(prec[:, hh], psum_[:, hh]).then_inc(s_rc, 1)
                            dve.wait_ge(s_rc, n + 1)
                            for q, i in enumerate(ORDER):
                                w = (i + 1) * PT_
                                nc.vector.tensor_scalar(P[:, hh, SEG[q]:SEG[q] + w], P[:, hh, SEG[q]:SEG[q] + w],
                                                        prec[:, hh, q:q + 1], None, ALU.mult).then_inc(s_pn, 1)
                        if valid(b):
                            n = 8 * b + h
                            wait(dve, s_tp, 2 * (n - 3))
                            for q, i in enumerate(ORDER):
                                w, at = (i + 1) * PT_, 0 if i != 1 else PT_
                                if q < 2:
                                    wait_apart(dve, s_sp, 2 * n + q + 1, s_on[0])
                                nc.vector.tensor_tensor_reduce(
                                    out=P[:, h % 4, SEG[q]:SEG[q] + w], in0=bS[min(q, 1)][:PT_, at:at + w],
                                    in1=nbias[:, h, (2 - i) * PT_:N], scale=1.0, scalar=MASKED, op0=ALU.add,
                                    op1=ALU.min, accum_out=nmax[:, h % 4, q:q + 1]).then_inc(s_s, 1)
                        m = b if h >= 2 else b - 1
                        if valid(m):
                            n, hh = 8 * m + (h - 2) % 8, (h - 2) % 4
                            dve.wait_ge(s_tp, 2 * n + 1)
                            wait(dve, s_pv, 4 * m + ((h - 2) % 8) // 2 - 1)
                            nc.vector.tensor_copy(PT[:, hh, 0:N], bT[0][:PT_, :N]).then_inc(s_pt0, 1)
                        if h == 0 and valid(b - 2):
                            m = b - 2
                            dve.wait_ge(s_le, m + 1)
                            nc.vector.reduce_sum(lsum[:], lg[:], AX_X).then_inc(s_lf, 1)
                            dve.wait_ge(s_lf, 3 * m + 1)
                            nc.vector.reciprocal(lrec[:], lsum[:]).then_inc(s_lf, 1)
                            dve.wait_ge(s_lf, 3 * m + 2)
                            nc.vector.tensor_tensor(row[:, :, C:ROW], lg[:],
                                                    lrec[:, :, None].broadcast_to([PT_, NT, E]),
                                                    ALU.mult).then_inc(s_lf, 1)
                        m, c = (b, 3) if h == 0 else (b + 1, h // 2 - 1)
                        if h % 2 == 0 and valid(m):
                            for q in range(2):
                                n = 8 * m + 2 * c + q
                                ps = (G0, G1)[q]
                                dve.wait_ge(s_t0, n + 1)
                                nc.vector.scalar_tensor_tensor(out=tap1[:, q], in0=ps[:, 1:N + 1],
                                                               scalar=qkd[:, q, c, 1:2], in1=tap0[:, q],
                                                               op0=ALU.mult, op1=ALU.add).then_inc(s_t1, 1)
                                dve.wait_ge(s_t1, n + 1)
                                wait(dve, s_sp, 16 * (m - 1) + 4 * c + 4)
                                nc.vector.scalar_tensor_tensor(out=QK[:, q, c], in0=ps[:, 2:N + 2],
                                                               scalar=qkd[:, q, c, 2:3], in1=tap1[:, q],
                                                               op0=ALU.mult, op1=ALU.add).then_inc(s_qk, 1)
                        if h == 1 and valid(b + 2):
                            m, base = b + 2, (2 * LN + 1) * (b + 2)
                            dve.wait_ge(s_ein, m + 1)
                            nc.vector.tensor_copy(Hall[:, m], G2[:PT_, :NT * C].rearrange("p (t c) -> p t c", c=C)
                                                  ).then_inc(s_lnd, 1)
                            wait_apart(dve, s_lnd, base + 1, s_on[0])
                            ln_stats(lambda t: Hall[:, m, t], lnstat, lnmv, s_lnd, base + 1)
                        if h == 2 and valid(b + 2):
                            m, base = b + 2, (2 * LN + 1) * (b + 2)
                            dve.wait_ge(s_lnp, 4 * m + 2)
                            ln_apply(n1, lambda t: Hall[:, m, t], lnmv, lnr, s_lnd)
                            dve.wait_ge(s_lnd, base + LN + 1)
                            ln_stats(lambda t: n1[:, t], lnstat, lnmv, s_lnd, base + LN + 1)
                        if h == 3 and valid(b + 2):
                            m, base = b + 2, (2 * LN + 1) * (b + 2)
                            dve.wait_ge(s_lnp, 4 * m + 4)
                            wait(dve, s_xtp, m)
                            ln_apply(n2, lambda t: n1[:, t], lnmv, lnr, s_lnd)
                        if h == 1 and valid(b - 2):
                            m = b - 2
                            dve.wait_ge(s_pp, m + 1)
                            wait(dve, s_ps, 16 * m)
                            nc.vector.tensor_copy(pTs[:], G1[:E, :N]).then_inc(s_pc, 1)
                        if h == 1 and valid(b + 3):
                            m = b + 3
                            wait(dve, s_wt, 6 * m)
                            nc.vector.tensor_copy(csb[:], csT[:, :, m]).then_inc(s_csb, 1)
                        if h == 3 and valid(b - 1):
                            m, base = b - 1, (LN + 1) * (b - 1)
                            dve.wait_ge(s_wo, m + 1)
                            nc.vector.tensor_tensor(Hall[:, m], Hall[:, m],
                                                    G2[:PT_, :NT * C].rearrange("p (t c) -> p t c", c=C),
                                                    ALU.add).then_inc(s_g, 1)
                            wait_apart(dve, s_g, base + 1, s_on[0])
                            ln_stats(lambda t: Hall[:, m, t], gstat, gmv, s_g, base + 1)
                        if h == 5 and valid(b - 1):
                            m = b - 1
                            dve.wait_ge(s_gp, 2 * m + 2)
                            wait(dve, s_tab, 16 * m)
                            wait(dve, s_ttp, m)
                            wait(dve, s_pp, m)
                            ln_apply(row, lambda t: Hall[:, m, t], gmv, gr, s_g)
                        if h == 7 and valid(b - 1):
                            m = b - 1
                            dve.wait_ge(s_lp, m + 1)
                            nc.vector.reduce_max(lmax[:], G1[:PT_, :NT * E].rearrange("p (t e) -> p t e", e=E),
                                                 AX_X).then_inc(s_lm, 1)
                            dve.wait_ge(s_lm, 2 * m + 1)
                            nc.vector.tensor_tensor(lg[:], G1[:PT_, :NT * E].rearrange("p (t e) -> p t e", e=E),
                                                    lmax[:, :, None].broadcast_to([PT_, NT, E]),
                                                    ALU.subtract).then_inc(s_lm, 1)
                        if h >= 2 and valid(b + 3):
                            m, k = b + 3, h - 2
                            dve.wait_ge(s_csb, m + 1)
                            wait(dve, s_ov, 6 * m + k)
                            nc.vector.tensor_scalar(cellmax[:], grid0[:], csb[:, TT_ + k:TT_ + k + 1], None,
                                                    ALU.max).then_inc(s_cm, 1)
                            dve.wait_ge(s_cm, 6 * m + k + 1)
                            wait(dve, s_wt, 6 * m + k - 1)
                            nc.vector.scalar_tensor_tensor(out=overlap[:, k % 2], in0=grid1[:], scalar=csb[:, k:k + 1],
                                                           in1=cellmax[:], op0=ALU.min,
                                                           op1=ALU.subtract).then_inc(s_ov, 1)

                bodies(dve, body)


        with ExitStack() as three:
            def sb_(name, shape, dt=F32):
                return three.enter_context(nc.sbuf_tensor(name, shape, dt))

            def sem(name):
                return three.enter_context(nc.semaphore(name))

            TOPBIT = 29
            hS = sb_("hS", [128, 2, DC, N])
            oS = sb_("oS", [PT_, 2, NT, C])
            diff = sb_("diff", [128, 128], I32)
            step = sb_("step", [128, 2], I32)
            cand = sb_("cand", [128, 1], I32)
            grow = sb_("grow", [128, 1], I32)
            flags = sb_("flags", [128, 2 * N])

            s_c = sem("s_pool_consts2")
            s_i = sem("s_dve_consts2")
            s_h = sem("s_shared_h_in_psum")
            s_hr = sem("s_shared_h_ready")
            s_y = sem("s_shared_y_in_psum")
            s_yr = sem("s_shared_steps")
            s_out = [sem(f"s_shared_stored{u}") for u in range(2)]
            s_n = sem("s_count_ready")
            s_tot = sem("s_total_in_psum")
            s_thr = sem("s_threshold_steps")

            block = three.enter_context(nc.Block())

            @block.gpsimd
            def _(pool):
                nc.gpsimd.iota(diff[:], pattern=[[-1, 128]], base=128, channel_multiplier=1).then_inc(s_c, 1)
                pool.wait_ge(s_i, 2)
                nc.gpsimd.affine_select(out=before[:], in_=same[:], compare_op=ALU.is_gt, fill=0.0, base=0,
                                        pattern=[[1, 128]], channel_multiplier=-1).then_inc(s_c, 1)

            @block.sync
            def _(sp):
                with sp.Fori(0, B // 2) as i:
                    for u in range(2):
                        sp.wait_ge(s_yr, 2 * (2 * i + u) + 2)
                        sp.dma_start(out[2 * i + u].rearrange("(t p) c -> p t c", p=PT_), oS[:, u]
                                     ).then_inc(s_out[u], 16)
                for u in range(2):
                    sp.wait_ge(s_out[u], 16 * (B // 2))

            @block.tensor
            def _(pe):
                def total(n):
                    pe.wait_ge(s_n, n + 1)
                    nc.tensor.matmul(bank[4][:, 0:1], same[:], cnt[:, 0:1], start=True, stop=True).then_inc(s_tot, 1)

                pe.wait_ge(s_i, 2)
                with pe.Fori(0, B // 2) as i:
                    for u in range(2):
                        b = 2 * i + u
                        for m in range(DC):
                            if m >= 2:
                                pe.wait_ge(s_hr, 4 * b + m - 1)
                            elif u == 1:
                                pe.wait_ge(s_hr, 8 * i + 4)
                            else:
                                pe.wait_ge(s_hr, 8 * i)
                            nc.tensor.matmul(bank[m % 2][:, :N], SW1[:, m * 128:(m + 1) * 128],
                                             tTall[:, bass.ds(b * N, N)], start=True, stop=True).then_inc(s_h, 1)
                        total(2 * b)
                        pe.wait_ge(s_hr, 4 * b + 4)
                        pe.wait_ge(s_yr, 2 * b)
                        for t in range(NT):
                            for k in range(DC):
                                last = nc.tensor.matmul(bank[2 + u][:PT_, t * C:(t + 1) * C],
                                                        hS[:, u, k, t * PT_:(t + 1) * PT_], SW2[:, k],
                                                        start=(k == 0), stop=(k == DC - 1))
                        last.then_inc(s_y, 1)
                        total(2 * b + 1)
            @block.scalar
            def _(act):
                with act.Fori(0, B // 2) as i:
                    for u in range(2):
                        b = 2 * i + u
                        for m in range(DC):
                            act.wait_ge(s_h, 4 * b + m + 1)
                            if m == 0 and u == 0:
                                act.wait_ge(s_y, 2 * i)
                            nc.scalar.activation(hS[:, u, m], bank[m % 2][:, :N], ACT.Gelu_apprx_tanh,
                                                 bias=sb1c[:, m:m + 1]).then_inc(s_hr, 1)

            @block.vector
            def _(dve):
                def count(n):
                    nc.vector.tensor_scalar(flags[:], probsT[:], cand[:, 0:1].bitcast(F32), 0.0, ALU.is_ge, ALU.add,
                                            accum_out=cnt[:, 0:1]).then_inc(s_n, 1)

                def decide(n, k):
                    dve.wait_ge(s_tot, n + 1)
                    nc.vector.scalar_tensor_tensor(out=grow[:], in0=bank[4][:, 0:1], scalar=float(CAP),
                                                   in1=step[:, k:k + 1], op0=ALU.is_ge, op1=ALU.mult).then_inc(s_thr, 1)
                    dve.wait_ge(s_thr, 4 * n + 1)
                    nc.vector.scalar_tensor_tensor(out=cand[:], in0=grow[:], scalar=thr[:, 0:1],
                                                   in1=step[:, 1 - k:2 - k], op0=ALU.bitwise_or,
                                                   op1=ALU.bitwise_or).then_inc(s_thr, 1)
                    dve.wait_ge(s_thr, 4 * n + 2)
                    count(n + 1)
                    nc.vector.tensor_tensor(thr[:], thr[:], grow[:], ALU.bitwise_or).then_inc(s_thr, 1)
                    nc.vector.tensor_scalar(step[:, k:k + 1], step[:, 1 - k:2 - k], 1, None,
                                            ALU.logical_shift_right).then_inc(s_thr, 1)
                    dve.wait_ge(s_thr, 4 * n + 4)

                dve.wait_ge(s_c, 1)
                nc.vector.tensor_scalar(diff[:], diff[:], E - 1, None, ALU.bitwise_and).then_inc(s_i, 1)
                dve.wait_ge(s_i, 1)
                nc.vector.tensor_scalar(same[:], diff[:], 0.0, None, ALU.is_equal).then_inc(s_i, 1)
                nc.vector.memset(thr[:], 0).then_inc(s_i, 1)
                nc.vector.memset(cand[:], 1 << TOPBIT).then_inc(s_i, 1)
                nc.vector.memset(step[:, 0:1], 1 << TOPBIT).then_inc(s_i, 1)
                nc.vector.memset(step[:, 1:2], 1 << (TOPBIT - 1)).then_inc(s_i, 1)
                dve.wait_ge(s_i, 6)
                count(0)
                with dve.Fori(0, B // 2) as i:
                    for u in range(2):
                        b = 2 * i + u
                        decide(2 * b, 0)
                        dve.wait_ge(s_y, b + 1)
                        dve.wait_ge(s_out[u], 16 * i)
                        nc.vector.tensor_tensor(oS[:, u], bank[2 + u][:PT_, :NT * C].rearrange(
                            "p (t c) -> p t c", c=C), Hall[:, b], ALU.add).then_inc(s_yr, 1)
                        dve.wait_ge(s_yr, 2 * b + 1)
                        nc.vector.tensor_tensor(oS[:, u], oS[:, u], sb2b[:, None, :].broadcast_to([PT_, NT, C]),
                                                ALU.add).then_inc(s_yr, 1)
                        decide(2 * b + 1, 1)

        mid.close()

        with ExitStack() as lst:
            def sb_(name, shape, dt=F32):
                return lst.enter_context(nc.sbuf_tensor(name, shape, dt))

            def sem(name):
                return lst.enter_context(nc.semaphore(name))

            TILES = T // PT_
            PAIRS = B // 2
            SLOT = 32
            NA = -(-CAP // SLOT)
            AW = 16
            COLS = TILES * PAIRS * E
            GE = 4

            over = sb_("over", [128, 2 * N])
            tied = sb_("tied", [128, 2 * N])
            ties = sb_("ties", [128, 2 * N])
            room = sb_("room", [128, 2])
            chosen = sb_("chosen", [128, 2 * N])
            place = sb_("place", [128, 2 * N])
            ones_r = sb_("ones_r", [128, 2 * N])
            slot = sb_("slot", [PT_, COLS], I32)
            slot_a = sb_("slot_a", [PT_, COLS], I32)
            slot_b = sb_("slot_b", [PT_, COLS], I32)
            fa = sb_("fa", [PT_, COLS], BF16)
            fb = sb_("fb", [PT_, COLS], BF16)
            pidx = sb_("pidx", [PT_, 1])
            tidx = sb_("tidx", [PT_, PAIRS, TILES], BF16)
            tcol = sb_("tcol", [PT_, COLS], BF16)
            hotA = sb_("hotA", [PT_, COLS, 2, AW], BF16)
            hotB = sb_("hotB", [PT_, SLOT, COLS], BF16)
            diagi = sb_("diagi", [128, GE], I32)
            diag = sb_("diag", [128, GE])
            picked = sb_("picked", [128, E // GE, SLOT, GE])
            lists = sb_("lists", [128, E // GE, SLOT])
            listp = sb_("listp", [E * NT, 2, PT_])
            idxf = sb_("idxf", [E * NT, PT_])
            list_dram = nc.dram_tensor("list_scratch", (2, E, NA * SLOT), F32, kind="Internal").ap()

            s_c = sem("s_pool_consts3")
            s_i = sem("s_diagonal_steps")
            s_sel = sem("s_selection_steps")
            s_m = sem("s_selection_matmuls")
            s_hot = sem("s_onehot_steps")
            s_ls = sem("s_list_stored")
            s_ll = sem("s_list_loaded")

            HOT = 7 + 2 * NA + SLOT
            HOT_LISTS = HOT + E // GE + 1

            block = lst.enter_context(nc.Block())

            @block.gpsimd
            def _(pool):
                nc.gpsimd.iota(diagi[:], pattern=[[-2 * AW, GE]], base=0, channel_multiplier=1).then_inc(s_c, 1)
                nc.gpsimd.iota(pidx[:], pattern=[[0, 1]], base=0, channel_multiplier=1,
                               allow_small_or_imprecise_dtypes=True).then_inc(s_c, 1)
                nc.gpsimd.iota(tidx[:], pattern=[[TILES, PAIRS], [1, TILES]], base=0, channel_multiplier=0,
                               allow_small_or_imprecise_dtypes=True).then_inc(s_c, 1)
                nc.gpsimd.memset(ones_r[:], 1.0).then_inc(s_c, 1)
                nc.gpsimd.memset(hotA[:, :, :, NA:], 0.0).then_inc(s_c, 1)

            @block.sync
            def _(sp):
                sp.wait_ge(s_hot, HOT_LISTS)
                for v in range(2):
                    for e in range(GE):
                        r = (2 * e + v) * AW
                        sp.dma_start(list_dram[v, e::GE].rearrange("g (a b) -> a g b", b=SLOT),
                                     lists[r:r + NA]).then_inc(s_ls, 16)
                sp.wait_ge(s_ls, 16 * 2 * GE)
                for v in range(2):
                    for e in range(E):
                        sp.dma_start(listp[e * NT:(e + 1) * NT, v],
                                     list_dram[v, e, 0:CAP].rearrange("(k p) -> k p", p=PT_)).then_inc(s_ll, 16)
                sp.wait_ge(s_ll, 16 * 2 * E)
            @block.tensor
            def _(pe):
                pe.wait_ge(s_sel, 2)
                nc.tensor.matmul(bank[5][:, 0:1], same[:], cnt[:, 1:2], start=True, stop=True)
                nc.tensor.matmul(bank[5][:, 1:2], before[:], cnt[:, 2:3], start=True, stop=True).then_inc(s_m, 1)
                pe.wait_ge(s_sel, 8)
                nc.tensor.matmul(bank[6][:, 0:1], before[:], place[:, 2 * N - 1:2 * N], start=True,
                                 stop=True).then_inc(s_m, 1)
                pe.wait_ge(s_sel, 9)
                for j in range(TILES):
                    last = nc.tensor.transpose(bank[j // 3][:PT_, (j % 3) * 128:(j % 3 + 1) * 128],
                                               chosen[:, j * PT_:(j + 1) * PT_], ident[:])
                last.then_inc(s_m, 1)
                pe.wait_ge(s_hot, HOT)
                pe.wait_ge(s_c, 5)

                def collect(n, first, final):
                    for g in range(E // GE):
                        c0 = n * E + g * GE
                        last = nc.tensor.matmul(bank[g][:, 0:SLOT * GE],
                                                hotA2[:, bass.ds(c0 * 2 * AW, GE * 2 * AW)],
                                                hotB[:, :, bass.ds(c0, GE)], start=first, stop=final)
                    return last

                hotA2 = hotA[:].rearrange("p c v a -> p (c v a)")
                collect(0, True, False)
                with pe.Fori(1, TILES * PAIRS - 1) as n:
                    collect(n, False, False)
                collect(TILES * PAIRS - 1, False, True).then_inc(s_m, 1)
                pe.wait_ge(s_hot, HOT_LISTS + 1)
                nc.tensor.transpose(bank[5][:PT_, :E * NT], idxf[:], ident[:E * NT, :E * NT]).then_inc(s_m, 1)

            @block.vector
            def _(dve):
                dve.wait_ge(s_c, 4)
                nc.vector.tensor_scalar(over[:], probsT[:], thr[:, 0:1].bitcast(F32), 0.0, ALU.is_gt, ALU.add,
                                        accum_out=cnt[:, 1:2]).then_inc(s_sel, 1)
                nc.vector.tensor_scalar(tied[:], probsT[:], thr[:, 0:1].bitcast(F32), 0.0, ALU.is_equal, ALU.add,
                                        accum_out=cnt[:, 2:3]).then_inc(s_sel, 1)
                dve.wait_ge(s_sel, 2)
                nc.vector.tensor_tensor_scan(ties[:], ones_r[:], tied[:], 0.0, ALU.mult, ALU.add).then_inc(s_sel, 1)
                dve.wait_ge(s_m, 1)
                nc.vector.tensor_scalar(room[:, 0:1], bank[5][:, 0:1], -1.0, float(CAP), ALU.mult,
                                        ALU.add).then_inc(s_sel, 1)
                dve.wait_ge(s_sel, 4)
                nc.vector.tensor_tensor(room[:, 1:2], room[:, 0:1], bank[5][:, 1:2], ALU.subtract).then_inc(s_sel, 1)
                dve.wait_ge(s_sel, 5)
                nc.vector.scalar_tensor_tensor(out=ties[:], in0=ties[:], scalar=room[:, 1:2], in1=tied[:],
                                               op0=ALU.is_le, op1=ALU.mult).then_inc(s_sel, 1)
                dve.wait_ge(s_sel, 6)
                nc.vector.tensor_tensor(chosen[:], over[:], ties[:], ALU.add).then_inc(s_sel, 1)
                dve.wait_ge(s_sel, 7)
                nc.vector.tensor_tensor_scan(place[:], ones_r[:], chosen[:], 0.0, ALU.mult, ALU.add).then_inc(s_sel, 1)
                dve.wait_ge(s_sel, 8)
                dve.wait_ge(s_m, 2)
                nc.vector.scalar_tensor_tensor(out=chosen[:], in0=place[:], scalar=bank[6][:, 0:1], in1=chosen[:],
                                               op0=ALU.add, op1=ALU.mult).then_inc(s_sel, 1)
                dve.wait_ge(s_m, 3)
                for n in range(2):
                    nc.vector.tensor_scalar(slot[:, n * 384:(n + 1) * 384], bank[n][:PT_, :384], -1.0, None,
                                            ALU.add).then_inc(s_hot, 1)
                dve.wait_ge(s_hot, 2)
                nc.vector.tensor_scalar(slot_a[:], slot[:], 5, None, ALU.arith_shift_right).then_inc(s_hot, 1)
                nc.vector.tensor_scalar(slot_b[:], slot[:], SLOT - 1, None, ALU.bitwise_and).then_inc(s_hot, 1)
                dve.wait_ge(s_hot, 4)
                nc.vector.tensor_copy(fa[:], slot_a[:]).then_inc(s_hot, 1)
                nc.vector.tensor_copy(fb[:], slot_b[:]).then_inc(s_hot, 1)
                nc.vector.tensor_copy(tcol[:].rearrange("p (j s e) -> p j s e", j=TILES, e=E),
                                      tidx[:].rearrange("p s j -> p j s")[:, :, :, None].broadcast_to(
                                          [PT_, TILES, PAIRS, E])).then_inc(s_hot, 1)
                dve.wait_ge(s_hot, 7)
                for a in range(NA):
                    nc.vector.tensor_scalar(hotA[:, :, 0, a], fa[:], float(a), pidx[:, 0:1], ALU.is_equal,
                                            ALU.mult).then_inc(s_hot, 1)
                    nc.vector.scalar_tensor_tensor(out=hotA[:, :, 1, a], in0=fa[:], scalar=float(a), in1=tcol[:],
                                                   op0=ALU.is_equal, op1=ALU.mult).then_inc(s_hot, 1)
                for s in range(SLOT):
                    nc.vector.tensor_scalar(hotB[:, s], fb[:], float(s), None, ALU.is_equal).then_inc(s_hot, 1)
                nc.vector.tensor_scalar(diagi[:], diagi[:], 5, None, ALU.arith_shift_right).then_inc(s_i, 1)
                dve.wait_ge(s_i, 1)
                nc.vector.tensor_scalar(diag[:], diagi[:], 0.0, None, ALU.is_equal).then_inc(s_i, 1)
                dve.wait_ge(s_i, 2)
                dve.wait_ge(s_m, 4)
                for g in range(E // GE):
                    nc.vector.tensor_tensor(picked[:, g], bank[g][:, :SLOT * GE].rearrange("p (b e) -> p b e", e=GE),
                                            diag[:, None, :].broadcast_to([128, SLOT, GE]),
                                            ALU.mult).then_inc(s_hot, 1)
                dve.wait_ge(s_hot, HOT_LISTS - 1)
                nc.vector.reduce_sum(lists[:].rearrange("p g b -> p (g b)"),
                                     picked[:].rearrange("p g b e -> p (g b) e"), AX_X).then_inc(s_hot, 1)
                dve.wait_ge(s_ll, 16 * 2 * E)
                nc.vector.scalar_tensor_tensor(out=idxf[:], in0=listp[:, 1], scalar=float(PT_), in1=listp[:, 0],
                                               op0=ALU.mult, op1=ALU.add).then_inc(s_hot, 1)
                dve.wait_ge(s_m, 5)
                nc.vector.tensor_copy(idx[:].rearrange("p e k -> p (e k)"), bank[5][:PT_, :E * NT])

        with ExitStack() as four:
            def sb_(name, shape, dt=F32):
                return four.enter_context(nc.sbuf_tensor(name, shape, dt))

            def sem(name):
                return four.enter_context(nc.semaphore(name))

            RING = 4

            EW1 = sb_("EW1", [128, 2, D])
            EW2 = sb_("EW2", [128, 2, DC, C])
            EB1 = sb_("EB1", [128, 2, DC])
            EB2 = sb_("EB2", [PT_, 2, C])
            ids = [[sb_(f"ids{r}_{k}", [PT_, 1], U32) for k in range(NT)] for r in range(RING)]
            tok = sb_("tok", [PT_, RING, NT, ROW])
            tokT = sb_("tokT", [128, 2, N])
            hE = sb_("hE", [128, 2, DC, N])
            score = sb_("score", [PT_, 2, NT])
            yE = sb_("yE", [PT_, 2, NT, C])

            s_w = [sem(f"s_expert_weights{u}") for u in range(2)]
            s_id = sem("s_ids_ready")
            s_ga = [sem(f"s_tokens_gathered{r}") for r in range(RING)]
            s_tp = sem("s_tokT_in_psum")
            s_tc = sem("s_tokT_ready")
            s_scr = sem("s_scores_taken")
            s_h = sem("s_expert_h_in_psum")
            s_hr = sem("s_expert_h_ready")
            s_y = sem("s_expert_y_in_psum")
            s_yb = sem("s_expert_y_biased")
            s_ys = sem("s_expert_y_scored")
            s_sc = sem("s_scattered")
            s_on = [sem(f"s_waits_passed{n}") for n in range(2)]

            block = four.enter_context(nc.Block())

            @block.sync
            def _(sp):
                def load(e, u):
                    sp.dma_start(EW1[:, u], ew1[e]).then_inc(s_w[u], 16)
                    sp.dma_start(EW2[:, u], ew2[e].rearrange("(k p) n -> p k n", p=128)).then_inc(s_w[u], 16)
                    sp.dma_start(EB1[:, u], eb1[e].rearrange("(m p) -> p m", p=128)).then_inc(s_w[u], 16)
                    sp.dma_start(EB2[:, u], eb2[e].rearrange("(o n) -> o n", o=1).broadcast_to([PT_, C])
                                 ).then_inc(s_w[u], 16)

                for u in range(2):
                    load(u, u)
                with sp.Fori(1, E // 2) as i:
                    for u in range(2):
                        sp.wait_ge(s_yb, 2 * i + u - 1)
                        load(2 * i + u, u)

            @block.gpsimd
            def _(pool):
                def gather(e, r):
                    wait_apart(pool, s_id, e + 1, s_on[1])
                    for k in range(NT):
                        nc.gpsimd.indirect_dma_start(
                            out=tok[:, r, k], out_offset=None, in_=table,
                            in_offset=bass.IndirectOffsetOnAxis(ap=ids[r][k][:, 0:1], axis=0)).then_inc(s_ga[r], 16)

                def scatter(e, r):
                    pool.wait_ge(s_ys, NT * (e + 1))
                    wait_apart(pool, s_sc, 16 * NT * e, s_on[1])
                    for k in range(NT):
                        nc.gpsimd.indirect_dma_start(
                            out=out_rows, out_offset=bass.IndirectOffsetOnAxis(ap=ids[r][k][:, 0:1], axis=0),
                            in_=yE[:, r % 2, k], in_offset=None, compute_op=ALU.add,
                            bounds_check=TOK - 1, oob_is_err=True).then_inc(s_sc, 16)

                gather(0, 0)
                gather(1, 1)
                with pool.Fori(0, E // RING) as i:
                    for r in range(RING):
                        gather(RING * i + r + 2, (r + 2) % RING)
                        scatter(RING * i + r, r)
                pool.wait_ge(s_sc, 16 * NT * E)
                for r in range(RING):
                    pool.wait_ge(s_ga[r], 16 * NT * (E // RING + (r < 2)))

            @block.tensor
            def _(pe):
                def transpose_tokens(e, r, turn):
                    pe.wait_ge(s_ga[r], 16 * NT * (turn + 1))
                    wait(pe, s_tc, e)
                    for k in range(NT):
                        last = nc.tensor.transpose(bank[6][:, k * PT_:(k + 1) * PT_], tok[:, r, k, 0:C],
                                                   ident[:PT_, :PT_])
                    last.then_inc(s_tp, 1)

                transpose_tokens(0, 0, 0)
                with pe.Fori(0, E // RING) as i:
                    for r in range(RING):
                        e, u = RING * i + r, r % 2
                        pe.wait_ge(s_w[u], 16 * 4 * (2 * i + r // 2 + 1))
                        pe.wait_ge(s_tc, e + 1)
                        for m in range(DC):
                            pe.wait_ge(s_hr, 4 * e + (m - 1 if m >= 2 else 0))
                            nc.tensor.matmul(bank[m % 2][:, :N], EW1[:, u, m * 128:(m + 1) * 128], tokT[:, u],
                                             start=True, stop=True).then_inc(s_h, 1)
                        transpose_tokens(e + 1, (r + 1) % RING, i + (r == RING - 1))
                        pe.wait_ge(s_hr, 4 * e + 4)
                        pe.wait_ge(s_yb, e)
                        for t in range(NT):
                            for k in range(DC):
                                last = nc.tensor.matmul(bank[2 + u][:PT_, t * C:(t + 1) * C],
                                                        hE[:, u, k, t * PT_:(t + 1) * PT_], EW2[:, u, k],
                                                        start=(k == 0), stop=(k == DC - 1))
                        last.then_inc(s_y, 1)

            @block.scalar
            def _(act):
                with act.Fori(0, E // RING) as i:
                    for r in range(RING):
                        e, u = RING * i + r, r % 2
                        for m in range(DC):
                            act.wait_ge(s_h, 4 * e + m + 1)
                            nc.scalar.activation(hE[:, u, m], bank[m % 2][:, :N], ACT.Gelu_apprx_tanh,
                                                 bias=EB1[:, u, m:m + 1]).then_inc(s_hr, 1)

            @block.vector
            def _(dve):
                def take_ids(e, r):
                    for k in range(NT):
                        last = nc.vector.tensor_copy(ids[r][k][:], idx[:, e, k:k + 1])
                    last.then_inc(s_id, 1)

                def take_tokens(e, r, turn, column):
                    dve.wait_ge(s_tp, e + 1)
                    nc.vector.tensor_copy(tokT[:, r % 2], bank[6][:, :N]).then_inc(s_tc, 1)
                    wait(dve, s_ys, NT * (e - 1))
                    nc.vector.tensor_copy(score[:, r % 2], tok[:, r, :, bass.ds(C + column, 1)].rearrange(
                        "p k o -> p (k o)")).then_inc(s_scr, 1)

                take_ids(0, 0)
                take_ids(1, 1)
                take_tokens(0, 0, 0, 0)
                with dve.Fori(0, E // RING) as i:
                    for r in range(RING):
                        e, u = RING * i + r, r % 2
                        dve.wait_ge(s_sc, 16 * NT * (e - 1) if r else 16 * NT * RING * i)
                        take_ids((e + 2) % E, (r + 2) % RING)
                        take_tokens(e + 1, (r + 1) % RING, i + (r == RING - 1), (e + 1) % E)
                        dve.wait_ge(s_y, e + 1)
                        dve.wait_ge(s_scr, e + 1)
                        nc.vector.tensor_tensor(yE[:, u], bank[2 + u][:PT_, :NT * C].rearrange(
                            "p (t c) -> p t c", c=C), EB2[:, u, None, :].broadcast_to([PT_, NT, C]),
                            ALU.add).then_inc(s_yb, 1)
                        dve.wait_ge(s_yb, e + 1)
                        for k in range(NT):
                            nc.vector.tensor_scalar(yE[:, u, k], yE[:, u, k], score[:, u, k:k + 1], None,
                                                    ALU.mult).then_inc(s_ys, 1)


_INS = ['x', 'L0_tok_W1', 'L0_tok_b1', 'L0_tok_W2', 'L0_tok_b2', 'L0_tok_W3', 'L0_tok_b3', 'L0_attn_gamma',
        'L0_attn_beta', 'L0_attn_wq1', 'L0_attn_wqd', 'L0_attn_wk1', 'L0_attn_wkd', 'L0_attn_wv1', 'L0_attn_wvd',
        'L0_attn_wout', 'L0_ffn_gate_w', 'L0_ffn_w1', 'L0_ffn_b1', 'L0_ffn_w2', 'L0_ffn_b2', 'L0_ffn_sw1',
        'L0_ffn_sb1', 'L0_ffn_sw2', 'L0_ffn_sb2']
_OUTS = [((B, N, C), 'float32')]


def kernel(**inputs):
    import numpy as _np
    import concourse.bacc as _bacc
    from concourse import mybir as _mybir
    from concourse.bass_utils import run_bass_kernel_spmd as _run

    nc = _bacc.Bacc("TRN2", target_bir_lowering=False, num_devices=1)
    arrays, args = {}, []
    for name in _INS:
        a = _np.ascontiguousarray(inputs[name])
        arrays[f"in_{name}_dram"] = a
        args.append(nc.dram_tensor(f"in_{name}_dram", a.shape, _mybir.dt.from_np(a.dtype), kind="ExternalInput").ap())
    for i, (shape, dtype) in enumerate(_OUTS):
        dt = _mybir.dt.from_np(_np.dtype(dtype))
        args.append(nc.dram_tensor(f"out_{i}_dram", shape, dt, kind="ExternalOutput").ap())
    build(nc, *args)
    r = _run(nc, [arrays], core_ids=[0])
    got = tuple(r.results[0][f"out_{i}_dram"] for i in range(len(_OUTS)))
    return got[0]
```

```python
import concourse.bass as bass
from concourse import mybir
from contextlib import ExitStack

F32 = mybir.dt.float32
F32R = mybir.dt.float32r
I32 = mybir.dt.int32
U32 = mybir.dt.uint32
BF16 = mybir.dt.bfloat16
ALU = mybir.AluOpType
ACT = mybir.ActivationFunctionType
AX_X = mybir.AxisListType.X

B, T, C = 16, 750, 128
N = T // 2
PT_ = 125
TT_, NT = T // PT_, N // PT_
D = 512
DC = D // 128
HEADS, DH = 8, 64
E = 16
TOK = B * N
CAP = TOK // E
NE = N + 1
ROW = C + E
TEMP, EPS = 1e-5, 1e-5
MASKED = 3.4028234663852886e38


def slopes(heads):
    return [2.0 ** (-8.0 * (h + 1) / heads) for h in range(heads)]


def wait(eng, sem, value):
    if isinstance(value, int) and value <= 0:
        return
    eng.wait_ge(sem, value)


def wait_apart(eng, sem, value, passed):
    wait(eng, sem, value)
    if not isinstance(value, int):
        eng.sem_inc(passed, 1)


def cap(value, most):
    return min(value, most) if isinstance(value, int) else value


def valid(m):
    return not isinstance(m, int) or 0 <= m < B


def build(nc, x, tW1, tb1, tW2, tb2, tW3, tb3, gamma, beta, wq1, wqd, wk1, wkd, wv1, wvd, wout,
          gate_w, ew1, eb1, ew2, eb2, sw1, sb1, sw2, sb2, out):
    ctx = ExitStack()
    with ctx:
        ctx.enter_context(nc.allow_non_contiguous_dma(reason="short vectors, once"))

        def sb(name, shape, dt=F32):
            return ctx.enter_context(nc.sbuf_tensor(name, shape, dt))

        mid = ctx.enter_context(ExitStack())

        def sbm(name, shape, dt=F32):
            return mid.enter_context(nc.sbuf_tensor(name, shape, dt))

        def sem(name):
            return ctx.enter_context(nc.semaphore(name))

        z_dram = nc.dram_tensor("z_scratch", (B, DC, T), F32, kind="Internal").ap()
        table = nc.dram_tensor("token_table", (TOK, ROW), F32, kind="Internal").ap()
        probs_dram = nc.dram_tensor("probs_scratch", (B, E, N), F32, kind="Internal").ap()
        table_b = table.rearrange("(b n) c -> b n c", n=N)

        bank = [ctx.enter_context(nc.psum_tensor(f"bank{i}", [128, 512], F32)) for i in range(8)]

        ident = sb("ident", [128, 128])
        gammac = sb("gammac", [128, 1])
        betac = sb("betac", [128, 1])
        sb1c = sb("sb1c", [128, DC])
        mhalf = sb("mhalf", [PT_, NT])
        probsT = sb("probsT", [128, 2 * N])
        idx = sb("idx", [PT_, E, NT], U32)
        thr = sb("thr", [128, 1], I32)
        cnt = sb("cnt", [128, 4])
        same = sb("same", [128, 128])
        before = sb("before", [128, 128])

        qkd = sbm("qkd", [128, 2, DC, 3])
        vd = sbm("vd", [128, DC, 3])
        WQKT = sbm("WQKT", [128, 2, 2, D], F32R)
        WVT = sbm("WVT", [128, 2, 3, D], F32R)
        WOT = sbm("WOT", [128, DC, 128])
        gate = sbm("gate", [128, E])
        SW1 = sbm("SW1", [128, D])
        SW2 = sbm("SW2", [128, DC, 128])
        sb2b = sbm("sb2b", [PT_, C])
        nbias = sbm("nbias", [PT_, HEADS, N])
        grid0 = sbm("grid0", [PT_, N])
        grid1 = sbm("grid1", [PT_, N])

        csT = sbm("csT", [PT_, 2 * TT_, B])

        Hall = sbm("Hall", [PT_, B, NT, C])
        tTall = sbm("tTall", [128, TOK])

        PASSES = ((0, 0), (0, 1), (1, 0))

        out_rows = out.rearrange("b n c -> (b n) c")

        with ExitStack() as one:
            def sb_(name, shape, dt=F32):
                return one.enter_context(nc.sbuf_tensor(name, shape, dt))

            def sem(name):
                return one.enter_context(nc.semaphore(name))

            W1 = tTall[:, 0:D]
            W2 = tTall[:, D:D + DC * D].rearrange("p (k n) -> p k n", n=D)
            W1hl = sb_("W1hl", [128, 2, D], F32R)
            W2hl = sb_("W2hl", [128, 2, DC, D], F32R)
            w3c = sb_("w3c", [128, DC])
            w3rep = sb_("w3rep", [128, DC, 32])
            b1c = sb_("b1c", [128, DC])
            b2c = sb_("b2c", [128, DC])
            b3c = sb_("b3c", [B, 1])
            wraw = sb_("wraw", [128, 3, DC, 128])
            wvtap = sb_("wvtap", [128, 3, DC, 128])
            woraw = sb_("woraw", [128, D])
            dist = sb_("dist", [PT_, N])
            zrow = sb_("zrow", [B, DC, T])
            imp = sb_("imp", [B, T])
            isum = sb_("isum", [B, 2])
            ones_t = sb_("ones_t", [B, T])
            cs = sb_("cs", [B, T + 1])
            X = sb_("X", [PT_, 2, TT_, C])
            xThl = sb_("xThl", [128, 2, 2, NE], F32R)
            h1 = sb_("h1", [128, DC, NE])
            h1hl = sb_("h1hl", [128, 2, 2, DC, NE], F32R)
            h2 = sb_("h2", [128, 2, DC, N])
            zsb = sb_("zsb", [128, 2, N])

            s_w = sem("s_tok_weights")
            s_w2 = sem("s_other_weights")
            s_wf = sem("s_first_weights")
            s_ws = sem("s_weights_split")
            s_xpad = sem("s_xT_padded")
            s_hs = sem("s_h1_split")
            s_high = sem("s_weights_high_part")
            s_pool = sem("s_pool_consts")
            s_id = sem("s_identity")
            s_w3 = sem("s_w3_replicated")
            s_prep = sem("s_scaled_weights")
            s_wt = sem("s_weights_transposed")
            s_wc = sem("s_weights_copied")
            s_x = [sem(f"s_x_loaded{u}") for u in range(2)]
            s_xp = sem("s_xT_in_psum")
            s_xt = sem("s_xT_ready")
            s_h1 = sem("s_h1_in_psum")
            s_g1 = sem("s_h1_ready")
            s_h2 = sem("s_h2_in_psum")
            s_g2 = sem("s_h2_ready")
            s_z = sem("s_z_in_psum")
            s_zc = sem("s_z_copied")
            s_zs = [sem(f"s_z_stored{u}") for u in range(2)]
            s_zl = sem("s_z_loaded")
            s_zsum = sem("s_z_steps")
            s_sig = sem("s_sigmoid_ready")
            s_cp = sem("s_cs_in_psum")

            block = one.enter_context(nc.Block())
            TOK_W, OTHER_W = 4, 14

            @block.sync
            def _(sp):
                sp.dma_start(X[:, 0], x[0].rearrange("(k p) c -> p k c", p=PT_)).then_inc(s_x[0], 16)
                sp.dma_start(W1, tW1).then_inc(s_wf, 16)
                sp.dma_start(b1c[:], tb1.rearrange("(m p) -> p m", p=128)).then_inc(s_wf, 16)
                sp.dma_start(W2, tW2.rearrange("(k p) n -> p k n", p=128)).then_inc(s_w, 16)
                sp.dma_start(b2c[:], tb2.rearrange("(m p) -> p m", p=128)).then_inc(s_w, 16)
                sp.dma_start(w3c[:], tW3.rearrange("(m p) o -> p (m o)", p=128)).then_inc(s_w, 16)
                sp.dma_start(b3c[:], tb3.rearrange("(o n) -> o n", o=1).broadcast_to([B, 1])).then_inc(s_w, 16)
                for n, w in enumerate((wq1, wk1, wv1)):
                    sp.dma_start(wraw[:, n], w.rearrange("(m p) d -> p m d", p=128)).then_inc(s_w2, 16)
                for n, w in enumerate((wqd, wkd)):
                    sp.dma_start(qkd[:, n], w.rearrange("(m p) a -> p m a", p=128)).then_inc(s_w2, 16)
                sp.dma_start(vd[:], wvd.rearrange("(m p) a -> p m a", p=128)).then_inc(s_w2, 16)
                sp.dma_start(woraw[:], wout).then_inc(s_w2, 16)
                sp.dma_start(gammac[:], gamma.rearrange("(p o) -> p o", o=1)).then_inc(s_w2, 16)
                sp.dma_start(betac[:], beta.rearrange("(p o) -> p o", o=1)).then_inc(s_w2, 16)
                sp.dma_start(gate[:], gate_w).then_inc(s_w2, 16)
                sp.dma_start(SW1[:], sw1).then_inc(s_w2, 16)
                sp.dma_start(SW2[:], sw2.rearrange("(k p) n -> p k n", p=128)).then_inc(s_w2, 16)
                sp.dma_start(sb1c[:], sb1.rearrange("(m p) -> p m", p=128)).then_inc(s_w2, 16)
                sp.dma_start(sb2b[:], sb2.rearrange("(o n) -> o n", o=1).broadcast_to([PT_, C])).then_inc(s_w2, 16)
                sp.dma_start(X[:, 1], x[1].rearrange("(k p) c -> p k c", p=PT_)).then_inc(s_x[1], 16)
                with sp.Fori(0, B // 2) as i:
                    for u in range(2):
                        for half in range(2):
                            sp.wait_ge(s_zc, 4 * i + 2 * u + half + 1)
                            sp.dma_start(z_dram[2 * i + u, :, half * N:(half + 1) * N],
                                         zsb[0:128:32, half]).then_inc(s_zs[half], 16)
                        sp.wait_ge(s_xp, 4 * i + 2 * u + 2)
                        nxt = (2 * i + u + 2) % B
                        sp.dma_start(X[:, u], x[nxt].rearrange("(k p) c -> p k c", p=PT_)).then_inc(s_x[u], 16)
                for half in range(2):
                    sp.wait_ge(s_zs[half], 16 * B)
                for u in range(2):
                    sp.wait_ge(s_x[u], 16 * (B // 2 + 1))
                sp.dma_start(zrow[:], z_dram).then_inc(s_zl, 16)
                sp.wait_ge(s_zl, 16)

            @block.gpsimd
            def _(pool):
                nc.gpsimd.memset(ident[:], 0.0).then_inc(s_pool, 1)
                pool.wait_ge(s_pool, 1)
                nc.gpsimd.affine_select(out=ident[:], in_=ident[:], compare_op=ALU.not_equal, fill=1.0, base=0,
                                        pattern=[[-1, 128]], channel_multiplier=1).then_inc(s_id, 1)
                nc.gpsimd.iota(dist[:], pattern=[[-1, N]], base=N - PT_, channel_multiplier=1,
                               allow_small_or_imprecise_dtypes=True).then_inc(s_pool, 1)
                nc.gpsimd.iota(grid0[:], pattern=[[1, N]], base=0, channel_multiplier=0,
                               allow_small_or_imprecise_dtypes=True).then_inc(s_pool, 1)
                nc.gpsimd.iota(grid1[:], pattern=[[1, N]], base=1, channel_multiplier=0,
                               allow_small_or_imprecise_dtypes=True).then_inc(s_pool, 1)
                pool.wait_ge(s_pool, 4)
                nc.gpsimd.memset(grid1[:, N - 1:N], 1e30).then_inc(s_pool, 1)
                nc.gpsimd.memset(mhalf[:], -0.5).then_inc(s_pool, 1)
                nc.gpsimd.memset(ones_t[:], 1.0).then_inc(s_pool, 1)
                nc.gpsimd.memset(cs[:, 0:1], 0.0).then_inc(s_pool, 1)
                for h, slope in enumerate(slopes(HEADS)):
                    nc.gpsimd.tensor_scalar(nbias[:, h], dist[:], slope, None, ALU.mult).then_inc(s_pool, 1)
                    pool.wait_ge(s_pool, 9 + 2 * h)
                    nc.gpsimd.affine_select(out=nbias[:, h], in_=nbias[:, h], compare_op=ALU.is_ge, fill=MASKED,
                                            base=N - PT_, pattern=[[-1, N]], channel_multiplier=1).then_inc(s_pool, 1)
                pool.wait_ge(s_w2, 16 * OTHER_W)
                nc.gpsimd.tensor_scalar(qkd[:, 0], qkd[:, 0], -(DH ** -0.5), None, ALU.mult).then_inc(s_prep, 1)
                for a in range(3):
                    for m in range(DC):
                        nc.gpsimd.tensor_scalar(wvtap[:, a, m], wraw[:, 2, m], vd[:, m, a:a + 1], None,
                                                ALU.mult).then_inc(s_prep, 1)

            split_jobs = [(wraw[:, n, m], WQKT[:, :, n, m * 128:(m + 1) * 128]) for n in range(2) for m in range(DC)]
            split_jobs += [(wvtap[:, a, m], WVT[:, :, a, m * 128:(m + 1) * 128]) for a in range(3) for m in range(DC)]
            jobs = split_jobs + [(woraw[:, m * 128:(m + 1) * 128], WOT[:, m]) for m in range(DC)]

            @block.tensor
            def _(pe):
                def layer1(g, p):
                    pe.wait_ge(s_xt, 2 * g + 2)
                    for m in range(DC):
                        wait(pe, s_g1, 4 * g + m - 1)
                        for n, (a, b) in enumerate(PASSES):
                            last = nc.tensor.matmul(bank[2 + m % 2][:, :NE], W1hl[:, a, m * 128:(m + 1) * 128],
                                                    xThl[:, p, b], start=(n == 0), stop=(n == 2))
                        last.then_inc(s_h1, 1)

                def layer2(g, p, ms):
                    pe.wait_ge(s_hs, 4 * g + 4)
                    for m in ms:
                        wait(pe, s_g2, 4 * g + m - 1)
                        for k in range(DC):
                            for n, (a, b) in enumerate(PASSES):
                                last = nc.tensor.matmul(bank[4 + m % 2][:, :NE],
                                                        W2hl[:, a, k, m * 128:(m + 1) * 128], h1hl[:, p, b, k],
                                                        start=(k == 0 and n == 0), stop=(k == DC - 1 and n == 2))
                        last.then_inc(s_h2, 1)

                def layer3(g, p):
                    pe.wait_ge(s_g2, 4 * g + 4)
                    wait(pe, s_zc, g - 1)
                    for c in range(DC):
                        last = nc.tensor.matmul(bank[6 + p][32 * c:32 * c + 32, :N], w3rep[:, c], h2[:, p, c],
                                                start=True, stop=True)
                    last.then_inc(s_z, 1)

                pe.wait_ge(s_id, 1)
                pe.wait_ge(s_x[0], 16)
                for k in range(3):
                    last = nc.tensor.transpose(bank[0][:, k * PT_:(k + 1) * PT_], X[:, 0, k], ident[:PT_, :PT_])
                last.then_inc(s_xp, 1)
                pe.wait_ge(s_ws, 1)
                layer1(0, 0)
                pe.wait_ge(s_w3, 1)
                pe.wait_ge(s_ws, 2)

                def two_batches(i):
                    for s in range(4):
                        g = 4 * i + s
                        p, nxt = s % 2, (s + 1) % 4
                        if nxt % 2 == 0:
                            pe.wait_ge(s_x[nxt // 2], 16 * (i + 1 + (nxt == 0)))
                        wait(pe, s_xt, 2 * g)
                        for k in range(3):
                            last = nc.tensor.transpose(bank[1 - p][:, k * PT_:(k + 1) * PT_],
                                                       X[:, nxt // 2, 3 * (nxt % 2) + k], ident[:PT_, :PT_])
                        last.then_inc(s_xp, 1)
                        layer2(g, p, (0, 1))
                        layer1(g + 1, 1 - p)
                        layer2(g, p, (2, 3))
                        layer3(g, p)

                two_batches(0)
                with pe.Fori(1, B // 2) as i:
                    two_batches(i)
                pe.wait_ge(s_g1, 4 * (2 * B + 1))
                pe.wait_ge(s_w2, 16 * OTHER_W)
                pe.wait_ge(s_prep, 13)
                for n, (src, _) in enumerate(jobs):
                    wait(pe, s_wc, n - 3)
                    nc.tensor.transpose(bank[n % 4][:, 0:128], src, ident[:]).then_inc(s_wt, 1)
                pe.wait_ge(s_zsum, 8)
                for n in range(2):
                    for k in range(TT_):
                        col = (n * TT_ + k) * B
                        last = nc.tensor.transpose(bank[4][:PT_, col:col + B],
                                                   cs[:, 1 - n + k * PT_:1 - n + (k + 1) * PT_], ident[:B, :B])
                last.then_inc(s_cp, 1)

            @block.scalar
            def _(act):
                def gelu1(g, p):
                    for m in range(DC):
                        act.wait_ge(s_h1, 4 * g + m + 1)
                        if m == 0:
                            wait(act, s_hs, 4 * g)
                        nc.scalar.activation(h1[:, m], bank[2 + m % 2][:, :NE], ACT.Gelu,
                                             bias=b1c[:, m:m + 1]).then_inc(s_g1, 1)

                def gelu2(g, p, ms):
                    for m in ms:
                        act.wait_ge(s_h2, 4 * g + m + 1)
                        if m == 0:
                            wait(act, s_z, g - 1)
                        nc.scalar.activation(h2[:, p, m], bank[4 + m % 2][:, :N], ACT.Gelu,
                                             bias=b2c[:, m:m + 1]).then_inc(s_g2, 1)

                act.wait_ge(s_wf, 32)
                gelu1(0, 0)
                act.wait_ge(s_w, 16 * TOK_W)

                def two_batches(i):
                    for s in range(4):
                        g, p = 4 * i + s, s % 2
                        gelu2(g, p, (0, 1))
                        gelu1(g + 1, 1 - p)
                        gelu2(g, p, (2, 3))

                two_batches(0)
                with act.Fori(1, B // 2) as i:
                    two_batches(i)
                act.wait_ge(s_zsum, 3)
                nc.scalar.activation(imp[:], zrow[:, 0], ACT.Sigmoid, bias=b3c[:, 0:1]).then_inc(s_sig, 1)

            @block.vector
            def _(dve):
                def split_x(g, p):
                    dve.wait_ge(s_xp, g + 1)
                    wait(dve, s_h1, 4 * g - 4)
                    nc.vector.tensor_copy(xThl[:, p, 0, :N], bank[p][:, :N]).then_inc(s_xt, 1)
                    dve.wait_ge(s_xt, 2 * g + 1)
                    nc.vector.tensor_tensor(xThl[:, p, 1, :N], bank[p][:, :N], xThl[:, p, 0, :N],
                                            ALU.subtract).then_inc(s_xt, 1)

                def split_h(g, p):
                    wait(dve, s_h2, 4 * g - 4)
                    for c in (0, 2):
                        dve.wait_ge(s_g1, 4 * g + c + 2)
                        nc.vector.tensor_copy(h1hl[:, p, 0, c:c + 2], h1[:, c:c + 2]).then_inc(s_hs, 1)
                        dve.wait_ge(s_hs, 4 * g + c + 1)
                        nc.vector.tensor_tensor(h1hl[:, p, 1, c:c + 2], h1[:, c:c + 2], h1hl[:, p, 0, c:c + 2],
                                                ALU.subtract).then_inc(s_hs, 1)

                nc.vector.memset(zsb[:, 0, 0:4], 0.0).then_inc(s_xpad, 1)
                dve.wait_ge(s_xpad, 1)
                nc.vector.tensor_copy(xThl[:, :, :, N], zsb[:, 0, 0:4].rearrange("p (a b) -> p a b", a=2)
                                      ).then_inc(s_xpad, 1)
                dve.wait_ge(s_wf, 32)
                nc.vector.tensor_copy(W1hl[:, 0], W1).then_inc(s_xpad, 1)
                dve.wait_ge(s_xpad, 3)
                nc.vector.tensor_tensor(W1hl[:, 1], W1, W1hl[:, 0], ALU.subtract).then_inc(s_ws, 1)
                split_x(0, 0)
                dve.wait_ge(s_w, 16 * TOK_W)
                nc.vector.tensor_copy(w3rep[:], w3c[:, :, None].broadcast_to([128, DC, 32])).then_inc(s_w3, 1)
                nc.vector.tensor_copy(W2hl[:, 0], W2).then_inc(s_xpad, 1)
                dve.wait_ge(s_xpad, 4)
                nc.vector.tensor_tensor(W2hl[:, 1], W2, W2hl[:, 0], ALU.subtract).then_inc(s_ws, 1)
                split_h(0, 0)
                with dve.Fori(0, B // 2) as i:
                    for s in range(4):
                        g, p = 4 * i + s, s % 2
                        split_x(g + 1, 1 - p)
                        split_h(g + 1, 1 - p)
                        dve.wait_ge(s_z, g + 1)
                        if s < 2:
                            dve.wait_ge(s_zs[p], 16 * (2 * i))
                        else:
                            dve.wait_ge(s_zs[p], 16 * (2 * i + 1))
                        nc.vector.tensor_copy(zsb[:, p], bank[6 + p][:, :N]).then_inc(s_zc, 1)
                for n, (_, dst) in enumerate(jobs):
                    dve.wait_ge(s_wt, n + 1)
                    if n < len(split_jobs):
                        nc.vector.tensor_copy(dst[:, 0], bank[n % 4][:, 0:128]).then_inc(s_high, 1)
                        dve.wait_ge(s_high, n + 1)
                        nc.vector.tensor_tensor(dst[:, 1], bank[n % 4][:, 0:128], dst[:, 0],
                                                ALU.subtract).then_inc(s_wc, 1)
                    else:
                        nc.vector.tensor_copy(dst, bank[n % 4][:, 0:128]).then_inc(s_wc, 1)
                dve.wait_ge(s_zl, 16)
                for c in range(1, DC):
                    nc.vector.tensor_tensor(zrow[:, 0], zrow[:, 0], zrow[:, c], ALU.add).then_inc(s_zsum, 1)
                    dve.wait_ge(s_zsum, c)
                dve.wait_ge(s_sig, 1)
                nc.vector.tensor_scalar(imp[:], imp[:], TEMP, None, ALU.add).then_inc(s_zsum, 1)
                dve.wait_ge(s_zsum, 4)
                nc.vector.reduce_sum(isum[:, 0:1], imp[:], AX_X).then_inc(s_zsum, 1)
                dve.wait_ge(s_zsum, 5)
                nc.vector.reciprocal(isum[:, 1:2], isum[:, 0:1]).then_inc(s_zsum, 1)
                dve.wait_ge(s_zsum, 6)
                nc.vector.tensor_scalar(imp[:], imp[:], isum[:, 1:2], float(N), ALU.mult, ALU.mult).then_inc(s_zsum, 1)
                dve.wait_ge(s_zsum, 7)
                dve.wait_ge(s_pool, 8)
                nc.vector.tensor_tensor_scan(cs[:, 1:T + 1], ones_t[:], imp[:], 0.0, ALU.mult,
                                             ALU.add).then_inc(s_zsum, 1)
                dve.wait_ge(s_cp, 1)
                nc.vector.tensor_copy(csT[:].rearrange("p k b -> p (k b)"), bank[4][:PT_, :2 * TT_ * B])

        with ExitStack() as two:
            def sb_(name, shape, dt=F32):
                return two.enter_context(nc.sbuf_tensor(name, shape, dt))

            def sem(name):
                return two.enter_context(nc.semaphore(name))

            FIRST, LAST = -3, B + 1
            LOOP0, LOOP1 = 3, 13
            XPAD = N + 2
            XE = XPAD + 1
            SEG = (0, N, N + PT_)
            ORDER = (2, 0, 1)
            LN = 9

            X2 = sb_("X2", [PT_, 2, TT_, C])
            csb = sb_("csb", [PT_, 2 * TT_])
            cellmax = sb_("cellmax", [PT_, N])
            overlap = sb_("overlap", [PT_, 2, N])
            Wt = sb_("Wt", [PT_, TT_, N])
            lnstat = sb_("lnstat", [PT_, NT, 6])
            lnmv = sb_("lnmv", [PT_, NT, 2])
            lnve = sb_("lnve", [PT_, NT])
            lnr = sb_("lnr", [PT_, NT])
            gstat = sb_("gstat", [PT_, NT, 6])
            gmv = sb_("gmv", [PT_, NT, 2])
            gve = sb_("gve", [PT_, NT])
            gr = sb_("gr", [PT_, NT])
            n1 = sb_("n1", [PT_, NT, C])
            n2 = sb_("n2", [PT_, NT, C])
            xnT = sb_("xnT", [128, N])
            xnThl = sb_("xnThl", [128, 2, 2, XE], F32R)
            xzero = sb_("xzero", [128, 2, 2, 2])
            tap0 = sb_("tap0", [128, 2, N])
            tap1 = sb_("tap1", [128, 2, N])
            QK = sb_("QK", [128, 2, DC, N])
            V = sb_("V", [PT_, 2, NT, D])
            P = sb_("P", [PT_, 4, 2 * N])
            nmax = sb_("nmax", [PT_, 4, NT])
            psum_ = sb_("psum_", [PT_, 4, NT])
            prec = sb_("prec", [PT_, 4, NT])
            PT = sb_("PT", [PT_, 4, 2 * N])
            OT = sb_("OT", [128, DC, N])
            row = sb_("row", [PT_, NT, ROW])
            tT = sb_("tT", [128, N])
            lg = sb_("lg", [PT_, NT, E])
            lmax = sb_("lmax", [PT_, NT])
            lsum = sb_("lsum", [PT_, NT])
            lrec = sb_("lrec", [PT_, NT])
            pTs = sb_("pTs", [E, N])

            bS, bT, bO = (bank[0], bank[1]), (bank[2], bank[3]), bank[4]
            G0, G1, G2 = bank[5], bank[6], bank[7]

            s_x2 = [sem(f"s_x2_loaded{u}") for u in range(2)]
            s_csb = sem("s_cs_of_batch")
            s_cm = sem("s_cellmax_ready")
            s_ov = sem("s_overlap_ready")
            s_wt = sem("s_pool_weights_ready")
            s_ein = sem("s_pooled_in_psum")
            s_lnd = sem("s_ln_dve_steps")
            s_lnp = sem("s_ln_rsqrt_steps")
            s_xtp = sem("s_xnT_in_psum")
            s_xt = sem("s_xnT_ready")
            s_xh = sem("s_xnT_steps")
            s_pad = sem("s_xnT_padded")
            s_qkp = sem("s_qk_in_psum")
            s_t0 = sem("s_tap0_ready")
            s_t1 = sem("s_tap1_ready")
            s_qk = sem("s_qk_ready")
            s_vp = sem("s_v_in_psum")
            s_v = sem("s_v_ready")
            s_sp = sem("s_scores_in_psum")
            s_s = sem("s_scores_ready")
            s_ex = sem("s_exp_ready")
            s_rc = sem("s_recip_ready")
            s_pn = sem("s_probs_normalised")
            s_tp = sem("s_probs_transposed_in_psum")
            s_pt0 = sem("s_probsT0_ready")
            s_pt1 = sem("s_probsT1_ready")
            s_pv = sem("s_pv_in_psum")
            s_o = sem("s_attended_ready")
            s_wo = sem("s_projected_in_psum")
            s_g = sem("s_residual_and_gate_steps")
            s_gp = sem("s_gate_ln_rsqrt_steps")
            s_ttp = sem("s_tT_in_psum")
            s_tt = sem("s_tT_ready")
            s_lp = sem("s_logits_in_psum")
            s_lm = sem("s_logits_shifted")
            s_le = sem("s_logits_exp")
            s_lf = sem("s_probabilities_steps")
            s_pp = sem("s_probsT_in_psum")
            s_pc = sem("s_probsT_copied")
            s_tab = sem("s_table_stored")
            s_tts = sem("s_tT_stored")
            s_ps = sem("s_probsT_stored")
            s_pl = sem("s_probsT_loaded")

            s_on = [sem(f"s_waits_passed{n}") for n in range(2)]

            block = two.enter_context(nc.Block())

            def parity(b, k):
                return (b + k) % 2

            def bodies(eng, body):
                for b in range(FIRST, LOOP0):
                    body(b, b % 2)
                with eng.Fori(LOOP0, LOOP1 - 1, 2) as i:
                    body(i, LOOP0 % 2)
                    body(i + 1, (LOOP0 + 1) % 2)
                for b in range(LOOP1, LAST + 1):
                    body(b, b % 2)

            @block.sync
            def _(sp):
                def body(b, u):
                    if valid(b + 3):
                        wait(sp, s_ein, b + 2)
                        sp.dma_start(X2[:, (u + 1) % 2], x[b + 3].rearrange("(k p) c -> p k c", p=PT_)
                                     ).then_inc(s_x2[(u + 1) % 2], 16)
                    m = b - 2
                    if valid(m):
                        sp.wait_ge(s_lf, 3 * m + 3)
                        sp.dma_start(table_b[m].rearrange("(t p) c -> p t c", p=PT_), row[:]
                                     ).then_inc(s_tab, 16)
                        sp.wait_ge(s_pc, m + 1)
                        sp.dma_start(probs_dram[m], pTs[:]).then_inc(s_ps, 16)
                    m = b - 1
                    if valid(m):
                        sp.wait_ge(s_tt, m + 1)
                        sp.dma_start(tTall[:, bass.ds(m * N, N)], tT[:]).then_inc(s_tts, 16)

                bodies(sp, body)
                sp.wait_ge(s_tab, 16 * B)
                sp.wait_ge(s_ps, 16 * B)
                for pair in range(B // 2):
                    sp.dma_start(probsT[pair * E:(pair + 1) * E].rearrange("e (u n) -> e u n", u=2),
                                 probs_dram[2 * pair:2 * pair + 2].rearrange("u e n -> e u n")
                                 ).then_inc(s_pl, 16)
                sp.wait_ge(s_pl, 16 * (B // 2))
                sp.wait_ge(s_tts, 16 * B)

            @block.tensor
            def _(pe):
                def scores(b, h):
                    c, r = h // 2, DH * (h % 2)
                    pe.wait_ge(s_qk, 8 * b + 2 * c + 2)
                    for unit, tiles in enumerate(((2,), (0, 1))):
                        wait(pe, s_s, 3 * (8 * b + h) - 2 + 2 * unit)
                        for i in tiles:
                            w, at = (i + 1) * PT_, 0 if i != 1 else PT_
                            last = nc.tensor.matmul(bS[unit][:PT_, at:at + w],
                                                    QK[r:r + DH, 0, c, i * PT_:(i + 1) * PT_],
                                                    QK[r:r + DH, 1, c, :w], start=True, stop=True)
                        last.then_inc(s_sp, 1)

                def transpose_probs(b, h):
                    n = 8 * b + h
                    pe.wait_ge(s_pn, 3 * n + 3)
                    wait(pe, s_pt0, n)
                    for i in range(NT):
                        last = nc.tensor.transpose(bT[0][:PT_, i * PT_:(i + 1) * PT_],
                                                   P[:, h % 4, SEG[ORDER.index(i)]:SEG[ORDER.index(i)] + PT_],
                                                   ident[:PT_, :PT_])
                    last.then_inc(s_tp, 1)
                    wait(pe, s_pt1, n)
                    for at, (i, j) in enumerate(((1, 1), (2, 1), (2, 2))):
                        f = SEG[ORDER.index(i)] + j * PT_
                        last = nc.tensor.transpose(bT[1][:PT_, at * PT_:(at + 1) * PT_], P[:, h % 4, f:f + PT_],
                                                   ident[:PT_, :PT_])
                    last.then_inc(s_tp, 1)

                def attend(b, c, u):
                    pe.wait_ge(s_pt0, 8 * b + 2 * c + 2)
                    pe.wait_ge(s_pt1, 8 * b + 2 * c + 2)
                    pe.wait_ge(s_v, 3 * b + 3)
                    wait(pe, s_o, 4 * b + c)
                    for j, at in enumerate((0, N, 2 * N - PT_)):
                        for h in (2 * c, 2 * c + 1):
                            r, w = DH * (h % 2), N - j * PT_
                            last = nc.tensor.matmul(bO[r:r + DH, j * PT_:N], V[:, u, j, h * DH:(h + 1) * DH],
                                                    PT[:, h % 4, at:at + w], start=(j == 0), stop=(j == NT - 1))
                    last.then_inc(s_pv, 1)

                def project_qk(m, c, u):
                    pe.wait_ge(s_xt, m + 1)
                    for n, g in enumerate((G0, G1)):
                        if n == 0 and c > 0:
                            wait(pe, s_v, 3 * m + c)
                        elif n == 0:
                            wait(pe, s_qk, 8 * m - 1)
                        else:
                            wait(pe, s_qk, 8 * m + 2 * c)
                            if c == 0:
                                wait(pe, s_pc, m - 2)
                            if c == 3:
                                wait(pe, s_lm, 2 * (m - 1))
                        for n_, (a, x_) in enumerate(PASSES):
                            last = nc.tensor.matmul(g[:, :XE], WQKT[:, a, n, c * 128:(c + 1) * 128], xnThl[:, u, x_],
                                                    start=(n_ == 0), stop=(n_ == 2))
                        last.then_inc(s_qkp, 1)

                def project_v(m, t, u):
                    pe.wait_ge(s_qk, 8 * m + 2 * t + 1)
                    for a in range(3):
                        for n_, (x_, w_) in enumerate(PASSES):
                            last = nc.tensor.matmul(G0[:PT_, :], xnThl[:, u, x_, t * PT_ + a:(t + 1) * PT_ + a],
                                                    WVT[:, w_, a], start=(a == 0 and n_ == 0),
                                                    stop=(a == 2 and n_ == 2))
                    last.then_inc(s_vp, 1)

                def pool_tokens(m, u):
                    pe.wait_ge(s_wt, 6 * m + 6)
                    pe.wait_ge(s_x2[u], (m - u) * 8 + 16)
                    wait(pe, s_xt, m)
                    wait(pe, s_tt, m - 3)
                    for t in range(NT):
                        for k in range(TT_):
                            last = nc.tensor.matmul(G2[:PT_, t * C:(t + 1) * C], Wt[:, k, t * PT_:(t + 1) * PT_],
                                                    X2[:, u, k], start=(k == 0), stop=(k == TT_ - 1))
                    last.then_inc(s_ein, 1)

                def transpose_tokens(src, done):
                    for t in range(NT):
                        last = nc.tensor.transpose(G2[:, t * PT_:(t + 1) * PT_], src[:, t, 0:C], ident[:PT_, :PT_])
                    last.then_inc(done, 1)

                def body(b, u):
                    v_ = 1 - u
                    for h in range(HEADS):
                        if valid(b):
                            scores(b, h)
                        if h < 2 and valid(b - 1):
                            transpose_probs(b - 1, HEADS - 2 + h)
                        if h >= 2 and valid(b):
                            transpose_probs(b, h - 2)
                        if h == 0 and valid(b):
                            project_qk(b, 3, u)
                        if h in (2, 4, 6) and valid(b + 1):
                            project_qk(b + 1, h // 2 - 1, v_)
                        if h == 1 and valid(b + 2):
                            pool_tokens(b + 2, u)
                        if h == 1 and valid(b - 2):
                            m = b - 2
                            pe.wait_ge(s_qk, cap(8 * b + 8, 8 * B))
                            pe.wait_ge(s_lf, 3 * m + 3)
                            for t in range(NT):
                                last = nc.tensor.transpose(G1[:E, t * PT_:(t + 1) * PT_], row[:, t, C:ROW],
                                                           ident[:PT_, :PT_])
                            last.then_inc(s_pp, 1)
                        if h in (0, 2) and valid(b - 1):
                            attend(b - 1, 2 + h // 2, v_)
                        if h in (4, 6) and valid(b):
                            attend(b, h // 2 - 2, u)
                        if h == 3 and valid(b - 1):
                            m = b - 1
                            pe.wait_ge(s_o, 4 * m + 4)
                            pe.wait_ge(s_lnd, cap((2 * LN + 1) * (b + 2) + 1, (2 * LN + 1) * B))
                            for t in range(NT):
                                for c in range(DC):
                                    last = nc.tensor.matmul(G2[:PT_, t * C:(t + 1) * C],
                                                            OT[:, c, t * PT_:(t + 1) * PT_], WOT[:, c],
                                                            start=(c == 0), stop=(c == DC - 1))
                            last.then_inc(s_wo, 1)
                        if h in (3, 5, 7) and valid(b + 1):
                            project_v(b + 1, (h - 3) // 2, v_)
                        if h == 4 and valid(b + 2):
                            m = b + 2
                            pe.wait_ge(s_lnd, (2 * LN + 1) * (m + 1))
                            wait(pe, s_g, (LN + 1) * (m - 3) + 1)
                            transpose_tokens(n2, s_xtp)
                        if h == 6 and valid(b - 1):
                            m = b - 1
                            pe.wait_ge(s_g, (LN + 1) * (m + 1))
                            pe.wait_ge(s_xh, cap(2 * (b + 3), 2 * B))
                            transpose_tokens(row, s_ttp)
                        if h == 7 and valid(b - 1):
                            m = b - 1
                            pe.wait_ge(s_tt, m + 1)
                            pe.wait_ge(s_qk, cap(8 * (b + 1) + 6, 8 * B))
                            wait(pe, s_pc, cap(m, B))
                            for t in range(NT):
                                last = nc.tensor.matmul(G1[:PT_, t * E:(t + 1) * E], tT[:, t * PT_:(t + 1) * PT_],
                                                        gate[:], start=True, stop=True)
                            last.then_inc(s_lp, 1)

                pe.wait_ge(s_pad, 3)
                bodies(pe, body)

            @block.scalar
            def _(act):
                def body(b, u):
                    for h in range(HEADS):
                        if valid(b):
                            n = 8 * b + h
                            for q, i in enumerate(ORDER):
                                w = (i + 1) * PT_
                                act.wait_ge(s_s, 3 * n + q + 1)
                                nc.scalar.activation(P[:, h % 4, SEG[q]:SEG[q] + w], P[:, h % 4, SEG[q]:SEG[q] + w],
                                                     ACT.Exp, bias=nmax[:, h % 4, q:q + 1], scale=-1.0,
                                                     accum_out=psum_[:, h % 4, q:q + 1]).then_inc(s_ex, 1)
                        m, c = (b, 3) if h == 0 else (b + 1, h // 2 - 1)
                        if h % 2 == 0 and valid(m):
                            for q in range(2):
                                n = 8 * m + 2 * c + q
                                act.wait_ge(s_qkp, n + 1)
                                wait(act, s_t1, n - 1)
                                nc.scalar.activation(tap0[:, q], (G0, G1)[q][:, 0:N], ACT.Copy,
                                                     scale=qkd[:, q, c, 0:1]).then_inc(s_t0, 1)
                        m = b if h >= 2 else b - 1
                        if valid(m):
                            n, hh = 8 * m + (h - 2) % 8, (h - 2) % 4
                            wait(act, s_pv, 4 * m + ((h - 2) % 8) // 2 - 1)
                            if h % 2:
                                act.wait_ge(s_tp, 2 * n + 1)
                                nc.scalar.copy(PT[:, hh, 0:N], bT[0][:PT_, :N]).then_inc(s_pt0, 1)
                            act.wait_ge(s_tp, 2 * n + 2)
                            nc.scalar.copy(PT[:, hh, N:2 * N], bT[1][:PT_, :N]).then_inc(s_pt1, 1)
                        m, c = (b, h // 2 - 2) if h >= 4 else (b - 1, h // 2 + 2)
                        if h % 2 == 0 and valid(m):
                            act.wait_ge(s_pv, 4 * m + c + 1)
                            wait(act, s_wo, m)
                            nc.scalar.copy(OT[:, c], bO[:, :N]).then_inc(s_o, 1)
                        if h in (3, 5, 7) and valid(b + 1):
                            m, t = b + 1, (h - 3) // 2
                            act.wait_ge(s_vp, 3 * m + t + 1)
                            wait(act, s_pv, 4 * (m - 1))
                            nc.scalar.copy(V[:, 1 - u, t], G0[:PT_, :]).then_inc(s_v, 1)
                        if h == 4 and valid(b + 2):
                            m = b + 2
                            act.wait_ge(s_xtp, m + 1)
                            wait(act, s_xt, m)
                            nc.scalar.activation(xnT[:], G2[:, :N], ACT.Identity, bias=betac[:, 0:1],
                                                 scale=gammac[:, 0:1]).then_inc(s_xh, 1)
                            nc.scalar.activation(xnThl[:, u, 0, 2:XPAD], G2[:, :N], ACT.Identity,
                                                 bias=betac[:, 0:1], scale=gammac[:, 0:1]).then_inc(s_xh, 1)
                        if h == 6 and valid(b - 1):
                            m = b - 1
                            act.wait_ge(s_ttp, m + 1)
                            wait(act, s_tts, 16 * m)
                            wait(act, s_lp, m)
                            nc.scalar.copy(tT[:], G2[:, :N]).then_inc(s_tt, 1)
                        if h == 7 and valid(b - 1):
                            m = b - 1
                            act.wait_ge(s_lm, 2 * m + 2)
                            nc.scalar.activation(lg[:], lg[:], ACT.Exp).then_inc(s_le, 1)
                        m, k = (b + 3, h - 3) if h else (b + 2, TT_ - 1)
                        if h not in (1, 2) and valid(m):
                            act.wait_ge(s_ov, 6 * m + k + 1)
                            wait(act, s_ein, m)
                            nc.scalar.activation(Wt[:, k], overlap[:, k % 2], ACT.Relu).then_inc(s_wt, 1)

                bodies(act, body)

            @block.gpsimd
            def _(pool):
                nc.gpsimd.memset(xzero[:], 0.0).then_inc(s_pad, 1)
                pool.wait_ge(s_pad, 1)
                nc.gpsimd.tensor_copy(xnThl[:, :, :, 0:2], xzero[:]).then_inc(s_pad, 1)
                nc.gpsimd.tensor_copy(xnThl[:, :, :, XPAD], xzero[:, :, :, 0]).then_inc(s_pad, 1)

                def rsqrt(ve, r, mv, sem_, n, dve_sem, dve_n):
                    wait_apart(pool, dve_sem, dve_n, s_on[1])
                    nc.gpsimd.tensor_scalar(ve[:], mv[:, :, 1], EPS, None, ALU.add).then_inc(sem_, 1)
                    pool.wait_ge(sem_, n + 1)
                    nc.gpsimd.tensor_tensor(r[:], ve[:], mhalf[:], ALU.pow).then_inc(sem_, 1)

                def body(b, u):
                    for h in range(HEADS):
                        if valid(b + 2):
                            m, base = b + 2, (2 * LN + 1) * (b + 2)
                            if h == 1:
                                rsqrt(lnve, lnr, lnmv, s_lnp, 4 * m, s_lnd, base + 7)
                            if h == 2:
                                rsqrt(lnve, lnr, lnmv, s_lnp, 4 * m + 2, s_lnd, base + LN + 7)
                        if h == 4 and valid(b - 1):
                            m = b - 1
                            rsqrt(gve, gr, gmv, s_gp, 2 * m, s_g, (LN + 1) * m + 7)

                bodies(pool, body)

            @block.vector
            def _(dve):
                def ln_stats(src, stat, mv, s, n):
                    for t in range(NT):
                        nc.vector.bn_stats(stat[:, t], src(t)).then_inc(s, 1)
                    for t in range(NT):
                        wait_apart(dve, s, n + t + 1, s_on[0])
                        nc.vector.bn_aggr(mv[:, t], stat[:, t]).then_inc(s, 1)

                def ln_apply(dst, src, mv, r, s):
                    for t in range(NT):
                        nc.vector.tensor_scalar(dst[:, t, 0:C], src(t), mv[:, t, 0:1], r[:, t:t + 1],
                                                ALU.subtract, ALU.mult).then_inc(s, 1)

                def body(b, u):
                    for h in range(HEADS):
                        m = b if h else b - 1
                        if valid(m):
                            n, hh = 8 * m + (h - 1) % 8, (h - 1) % 4
                            dve.wait_ge(s_ex, 3 * n + 3)
                            nc.vector.reciprocal(prec[:, hh], psum_[:, hh]).then_inc(s_rc, 1)
                            dve.wait_ge(s_rc, n + 1)
                            for q, i in enumerate(ORDER):
                                w = (i + 1) * PT_
                                nc.vector.tensor_scalar(P[:, hh, SEG[q]:SEG[q] + w], P[:, hh, SEG[q]:SEG[q] + w],
                                                        prec[:, hh, q:q + 1], None, ALU.mult).then_inc(s_pn, 1)
                        if valid(b):
                            n = 8 * b + h
                            wait(dve, s_tp, 2 * (n - 3))
                            for q, i in enumerate(ORDER):
                                w, at = (i + 1) * PT_, 0 if i != 1 else PT_
                                if q < 2:
                                    wait_apart(dve, s_sp, 2 * n + q + 1, s_on[0])
                                nc.vector.tensor_tensor_reduce(
                                    out=P[:, h % 4, SEG[q]:SEG[q] + w], in0=bS[min(q, 1)][:PT_, at:at + w],
                                    in1=nbias[:, h, (2 - i) * PT_:N], scale=1.0, scalar=MASKED, op0=ALU.add,
                                    op1=ALU.min, accum_out=nmax[:, h % 4, q:q + 1]).then_inc(s_s, 1)
                        m = b if h >= 2 else b - 1
                        if valid(m) and h % 2 == 0:
                            n, hh = 8 * m + (h - 2) % 8, (h - 2) % 4
                            dve.wait_ge(s_tp, 2 * n + 1)
                            wait(dve, s_pv, 4 * m + ((h - 2) % 8) // 2 - 1)
                            nc.vector.tensor_copy(PT[:, hh, 0:N], bT[0][:PT_, :N]).then_inc(s_pt0, 1)
                        if h == 0 and valid(b - 2):
                            m = b - 2
                            dve.wait_ge(s_le, m + 1)
                            nc.vector.reduce_sum(lsum[:], lg[:], AX_X).then_inc(s_lf, 1)
                            dve.wait_ge(s_lf, 3 * m + 1)
                            nc.vector.reciprocal(lrec[:], lsum[:]).then_inc(s_lf, 1)
                            dve.wait_ge(s_lf, 3 * m + 2)
                            nc.vector.tensor_tensor(row[:, :, C:ROW], lg[:],
                                                    lrec[:, :, None].broadcast_to([PT_, NT, E]),
                                                    ALU.mult).then_inc(s_lf, 1)
                        if h >= 2 and valid(b + 3):
                            m, k = b + 3, h - 2
                            dve.wait_ge(s_csb, m + 1)
                            wait(dve, s_ov, 6 * m + k)
                            nc.vector.tensor_scalar(cellmax[:], grid0[:], csb[:, TT_ + k:TT_ + k + 1], None,
                                                    ALU.max).then_inc(s_cm, 1)
                            dve.wait_ge(s_cm, 6 * m + k + 1)
                            wait(dve, s_wt, 6 * m + k - 1)
                            nc.vector.scalar_tensor_tensor(out=overlap[:, k % 2], in0=grid1[:], scalar=csb[:, k:k + 1],
                                                           in1=cellmax[:], op0=ALU.min,
                                                           op1=ALU.subtract).then_inc(s_ov, 1)
                        m, c = (b, 3) if h == 0 else (b + 1, h // 2 - 1)
                        if h % 2 == 0 and valid(m):
                            for q in range(2):
                                n = 8 * m + 2 * c + q
                                ps = (G0, G1)[q]
                                dve.wait_ge(s_t0, n + 1)
                                nc.vector.scalar_tensor_tensor(out=tap1[:, q], in0=ps[:, 1:N + 1],
                                                               scalar=qkd[:, q, c, 1:2], in1=tap0[:, q],
                                                               op0=ALU.mult, op1=ALU.add).then_inc(s_t1, 1)
                                dve.wait_ge(s_t1, n + 1)
                                wait(dve, s_sp, 16 * (m - 1) + 4 * c + 4)
                                nc.vector.scalar_tensor_tensor(out=QK[:, q, c], in0=ps[:, 2:N + 2],
                                                               scalar=qkd[:, q, c, 2:3], in1=tap1[:, q],
                                                               op0=ALU.mult, op1=ALU.add).then_inc(s_qk, 1)
                        if h == 1 and valid(b + 2):
                            m, base = b + 2, (2 * LN + 1) * (b + 2)
                            dve.wait_ge(s_ein, m + 1)
                            nc.vector.tensor_copy(Hall[:, m], G2[:PT_, :NT * C].rearrange("p (t c) -> p t c", c=C)
                                                  ).then_inc(s_lnd, 1)
                            wait_apart(dve, s_lnd, base + 1, s_on[0])
                            ln_stats(lambda t: Hall[:, m, t], lnstat, lnmv, s_lnd, base + 1)
                        if h == 2 and valid(b + 2):
                            m, base = b + 2, (2 * LN + 1) * (b + 2)
                            dve.wait_ge(s_lnp, 4 * m + 2)
                            ln_apply(n1, lambda t: Hall[:, m, t], lnmv, lnr, s_lnd)
                            dve.wait_ge(s_lnd, base + LN + 1)
                            ln_stats(lambda t: n1[:, t], lnstat, lnmv, s_lnd, base + LN + 1)
                        if h == 3 and valid(b + 2):
                            m, base = b + 2, (2 * LN + 1) * (b + 2)
                            dve.wait_ge(s_lnp, 4 * m + 4)
                            wait(dve, s_xtp, m)
                            ln_apply(n2, lambda t: n1[:, t], lnmv, lnr, s_lnd)
                        if h == 5 and valid(b + 2):
                            m = b + 2
                            dve.wait_ge(s_xh, 2 * m + 2)
                            nc.vector.tensor_tensor(xnThl[:, u, 1, 2:XPAD], xnT[:], xnThl[:, u, 0, 2:XPAD],
                                                    ALU.subtract).then_inc(s_xt, 1)
                        if h == 1 and valid(b - 2):
                            m = b - 2
                            dve.wait_ge(s_pp, m + 1)
                            wait(dve, s_ps, 16 * m)
                            nc.vector.tensor_copy(pTs[:], G1[:E, :N]).then_inc(s_pc, 1)
                        if h == 1 and valid(b + 3):
                            m = b + 3
                            wait(dve, s_wt, 6 * m)
                            nc.vector.tensor_copy(csb[:], csT[:, :, m]).then_inc(s_csb, 1)
                        if h == 3 and valid(b - 1):
                            m, base = b - 1, (LN + 1) * (b - 1)
                            dve.wait_ge(s_wo, m + 1)
                            nc.vector.tensor_tensor(Hall[:, m], Hall[:, m],
                                                    G2[:PT_, :NT * C].rearrange("p (t c) -> p t c", c=C),
                                                    ALU.add).then_inc(s_g, 1)
                            wait_apart(dve, s_g, base + 1, s_on[0])
                            ln_stats(lambda t: Hall[:, m, t], gstat, gmv, s_g, base + 1)
                        if h == 5 and valid(b - 1):
                            m = b - 1
                            dve.wait_ge(s_gp, 2 * m + 2)
                            wait(dve, s_tab, 16 * m)
                            wait(dve, s_ttp, m)
                            wait(dve, s_pp, m)
                            ln_apply(row, lambda t: Hall[:, m, t], gmv, gr, s_g)
                        if h == 7 and valid(b - 1):
                            m = b - 1
                            dve.wait_ge(s_lp, m + 1)
                            nc.vector.reduce_max(lmax[:], G1[:PT_, :NT * E].rearrange("p (t e) -> p t e", e=E),
                                                 AX_X).then_inc(s_lm, 1)
                            dve.wait_ge(s_lm, 2 * m + 1)
                            nc.vector.tensor_tensor(lg[:], G1[:PT_, :NT * E].rearrange("p (t e) -> p t e", e=E),
                                                    lmax[:, :, None].broadcast_to([PT_, NT, E]),
                                                    ALU.subtract).then_inc(s_lm, 1)

                bodies(dve, body)


        with ExitStack() as three:
            def sb_(name, shape, dt=F32):
                return three.enter_context(nc.sbuf_tensor(name, shape, dt))

            def sem(name):
                return three.enter_context(nc.semaphore(name))

            TOPBIT = 29
            hS = sb_("hS", [128, 2, DC, N])
            oS = sb_("oS", [PT_, 2, NT, C])
            diff = sb_("diff", [128, 128], I32)
            step = sb_("step", [128, 2], I32)
            cand = sb_("cand", [128, 1], I32)
            grow = sb_("grow", [128, 1], I32)
            flags = sb_("flags", [128, 2 * N])

            s_c = sem("s_pool_consts2")
            s_i = sem("s_dve_consts2")
            s_h = sem("s_shared_h_in_psum")
            s_hr = sem("s_shared_h_ready")
            s_y = sem("s_shared_y_in_psum")
            s_yr = sem("s_shared_steps")
            s_out = [sem(f"s_shared_stored{u}") for u in range(2)]
            s_n = sem("s_count_ready")
            s_tot = sem("s_total_in_psum")
            s_thr = sem("s_threshold_steps")

            block = three.enter_context(nc.Block())

            @block.gpsimd
            def _(pool):
                nc.gpsimd.iota(diff[:], pattern=[[-1, 128]], base=128, channel_multiplier=1).then_inc(s_c, 1)
                pool.wait_ge(s_i, 2)
                nc.gpsimd.affine_select(out=before[:], in_=same[:], compare_op=ALU.is_gt, fill=0.0, base=0,
                                        pattern=[[1, 128]], channel_multiplier=-1).then_inc(s_c, 1)

            @block.sync
            def _(sp):
                with sp.Fori(0, B // 2) as i:
                    for u in range(2):
                        sp.wait_ge(s_yr, 2 * (2 * i + u) + 2)
                        sp.dma_start(out[2 * i + u].rearrange("(t p) c -> p t c", p=PT_), oS[:, u]
                                     ).then_inc(s_out[u], 16)
                for u in range(2):
                    sp.wait_ge(s_out[u], 16 * (B // 2))

            @block.tensor
            def _(pe):
                def total(n):
                    pe.wait_ge(s_n, n + 1)
                    nc.tensor.matmul(bank[4][:, 0:1], same[:], cnt[:, 0:1], start=True, stop=True).then_inc(s_tot, 1)

                pe.wait_ge(s_i, 2)
                with pe.Fori(0, B // 2) as i:
                    for u in range(2):
                        b = 2 * i + u
                        for m in range(DC):
                            if m >= 2:
                                pe.wait_ge(s_hr, 4 * b + m - 1)
                            elif u == 1:
                                pe.wait_ge(s_hr, 8 * i + 4)
                            else:
                                pe.wait_ge(s_hr, 8 * i)
                            nc.tensor.matmul(bank[m % 2][:, :N], SW1[:, m * 128:(m + 1) * 128],
                                             tTall[:, bass.ds(b * N, N)], start=True, stop=True).then_inc(s_h, 1)
                        total(2 * b)
                        pe.wait_ge(s_hr, 4 * b + 4)
                        pe.wait_ge(s_yr, 2 * b)
                        for t in range(NT):
                            for k in range(DC):
                                last = nc.tensor.matmul(bank[2 + u][:PT_, t * C:(t + 1) * C],
                                                        hS[:, u, k, t * PT_:(t + 1) * PT_], SW2[:, k],
                                                        start=(k == 0), stop=(k == DC - 1))
                        last.then_inc(s_y, 1)
                        total(2 * b + 1)
            @block.scalar
            def _(act):
                with act.Fori(0, B // 2) as i:
                    for u in range(2):
                        b = 2 * i + u
                        for m in range(DC):
                            act.wait_ge(s_h, 4 * b + m + 1)
                            if m == 0 and u == 0:
                                act.wait_ge(s_y, 2 * i)
                            nc.scalar.activation(hS[:, u, m], bank[m % 2][:, :N], ACT.Gelu_apprx_tanh,
                                                 bias=sb1c[:, m:m + 1]).then_inc(s_hr, 1)

            @block.vector
            def _(dve):
                def count(n):
                    nc.vector.tensor_scalar(flags[:], probsT[:], cand[:, 0:1].bitcast(F32), 0.0, ALU.is_ge, ALU.add,
                                            accum_out=cnt[:, 0:1]).then_inc(s_n, 1)

                def decide(n, k):
                    dve.wait_ge(s_tot, n + 1)
                    nc.vector.scalar_tensor_tensor(out=grow[:], in0=bank[4][:, 0:1], scalar=float(CAP),
                                                   in1=step[:, k:k + 1], op0=ALU.is_ge, op1=ALU.mult).then_inc(s_thr, 1)
                    dve.wait_ge(s_thr, 4 * n + 1)
                    nc.vector.scalar_tensor_tensor(out=cand[:], in0=grow[:], scalar=thr[:, 0:1],
                                                   in1=step[:, 1 - k:2 - k], op0=ALU.bitwise_or,
                                                   op1=ALU.bitwise_or).then_inc(s_thr, 1)
                    dve.wait_ge(s_thr, 4 * n + 2)
                    count(n + 1)
                    nc.vector.tensor_tensor(thr[:], thr[:], grow[:], ALU.bitwise_or).then_inc(s_thr, 1)
                    nc.vector.tensor_scalar(step[:, k:k + 1], step[:, 1 - k:2 - k], 1, None,
                                            ALU.logical_shift_right).then_inc(s_thr, 1)
                    dve.wait_ge(s_thr, 4 * n + 4)

                dve.wait_ge(s_c, 1)
                nc.vector.tensor_scalar(diff[:], diff[:], E - 1, None, ALU.bitwise_and).then_inc(s_i, 1)
                dve.wait_ge(s_i, 1)
                nc.vector.tensor_scalar(same[:], diff[:], 0.0, None, ALU.is_equal).then_inc(s_i, 1)
                nc.vector.memset(thr[:], 0).then_inc(s_i, 1)
                nc.vector.memset(cand[:], 1 << TOPBIT).then_inc(s_i, 1)
                nc.vector.memset(step[:, 0:1], 1 << TOPBIT).then_inc(s_i, 1)
                nc.vector.memset(step[:, 1:2], 1 << (TOPBIT - 1)).then_inc(s_i, 1)
                dve.wait_ge(s_i, 6)
                count(0)
                with dve.Fori(0, B // 2) as i:
                    for u in range(2):
                        b = 2 * i + u
                        decide(2 * b, 0)
                        dve.wait_ge(s_y, b + 1)
                        dve.wait_ge(s_out[u], 16 * i)
                        nc.vector.tensor_tensor(oS[:, u], bank[2 + u][:PT_, :NT * C].rearrange(
                            "p (t c) -> p t c", c=C), Hall[:, b], ALU.add).then_inc(s_yr, 1)
                        dve.wait_ge(s_yr, 2 * b + 1)
                        nc.vector.tensor_tensor(oS[:, u], oS[:, u], sb2b[:, None, :].broadcast_to([PT_, NT, C]),
                                                ALU.add).then_inc(s_yr, 1)
                        decide(2 * b + 1, 1)

        mid.close()

        with ExitStack() as lst:
            def sb_(name, shape, dt=F32):
                return lst.enter_context(nc.sbuf_tensor(name, shape, dt))

            def sem(name):
                return lst.enter_context(nc.semaphore(name))

            TILES = T // PT_
            PAIRS = B // 2
            NSUB = 5
            SLOT = PT_ // NSUB
            NA = CAP // SLOT
            AW = 16
            COLS = TILES * PAIRS * E
            GE = 8
            NG = E // GE
            ROUND = 1.5 * 2.0 ** 23

            over = sb_("over", [128, 2 * N])
            tied = sb_("tied", [128, 2 * N])
            ties = sb_("ties", [128, 2 * N])
            room = sb_("room", [128, 2])
            chosen = sb_("chosen", [128, 2 * N])
            place = sb_("place", [128, 2 * N])
            ones_r = sb_("ones_r", [128, 2 * N])
            quot = sb_("quot", [PT_, COLS])
            fa = sb_("fa", [PT_, COLS], BF16)
            fb = sb_("fb", [PT_, COLS], BF16)
            pidx = sb_("pidx", [PT_, 1])
            hotA = sb_("hotA", [PT_, COLS, AW], BF16)
            hotB = sb_("hotB", [PT_, SLOT, COLS], BF16)
            diagi = sb_("diagi", [128, GE], I32)
            diag = sb_("diag", [128, GE])
            picked = sb_("picked", [128, NG, SLOT, GE])
            lists = sb_("lists", [128, NG, SLOT])
            listT = sb_("listT", [SLOT, E, AW])
            spread = sb_("spread", [SLOT, 2 * PT_ - SLOT])
            slots = sb_("slots", [128, N])
            ends = sb_("ends", [128, TILES])
            passed = sb_("passed", [128, N])
            tile_of = sb_("tile_of", [128, E])

            s_c = sem("s_pool_consts3")
            s_i = sem("s_dve_consts3")
            s_sel = sem("s_selection_steps")
            s_m = sem("s_selection_matmuls")
            s_hot = sem("s_onehot_steps")
            s_end = sem("s_passed_tiles_steps")

            HOT = 5 + NA + SLOT
            HOT_LISTS = HOT + NG + 1

            block = lst.enter_context(nc.Block())

            @block.gpsimd
            def _(pool):
                nc.gpsimd.memset(ones_r[:], 1.0).then_inc(s_c, 1)
                nc.gpsimd.iota(pidx[:], pattern=[[0, 1]], base=0, channel_multiplier=1,
                               allow_small_or_imprecise_dtypes=True).then_inc(s_c, 1)
                nc.gpsimd.memset(hotA[:, :, NA:], 0.0).then_inc(s_c, 1)
                nc.gpsimd.iota(slots[:], pattern=[[1, N]], base=0, channel_multiplier=0,
                               allow_small_or_imprecise_dtypes=True).then_inc(s_c, 1)
                nc.gpsimd.iota(diagi[:], pattern=[[-AW, GE]], base=0, channel_multiplier=1).then_inc(s_c, 1)
                nc.gpsimd.memset(spread[:], 0.0).then_inc(s_c, 1)
                pool.wait_ge(s_c, 6)
                nc.gpsimd.affine_select(out=spread[:], in_=spread[:], compare_op=ALU.not_equal, fill=1.0,
                                        base=PT_ - SLOT, pattern=[[-1, 2 * PT_ - SLOT]],
                                        channel_multiplier=1).then_inc(s_c, 1)

            @block.tensor
            def _(pe):
                pe.wait_ge(s_sel, 2)
                nc.tensor.matmul(bank[5][:, 0:1], same[:], cnt[:, 1:2], start=True, stop=True)
                nc.tensor.matmul(bank[5][:, 1:2], before[:], cnt[:, 2:3], start=True, stop=True).then_inc(s_m, 1)
                pe.wait_ge(s_sel, 8)
                nc.tensor.matmul(bank[6][:, 0:1], before[:], place[:, 2 * N - 1:2 * N], start=True,
                                 stop=True).then_inc(s_m, 1)
                pe.wait_ge(s_sel, 9)
                for j in range(TILES):
                    last = nc.tensor.transpose(bank[j // 3][:PT_, (j % 3) * 128:(j % 3 + 1) * 128],
                                               chosen[:, j * PT_:(j + 1) * PT_], ident[:])
                last.then_inc(s_m, 1)
                pe.wait_ge(s_hot, HOT)
                pe.wait_ge(s_c, 3)

                def collect(j, first, final):
                    for pair in range(PAIRS):
                        for g in range(NG):
                            c0 = j * PAIRS * E + pair * E + g * GE
                            last = nc.tensor.matmul(bank[3 + g][:, 0:SLOT * GE], hotA2[:, bass.ds(c0 * AW, GE * AW)],
                                                    hotB[:, :, bass.ds(c0, GE)], start=first and pair == 0,
                                                    stop=final and pair == PAIRS - 1)
                    return last

                hotA2 = hotA[:].rearrange("p c a -> p (c a)")
                collect(0, True, False)
                with pe.Fori(1, TILES - 1) as j:
                    collect(j, False, False)
                collect(TILES - 1, False, True).then_inc(s_m, 1)
                pe.wait_ge(s_hot, HOT_LISTS)
                for g in range(NG):
                    last = nc.tensor.transpose(bank[5][:SLOT, g * 128:(g + 1) * 128], lists[:, g], ident[:])
                last.then_inc(s_m, 1)
                pe.wait_ge(s_hot, HOT_LISTS + 1)
                pe.wait_ge(s_c, 7)
                pe.wait_ge(s_i, 3)
                pe.wait_ge(s_end, TILES + 1)
                for a in range(NSUB):
                    at = PT_ - SLOT - a * SLOT
                    nc.tensor.matmul(bank[7][:PT_, :NT * E], spread[:, at:at + PT_],
                                     listT[:, :, a:NA:NSUB].rearrange("b e k -> b k e"),
                                     start=(a == 0), stop=False)
                for k in range(NT):
                    last = nc.tensor.matmul(bank[7][:PT_, k * E:(k + 1) * E], passed[:, k * PT_:(k + 1) * PT_],
                                            tile_of[:], start=False, stop=(k == NT - 1))
                last.then_inc(s_m, 1)

            @block.vector
            def _(dve):
                nc.vector.tensor_scalar(over[:], probsT[:], thr[:, 0:1].bitcast(F32), 0.0, ALU.is_gt, ALU.add,
                                        accum_out=cnt[:, 1:2]).then_inc(s_sel, 1)
                nc.vector.tensor_scalar(tied[:], probsT[:], thr[:, 0:1].bitcast(F32), 0.0, ALU.is_equal, ALU.add,
                                        accum_out=cnt[:, 2:3]).then_inc(s_sel, 1)
                dve.wait_ge(s_sel, 2)
                dve.wait_ge(s_c, 1)
                nc.vector.tensor_tensor_scan(ties[:], ones_r[:], tied[:], 0.0, ALU.mult, ALU.add).then_inc(s_sel, 1)
                dve.wait_ge(s_m, 1)
                nc.vector.tensor_scalar(room[:, 0:1], bank[5][:, 0:1], -1.0, float(CAP), ALU.mult,
                                        ALU.add).then_inc(s_sel, 1)
                dve.wait_ge(s_sel, 4)
                nc.vector.tensor_tensor(room[:, 1:2], room[:, 0:1], bank[5][:, 1:2], ALU.subtract).then_inc(s_sel, 1)
                dve.wait_ge(s_sel, 5)
                nc.vector.scalar_tensor_tensor(out=ties[:], in0=ties[:], scalar=room[:, 1:2], in1=tied[:],
                                               op0=ALU.is_le, op1=ALU.mult).then_inc(s_sel, 1)
                dve.wait_ge(s_sel, 6)
                nc.vector.tensor_tensor(chosen[:], over[:], ties[:], ALU.add).then_inc(s_sel, 1)
                dve.wait_ge(s_sel, 7)
                nc.vector.tensor_tensor_scan(place[:], ones_r[:], chosen[:], 0.0, ALU.mult, ALU.add).then_inc(s_sel, 1)
                dve.wait_ge(s_sel, 8)
                dve.wait_ge(s_m, 2)
                nc.vector.scalar_tensor_tensor(out=chosen[:], in0=place[:], scalar=bank[6][:, 0:1], in1=chosen[:],
                                               op0=ALU.add, op1=ALU.mult).then_inc(s_sel, 1)
                nc.vector.tensor_scalar(ends[:], place[:, PT_ - 1::PT_], bank[6][:, 0:1], None,
                                        ALU.add).then_inc(s_end, 1)
                dve.wait_ge(s_m, 3)
                for n in range(2):
                    nc.vector.tensor_scalar(quot[:, n * 384:(n + 1) * 384], bank[n][:PT_, :384], 1.0 / SLOT,
                                            -(1.0 + SLOT // 2) / SLOT, ALU.mult, ALU.add).then_inc(s_hot, 1)
                dve.wait_ge(s_hot, 2)
                nc.vector.tensor_scalar(fa[:], quot[:], ROUND, -ROUND, ALU.add, ALU.add).then_inc(s_hot, 1)
                dve.wait_ge(s_hot, 3)
                for n in range(2):
                    nc.vector.scalar_tensor_tensor(out=fb[:, n * 384:(n + 1) * 384], in0=fa[:, n * 384:(n + 1) * 384],
                                                   scalar=-float(SLOT), in1=bank[n][:PT_, :384], op0=ALU.mult,
                                                   op1=ALU.add).then_inc(s_hot, 1)
                dve.wait_ge(s_c, 2)
                for a in range(NA):
                    nc.vector.tensor_scalar(hotA[:, :, a], fa[:], float(a), pidx[:, 0:1], ALU.is_equal,
                                            ALU.mult).then_inc(s_hot, 1)
                dve.wait_ge(s_hot, 5)
                for b in range(SLOT):
                    nc.vector.tensor_scalar(hotB[:, b], fb[:], float(b + 1), None, ALU.is_equal).then_inc(s_hot, 1)
                dve.wait_ge(s_c, 5)
                nc.vector.tensor_scalar(diagi[:], diagi[:], 4, None, ALU.arith_shift_right).then_inc(s_i, 1)
                nc.vector.tensor_scalar(tile_of[:], same[:, 0:E], float(PT_), None, ALU.mult).then_inc(s_i, 1)
                dve.wait_ge(s_i, 1)
                nc.vector.tensor_scalar(diag[:], diagi[:], 0.0, None, ALU.is_equal).then_inc(s_i, 1)
                for j in range(TILES):
                    dve.wait_ge(s_end, j + 1)
                    if j == 0:
                        nc.vector.tensor_scalar(passed[:], slots[:], ends[:, 0:1], None, ALU.is_ge).then_inc(s_end, 1)
                    else:
                        nc.vector.scalar_tensor_tensor(out=passed[:], in0=slots[:], scalar=ends[:, j:j + 1],
                                                       in1=passed[:], op0=ALU.is_ge, op1=ALU.add).then_inc(s_end, 1)
                dve.wait_ge(s_i, 3)
                dve.wait_ge(s_m, 4)
                for g in range(NG):
                    nc.vector.tensor_tensor(picked[:, g], bank[3 + g][:, :SLOT * GE].rearrange(
                        "p (b e) -> p b e", e=GE), diag[:, None, :].broadcast_to([128, SLOT, GE]),
                        ALU.mult).then_inc(s_hot, 1)
                dve.wait_ge(s_hot, HOT_LISTS - 1)
                nc.vector.reduce_sum(lists[:].rearrange("p g b -> p (g b)"),
                                     picked[:].rearrange("p g b e -> p (g b) e"), AX_X).then_inc(s_hot, 1)
                dve.wait_ge(s_m, 5)
                nc.vector.tensor_copy(listT[:].rearrange("b e a -> b (e a)"), bank[5][:SLOT, :E * AW]
                                      ).then_inc(s_hot, 1)
                dve.wait_ge(s_m, 6)
                nc.vector.tensor_copy(idx[:].rearrange("p e k -> p k e"), bank[7][:PT_, :NT * E].rearrange(
                    "p (k e) -> p k e", e=E))

        with ExitStack() as four:
            def sb_(name, shape, dt=F32):
                return four.enter_context(nc.sbuf_tensor(name, shape, dt))

            def sem(name):
                return four.enter_context(nc.semaphore(name))

            RING = 4

            EW1 = sb_("EW1", [128, 2, D])
            EW2 = sb_("EW2", [128, 2, DC, C])
            EB1 = sb_("EB1", [128, 2, DC])
            EB2 = sb_("EB2", [PT_, 2, C])
            ids = [[sb_(f"ids{r}_{k}", [PT_, 1], U32) for k in range(NT)] for r in range(RING)]
            tok = sb_("tok", [PT_, RING, NT, ROW])
            tokT = sb_("tokT", [128, 2, N])
            hE = sb_("hE", [128, 2, DC, N])
            score = sb_("score", [PT_, 2, NT])
            yE = sb_("yE", [PT_, 2, NT, C])

            s_w = [sem(f"s_expert_weights{u}") for u in range(2)]
            s_id = sem("s_ids_ready")
            s_ga = [sem(f"s_tokens_gathered{r}") for r in range(RING)]
            s_tp = sem("s_tokT_in_psum")
            s_tc = sem("s_tokT_ready")
            s_scr = sem("s_scores_taken")
            s_h = sem("s_expert_h_in_psum")
            s_hr = sem("s_expert_h_ready")
            s_y = sem("s_expert_y_in_psum")
            s_yb = sem("s_expert_y_biased")
            s_ys = sem("s_expert_y_scored")
            s_sc = sem("s_scattered")
            s_on = [sem(f"s_waits_passed{n}") for n in range(2)]

            block = four.enter_context(nc.Block())

            @block.sync
            def _(sp):
                def load(e, u):
                    sp.dma_start(EW1[:, u], ew1[e]).then_inc(s_w[u], 16)
                    sp.dma_start(EW2[:, u], ew2[e].rearrange("(k p) n -> p k n", p=128)).then_inc(s_w[u], 16)
                    sp.dma_start(EB1[:, u], eb1[e].rearrange("(m p) -> p m", p=128)).then_inc(s_w[u], 16)
                    sp.dma_start(EB2[:, u], eb2[e].rearrange("(o n) -> o n", o=1).broadcast_to([PT_, C])
                                 ).then_inc(s_w[u], 16)

                for u in range(2):
                    load(u, u)
                with sp.Fori(1, E // 2) as i:
                    for u in range(2):
                        sp.wait_ge(s_yb, 2 * i + u - 1)
                        load(2 * i + u, u)

            @block.gpsimd
            def _(pool):
                def gather(e, r):
                    wait_apart(pool, s_id, e + 1, s_on[1])
                    for k in range(NT):
                        nc.gpsimd.indirect_dma_start(
                            out=tok[:, r, k], out_offset=None, in_=table,
                            in_offset=bass.IndirectOffsetOnAxis(ap=ids[r][k][:, 0:1], axis=0)).then_inc(s_ga[r], 16)

                def scatter(e, r):
                    pool.wait_ge(s_ys, NT * (e + 1))
                    wait_apart(pool, s_sc, 16 * NT * e, s_on[1])
                    for k in range(NT):
                        nc.gpsimd.indirect_dma_start(
                            out=out_rows, out_offset=bass.IndirectOffsetOnAxis(ap=ids[r][k][:, 0:1], axis=0),
                            in_=yE[:, r % 2, k], in_offset=None, compute_op=ALU.add,
                            bounds_check=TOK - 1, oob_is_err=True).then_inc(s_sc, 16)

                gather(0, 0)
                gather(1, 1)
                with pool.Fori(0, E // RING) as i:
                    for r in range(RING):
                        gather(RING * i + r + 2, (r + 2) % RING)
                        scatter(RING * i + r, r)
                pool.wait_ge(s_sc, 16 * NT * E)
                for r in range(RING):
                    pool.wait_ge(s_ga[r], 16 * NT * (E // RING + (r < 2)))

            @block.tensor
            def _(pe):
                def transpose_tokens(e, r, turn):
                    pe.wait_ge(s_ga[r], 16 * NT * (turn + 1))
                    wait(pe, s_tc, e)
                    for k in range(NT):
                        last = nc.tensor.transpose(bank[6][:, k * PT_:(k + 1) * PT_], tok[:, r, k, 0:C],
                                                   ident[:PT_, :PT_])
                    last.then_inc(s_tp, 1)

                transpose_tokens(0, 0, 0)
                with pe.Fori(0, E // RING) as i:
                    for r in range(RING):
                        e, u = RING * i + r, r % 2
                        pe.wait_ge(s_w[u], 16 * 4 * (2 * i + r // 2 + 1))
                        pe.wait_ge(s_tc, e + 1)
                        for m in range(DC):
                            pe.wait_ge(s_hr, 4 * e + (m - 1 if m >= 2 else 0))
                            nc.tensor.matmul(bank[m % 2][:, :N], EW1[:, u, m * 128:(m + 1) * 128], tokT[:, u],
                                             start=True, stop=True).then_inc(s_h, 1)
                        transpose_tokens(e + 1, (r + 1) % RING, i + (r == RING - 1))
                        pe.wait_ge(s_hr, 4 * e + 4)
                        pe.wait_ge(s_yb, e)
                        for t in range(NT):
                            for k in range(DC):
                                last = nc.tensor.matmul(bank[2 + u][:PT_, t * C:(t + 1) * C],
                                                        hE[:, u, k, t * PT_:(t + 1) * PT_], EW2[:, u, k],
                                                        start=(k == 0), stop=(k == DC - 1))
                        last.then_inc(s_y, 1)

            @block.scalar
            def _(act):
                with act.Fori(0, E // RING) as i:
                    for r in range(RING):
                        e, u = RING * i + r, r % 2
                        for m in range(DC):
                            act.wait_ge(s_h, 4 * e + m + 1)
                            nc.scalar.activation(hE[:, u, m], bank[m % 2][:, :N], ACT.Gelu_apprx_tanh,
                                                 bias=EB1[:, u, m:m + 1]).then_inc(s_hr, 1)

            @block.vector
            def _(dve):
                def take_ids(e, r):
                    for k in range(NT):
                        last = nc.vector.tensor_copy(ids[r][k][:], idx[:, e, k:k + 1])
                    last.then_inc(s_id, 1)

                def take_tokens(e, r, turn, column):
                    dve.wait_ge(s_tp, e + 1)
                    nc.vector.tensor_copy(tokT[:, r % 2], bank[6][:, :N]).then_inc(s_tc, 1)
                    wait(dve, s_ys, NT * (e - 1))
                    nc.vector.tensor_copy(score[:, r % 2], tok[:, r, :, bass.ds(C + column, 1)].rearrange(
                        "p k o -> p (k o)")).then_inc(s_scr, 1)

                take_ids(0, 0)
                take_ids(1, 1)
                take_tokens(0, 0, 0, 0)
                with dve.Fori(0, E // RING) as i:
                    for r in range(RING):
                        e, u = RING * i + r, r % 2
                        dve.wait_ge(s_sc, 16 * NT * (e - 1) if r else 16 * NT * RING * i)
                        take_ids((e + 2) % E, (r + 2) % RING)
                        take_tokens(e + 1, (r + 1) % RING, i + (r == RING - 1), (e + 1) % E)
                        dve.wait_ge(s_y, e + 1)
                        dve.wait_ge(s_scr, e + 1)
                        nc.vector.tensor_tensor(yE[:, u], bank[2 + u][:PT_, :NT * C].rearrange(
                            "p (t c) -> p t c", c=C), EB2[:, u, None, :].broadcast_to([PT_, NT, C]),
                            ALU.add).then_inc(s_yb, 1)
                        dve.wait_ge(s_yb, e + 1)
                        for k in range(NT):
                            nc.vector.tensor_scalar(yE[:, u, k], yE[:, u, k], score[:, u, k:k + 1], None,
                                                    ALU.mult).then_inc(s_ys, 1)


_INS = ['x', 'L0_tok_W1', 'L0_tok_b1', 'L0_tok_W2', 'L0_tok_b2', 'L0_tok_W3', 'L0_tok_b3', 'L0_attn_gamma',
        'L0_attn_beta', 'L0_attn_wq1', 'L0_attn_wqd', 'L0_attn_wk1', 'L0_attn_wkd', 'L0_attn_wv1', 'L0_attn_wvd',
        'L0_attn_wout', 'L0_ffn_gate_w', 'L0_ffn_w1', 'L0_ffn_b1', 'L0_ffn_w2', 'L0_ffn_b2', 'L0_ffn_sw1',
        'L0_ffn_sb1', 'L0_ffn_sw2', 'L0_ffn_sb2']
_OUTS = [((B, N, C), 'float32')]


def kernel(**inputs):
    import numpy as _np
    import concourse.bacc as _bacc
    from concourse import mybir as _mybir
    from concourse.bass_utils import run_bass_kernel_spmd as _run

    nc = _bacc.Bacc("TRN2", target_bir_lowering=False, num_devices=1)
    arrays, args = {}, []
    for name in _INS:
        a = _np.ascontiguousarray(inputs[name])
        arrays[f"in_{name}_dram"] = a
        args.append(nc.dram_tensor(f"in_{name}_dram", a.shape, _mybir.dt.from_np(a.dtype), kind="ExternalInput").ap())
    for i, (shape, dtype) in enumerate(_OUTS):
        dt = _mybir.dt.from_np(_np.dtype(dtype))
        args.append(nc.dram_tensor(f"out_{i}_dram", shape, dt, kind="ExternalOutput").ap())
    build(nc, *args)
    r = _run(nc, [arrays], core_ids=[0])
    got = tuple(r.results[0][f"out_{i}_dram"] for i in range(len(_OUTS)))
    return got[0]
```

```python
import concourse.bass as bass
from concourse import mybir
from contextlib import ExitStack

F32 = mybir.dt.float32
F32R = mybir.dt.float32r
I32 = mybir.dt.int32
U32 = mybir.dt.uint32
BF16 = mybir.dt.bfloat16
ALU = mybir.AluOpType
ACT = mybir.ActivationFunctionType
AX_X = mybir.AxisListType.X

B, T, C = 16, 750, 128
N = T // 2
PT_ = 125
TT_, NT = T // PT_, N // PT_
D = 512
DC = D // 128
HEADS, DH = 8, 64
E = 16
TOK = B * N
CAP = TOK // E
NE = N + 1
ROW = C + E
TEMP, EPS = 1e-5, 1e-5
MASKED = 3.4028234663852886e38


def slopes(heads):
    return [2.0 ** (-8.0 * (h + 1) / heads) for h in range(heads)]


def wait(eng, sem, value):
    if isinstance(value, int) and value <= 0:
        return
    eng.wait_ge(sem, value)


def wait_apart(eng, sem, value, passed):
    wait(eng, sem, value)
    if not isinstance(value, int):
        eng.sem_inc(passed, 1)


def cap(value, most):
    return min(value, most) if isinstance(value, int) else value


def valid(m):
    return not isinstance(m, int) or 0 <= m < B


def build(nc, x, tW1, tb1, tW2, tb2, tW3, tb3, gamma, beta, wq1, wqd, wk1, wkd, wv1, wvd, wout,
          gate_w, ew1, eb1, ew2, eb2, sw1, sb1, sw2, sb2, out):
    ctx = ExitStack()
    with ctx:
        ctx.enter_context(nc.allow_non_contiguous_dma(reason="short vectors, once"))

        def sb(name, shape, dt=F32):
            return ctx.enter_context(nc.sbuf_tensor(name, shape, dt))

        mid = ctx.enter_context(ExitStack())

        def sbm(name, shape, dt=F32):
            return mid.enter_context(nc.sbuf_tensor(name, shape, dt))

        def sem(name):
            return ctx.enter_context(nc.semaphore(name))

        z_dram = nc.dram_tensor("z_scratch", (B, DC, T), F32, kind="Internal").ap()
        table = nc.dram_tensor("token_table", (TOK, ROW), F32, kind="Internal").ap()
        probs_dram = nc.dram_tensor("probs_scratch", (B, E, N), F32, kind="Internal").ap()
        table_b = table.rearrange("(b n) c -> b n c", n=N)

        bank = [ctx.enter_context(nc.psum_tensor(f"bank{i}", [128, 512], F32)) for i in range(8)]

        ident = sb("ident", [128, 128])
        gammac = sb("gammac", [128, 1])
        betac = sb("betac", [128, 1])
        sb1c = sb("sb1c", [128, DC])
        mhalf = sb("mhalf", [PT_, NT])
        probsT = sb("probsT", [128, 2 * N])
        idx = sb("idx", [PT_, E, NT], U32)
        thr = sb("thr", [128, 1], I32)
        cnt = sb("cnt", [128, 4])
        same = sb("same", [128, 128])
        before = sb("before", [128, 128])

        qkd = sbm("qkd", [128, 2, DC, 3])
        vd = sbm("vd", [128, DC, 3])
        WQKT = sbm("WQKT", [128, 2, 2, D], F32R)
        WVT = sbm("WVT", [128, 2, 3, D], F32R)
        WOT = sbm("WOT", [128, DC, 128])
        gate = sbm("gate", [128, E])
        SW1 = sbm("SW1", [128, D])
        SW2 = sbm("SW2", [128, DC, 128])
        sb2b = sbm("sb2b", [PT_, C])
        nbias = sbm("nbias", [PT_, HEADS, N])
        grid0 = sbm("grid0", [PT_, N])
        grid1 = sbm("grid1", [PT_, N])

        csT = sbm("csT", [PT_, 2 * TT_, B])

        Hall = sbm("Hall", [PT_, B, NT, C])
        tTall = sbm("tTall", [128, TOK])

        PASSES = ((0, 0), (0, 1), (1, 0))

        at = [0, DC * D, DC * D + 3 * D, DC * D + 6 * D, DC * D + 7 * D]
        W2 = tTall[:, at[0]:at[1]].rearrange("p (k n) -> p k n", n=D)
        wraw = tTall[:, at[1]:at[2]].rearrange("p (n m d) -> p n m d", n=3, m=DC)
        wvtap = tTall[:, at[2]:at[3]].rearrange("p (n m d) -> p n m d", n=3, m=DC)
        woraw = tTall[:, at[3]:at[4]]

        out_rows = out.rearrange("b n c -> (b n) c")

        with ExitStack() as one:
            def sb_(name, shape, dt=F32):
                return one.enter_context(nc.sbuf_tensor(name, shape, dt))

            def sem(name):
                return one.enter_context(nc.semaphore(name))

            W1 = sb_("W1", [128, D])[:]
            W1hl = sb_("W1hl", [128, 2, D], F32R)
            W2hl = sb_("W2hl", [128, 2, DC, D], F32R)
            w3c = sb_("w3c", [128, DC])
            w3rep = sb_("w3rep", [128, DC, 32])
            b1c = sb_("b1c", [128, DC])
            b2c = sb_("b2c", [128, DC])
            b3c = sb_("b3c", [B, 1])
            dist = sb_("dist", [PT_, N])
            zrow = sb_("zrow", [B, DC, T])
            imp = sb_("imp", [B, T])
            isum = sb_("isum", [B, 2])
            ones_t = sb_("ones_t", [B, T])
            cs = sb_("cs", [B, T + 1])
            X = sb_("X", [PT_, 2, TT_, C])
            xThl = sb_("xThl", [128, 2, 2, NE], F32R)
            h1 = sb_("h1", [128, DC, NE])
            h1hl = sb_("h1hl", [128, 2, 2, DC, NE], F32R)
            h2 = sb_("h2", [128, 2, DC, N])
            zsb = sb_("zsb", [128, 2, N])

            s_w = sem("s_tok_weights")
            s_w2 = sem("s_other_weights")
            s_wf = sem("s_first_weights")
            s_ws = sem("s_weights_split")
            s_setup = sem("s_split_setup_steps")
            s_hs = sem("s_h1_split")
            s_pool = sem("s_pool_consts")
            s_id = sem("s_identity")
            s_w3 = sem("s_w3_replicated")
            s_prep = sem("s_scaled_weights")
            s_x = [sem(f"s_x_loaded{u}") for u in range(2)]
            s_xp = sem("s_xT_in_psum")
            s_xt = sem("s_xT_ready")
            s_h1 = sem("s_h1_in_psum")
            s_g1 = sem("s_h1_ready")
            s_h2 = sem("s_h2_in_psum")
            s_g2 = sem("s_h2_ready")
            s_z = sem("s_z_in_psum")
            s_zc = sem("s_z_copied")
            s_zs = [sem(f"s_z_stored{u}") for u in range(2)]
            s_zl = sem("s_z_loaded")
            s_zsum = sem("s_z_steps")
            s_sig = sem("s_sigmoid_ready")
            s_cp = sem("s_cs_in_psum")

            block = one.enter_context(nc.Block())
            TOK_W, OTHER_W = 4, 14
            L1_BANKS = (2, 3, 7, 2)

            @block.sync
            def _(sp):
                sp.dma_start(X[:, 0], x[0].rearrange("(k p) c -> p k c", p=PT_)).then_inc(s_x[0], 16)
                sp.dma_start(W1, tW1).then_inc(s_wf, 16)
                sp.dma_start(b1c[:], tb1.rearrange("(m p) -> p m", p=128)).then_inc(s_wf, 16)
                sp.dma_start(W2, tW2.rearrange("(k p) n -> p k n", p=128)).then_inc(s_w, 16)
                sp.dma_start(b2c[:], tb2.rearrange("(m p) -> p m", p=128)).then_inc(s_w, 16)
                sp.dma_start(w3c[:], tW3.rearrange("(m p) o -> p (m o)", p=128)).then_inc(s_w, 16)
                sp.dma_start(b3c[:], tb3.rearrange("(o n) -> o n", o=1).broadcast_to([B, 1])).then_inc(s_w, 16)
                for n, w in enumerate((wq1, wk1, wv1)):
                    sp.dma_start(wraw[:, n], w.rearrange("(m p) d -> p m d", p=128)).then_inc(s_w2, 16)
                for n, w in enumerate((wqd, wkd)):
                    sp.dma_start(qkd[:, n], w.rearrange("(m p) a -> p m a", p=128)).then_inc(s_w2, 16)
                sp.dma_start(vd[:], wvd.rearrange("(m p) a -> p m a", p=128)).then_inc(s_w2, 16)
                sp.dma_start(woraw, wout).then_inc(s_w2, 16)
                sp.dma_start(gammac[:], gamma.rearrange("(p o) -> p o", o=1)).then_inc(s_w2, 16)
                sp.dma_start(betac[:], beta.rearrange("(p o) -> p o", o=1)).then_inc(s_w2, 16)
                sp.dma_start(gate[:], gate_w).then_inc(s_w2, 16)
                sp.dma_start(SW1[:], sw1).then_inc(s_w2, 16)
                sp.dma_start(SW2[:], sw2.rearrange("(k p) n -> p k n", p=128)).then_inc(s_w2, 16)
                sp.dma_start(sb1c[:], sb1.rearrange("(m p) -> p m", p=128)).then_inc(s_w2, 16)
                sp.dma_start(sb2b[:], sb2.rearrange("(o n) -> o n", o=1).broadcast_to([PT_, C])).then_inc(s_w2, 16)
                sp.dma_start(X[:, 1], x[1].rearrange("(k p) c -> p k c", p=PT_)).then_inc(s_x[1], 16)
                with sp.Fori(0, B // 2) as i:
                    for u in range(2):
                        sp.wait_ge(s_xp, 4 * i + 2 * u + 2)
                        nxt = (2 * i + u + 2) % B
                        sp.dma_start(X[:, u], x[nxt].rearrange("(k p) c -> p k c", p=PT_)).then_inc(s_x[u], 16)
                        for half in range(2):
                            sp.wait_ge(s_zc, 4 * i + 2 * u + half + 1)
                            sp.dma_start(z_dram[2 * i + u, :, half * N:(half + 1) * N],
                                         zsb[0:128:32, half]).then_inc(s_zs[half], 16)
                for half in range(2):
                    sp.wait_ge(s_zs[half], 16 * B)
                for u in range(2):
                    sp.wait_ge(s_x[u], 16 * (B // 2 + 1))
                sp.dma_start(zrow[:], z_dram).then_inc(s_zl, 16)
                sp.wait_ge(s_zl, 16)

            @block.gpsimd
            def _(pool):
                nc.gpsimd.memset(ident[:], 0.0).then_inc(s_pool, 1)
                pool.wait_ge(s_pool, 1)
                nc.gpsimd.affine_select(out=ident[:], in_=ident[:], compare_op=ALU.not_equal, fill=1.0, base=0,
                                        pattern=[[-1, 128]], channel_multiplier=1).then_inc(s_id, 1)
                nc.gpsimd.iota(dist[:], pattern=[[-1, N]], base=N - PT_, channel_multiplier=1,
                               allow_small_or_imprecise_dtypes=True).then_inc(s_pool, 1)
                nc.gpsimd.iota(grid0[:], pattern=[[1, N]], base=0, channel_multiplier=0,
                               allow_small_or_imprecise_dtypes=True).then_inc(s_pool, 1)
                nc.gpsimd.iota(grid1[:], pattern=[[1, N]], base=1, channel_multiplier=0,
                               allow_small_or_imprecise_dtypes=True).then_inc(s_pool, 1)
                pool.wait_ge(s_pool, 4)
                nc.gpsimd.memset(grid1[:, N - 1:N], 1e30).then_inc(s_pool, 1)
                nc.gpsimd.memset(mhalf[:], -0.5).then_inc(s_pool, 1)
                nc.gpsimd.memset(ones_t[:], 1.0).then_inc(s_pool, 1)
                nc.gpsimd.memset(cs[:, 0:1], 0.0).then_inc(s_pool, 1)
                for h, slope in enumerate(slopes(HEADS)):
                    nc.gpsimd.tensor_scalar(nbias[:, h], dist[:], slope, None, ALU.mult).then_inc(s_pool, 1)
                    pool.wait_ge(s_pool, 9 + 2 * h)
                    nc.gpsimd.affine_select(out=nbias[:, h], in_=nbias[:, h], compare_op=ALU.is_ge, fill=MASKED,
                                            base=N - PT_, pattern=[[-1, N]], channel_multiplier=1).then_inc(s_pool, 1)
                pool.wait_ge(s_w2, 16 * OTHER_W)
                nc.gpsimd.tensor_scalar(qkd[:, 0], qkd[:, 0], -(DH ** -0.5), None, ALU.mult).then_inc(s_prep, 1)
                for a in range(3):
                    for m in range(DC):
                        nc.gpsimd.tensor_scalar(wvtap[:, a, m], wraw[:, 2, m], vd[:, m, a:a + 1], None,
                                                ALU.mult).then_inc(s_prep, 1)

            @block.tensor
            def _(pe):
                def layer1(g, p):
                    pe.wait_ge(s_xt, 2 * g + 2)
                    for m in range(DC):
                        wait(pe, s_g1, 4 * g + (m == DC - 1))
                        for n, (a, b) in enumerate(PASSES):
                            last = nc.tensor.matmul(bank[L1_BANKS[m]][:, :NE], W1hl[:, a, m * 128:(m + 1) * 128],
                                                    xThl[:, p, b], start=(n == 0), stop=(n == 2))
                        last.then_inc(s_h1, 1)

                def layer2(g, p, ms):
                    pe.wait_ge(s_hs, 4 * g + 4)
                    for m in ms:
                        wait(pe, s_g2, 4 * g + m - 1)
                        for k in range(DC):
                            for n, (a, b) in enumerate(PASSES):
                                last = nc.tensor.matmul(bank[4 + m % 2][:, :NE],
                                                        W2hl[:, a, k, m * 128:(m + 1) * 128], h1hl[:, p, b, k],
                                                        start=(k == 0 and n == 0), stop=(k == DC - 1 and n == 2))
                        last.then_inc(s_h2, 1)

                def layer3(g, p):
                    pe.wait_ge(s_g2, 4 * g + 4)
                    wait(pe, s_zc, g)
                    for c in range(DC):
                        last = nc.tensor.matmul(bank[6][32 * c:32 * c + 32, :N], w3rep[:, c], h2[:, p, c],
                                                start=True, stop=True)
                    last.then_inc(s_z, 1)

                pe.wait_ge(s_id, 1)
                pe.wait_ge(s_x[0], 16)
                for k in range(3):
                    last = nc.tensor.transpose(bank[0][:, k * PT_:(k + 1) * PT_], X[:, 0, k], ident[:PT_, :PT_])
                last.then_inc(s_xp, 1)
                pe.wait_ge(s_ws, 1)
                layer1(0, 0)
                pe.wait_ge(s_w3, 1)
                pe.wait_ge(s_ws, 2)

                def two_batches(i):
                    for s in range(4):
                        g = 4 * i + s
                        p, nxt = s % 2, (s + 1) % 4
                        if nxt % 2 == 0:
                            pe.wait_ge(s_x[nxt // 2], 16 * (i + 1 + (nxt == 0)))
                        wait(pe, s_xt, 2 * g)
                        for k in range(3):
                            last = nc.tensor.transpose(bank[1 - p][:, k * PT_:(k + 1) * PT_],
                                                       X[:, nxt // 2, 3 * (nxt % 2) + k], ident[:PT_, :PT_])
                        last.then_inc(s_xp, 1)
                        layer2(g, p, (0, 1))
                        if not isinstance(g, int) or g > 0:
                            layer3(g - 1, 1 - p)
                        layer1(g + 1, 1 - p)
                        layer2(g, p, (2, 3))

                two_batches(0)
                with pe.Fori(1, B // 2) as i:
                    two_batches(i)
                layer3(2 * B - 1, 1)
                pe.wait_ge(s_g1, 4 * (2 * B + 1))
                pe.wait_ge(s_zsum, 8)
                for n in range(2):
                    for k in range(TT_):
                        col = (n * TT_ + k) * B
                        last = nc.tensor.transpose(bank[4][:PT_, col:col + B],
                                                   cs[:, 1 - n + k * PT_:1 - n + (k + 1) * PT_], ident[:B, :B])
                last.then_inc(s_cp, 1)

            @block.scalar
            def _(act):
                def gelu1(g, p):
                    for m in range(DC):
                        act.wait_ge(s_h1, 4 * g + m + 1)
                        if m == 0:
                            wait(act, s_hs, 4 * g)
                        nc.scalar.activation(h1[:, m], bank[L1_BANKS[m]][:, :NE], ACT.Gelu,
                                             bias=b1c[:, m:m + 1]).then_inc(s_g1, 1)

                def gelu2(g, p, ms):
                    for m in ms:
                        act.wait_ge(s_h2, 4 * g + m + 1)
                        if m == 0:
                            wait(act, s_z, g - 1)
                        nc.scalar.activation(h2[:, p, m], bank[4 + m % 2][:, :N], ACT.Gelu,
                                             bias=b2c[:, m:m + 1]).then_inc(s_g2, 1)

                act.wait_ge(s_wf, 32)
                gelu1(0, 0)
                act.wait_ge(s_w, 16 * TOK_W)

                def two_batches(i):
                    for s in range(4):
                        g, p = 4 * i + s, s % 2
                        gelu2(g, p, (0, 1))
                        gelu1(g + 1, 1 - p)
                        gelu2(g, p, (2, 3))

                two_batches(0)
                with act.Fori(1, B // 2) as i:
                    two_batches(i)
                act.wait_ge(s_zsum, 3)
                nc.scalar.activation(imp[:], zrow[:, 0], ACT.Sigmoid, bias=b3c[:, 0:1]).then_inc(s_sig, 1)

            @block.vector
            def _(dve):
                def split_x(g, p):
                    dve.wait_ge(s_xp, g + 1)
                    wait(dve, s_h1, 4 * g - 4)
                    nc.vector.tensor_copy(xThl[:, p, 0, :N], bank[p][:, :N]).then_inc(s_xt, 1)
                    dve.wait_ge(s_xt, 2 * g + 1)
                    nc.vector.tensor_tensor(xThl[:, p, 1, :N], bank[p][:, :N], xThl[:, p, 0, :N],
                                            ALU.subtract).then_inc(s_xt, 1)

                def split_h(g, p):
                    wait(dve, s_h2, 4 * g - 4)
                    for c in (0, 2):
                        dve.wait_ge(s_g1, 4 * g + c + 2)
                        nc.vector.tensor_copy(h1hl[:, p, 0, c:c + 2], h1[:, c:c + 2]).then_inc(s_hs, 1)
                        dve.wait_ge(s_hs, 4 * g + c + 1)
                        nc.vector.tensor_tensor(h1hl[:, p, 1, c:c + 2], h1[:, c:c + 2], h1hl[:, p, 0, c:c + 2],
                                                ALU.subtract).then_inc(s_hs, 1)

                nc.vector.memset(zsb[:, 0, 0:4], 0.0).then_inc(s_setup, 1)
                dve.wait_ge(s_setup, 1)
                nc.vector.tensor_copy(xThl[:, :, :, N], zsb[:, 0, 0:4].rearrange("p (a b) -> p a b", a=2)
                                      ).then_inc(s_setup, 1)
                dve.wait_ge(s_wf, 32)
                nc.vector.tensor_copy(W1hl[:, 0], W1).then_inc(s_setup, 1)
                dve.wait_ge(s_setup, 3)
                nc.vector.tensor_tensor(W1hl[:, 1], W1, W1hl[:, 0], ALU.subtract).then_inc(s_ws, 1)
                split_x(0, 0)
                dve.wait_ge(s_w, 16 * TOK_W)
                nc.vector.tensor_copy(w3rep[:], w3c[:, :, None].broadcast_to([128, DC, 32])).then_inc(s_w3, 1)
                nc.vector.tensor_copy(W2hl[:, 0], W2).then_inc(s_setup, 1)
                dve.wait_ge(s_setup, 4)
                nc.vector.tensor_tensor(W2hl[:, 1], W2, W2hl[:, 0], ALU.subtract).then_inc(s_ws, 1)
                split_h(0, 0)

                def copy_z(g, p, b):
                    dve.wait_ge(s_z, g + 1)
                    wait(dve, s_zs[p], 16 * b)
                    nc.vector.tensor_copy(zsb[:, p], bank[6][:, :N]).then_inc(s_zc, 1)

                def two_batches(i):
                    for s in range(4):
                        g, p = 4 * i + s, s % 2
                        split_x(g + 1, 1 - p)
                        if not isinstance(g, int) or g > 0:
                            copy_z(g - 1, 1 - p, 2 * i + (s - 1) // 2)
                        split_h(g + 1, 1 - p)

                two_batches(0)
                with dve.Fori(1, B // 2) as i:
                    two_batches(i)
                copy_z(2 * B - 1, 1, B - 1)
                dve.wait_ge(s_zl, 16)
                for c in range(1, DC):
                    nc.vector.tensor_tensor(zrow[:, 0], zrow[:, 0], zrow[:, c], ALU.add).then_inc(s_zsum, 1)
                    dve.wait_ge(s_zsum, c)
                dve.wait_ge(s_sig, 1)
                nc.vector.tensor_scalar(imp[:], imp[:], TEMP, None, ALU.add).then_inc(s_zsum, 1)
                dve.wait_ge(s_zsum, 4)
                nc.vector.reduce_sum(isum[:, 0:1], imp[:], AX_X).then_inc(s_zsum, 1)
                dve.wait_ge(s_zsum, 5)
                nc.vector.reciprocal(isum[:, 1:2], isum[:, 0:1]).then_inc(s_zsum, 1)
                dve.wait_ge(s_zsum, 6)
                nc.vector.tensor_scalar(imp[:], imp[:], isum[:, 1:2], float(N), ALU.mult, ALU.mult).then_inc(s_zsum, 1)
                dve.wait_ge(s_zsum, 7)
                dve.wait_ge(s_pool, 8)
                nc.vector.tensor_tensor_scan(cs[:, 1:T + 1], ones_t[:], imp[:], 0.0, ALU.mult,
                                             ALU.add).then_inc(s_zsum, 1)
                dve.wait_ge(s_cp, 1)
                nc.vector.tensor_copy(csT[:].rearrange("p k b -> p (k b)"), bank[4][:PT_, :2 * TT_ * B])

        with ExitStack() as two:
            def sb_(name, shape, dt=F32):
                return two.enter_context(nc.sbuf_tensor(name, shape, dt))

            def sem(name):
                return two.enter_context(nc.semaphore(name))

            FIRST, LAST = -3, B + 1
            LOOP0, LOOP1 = 3, 13
            XPAD = N + 2
            XE = XPAD + 1
            SEG = (0, N, N + PT_)
            ORDER = (2, 0, 1)
            LN = 9

            X2 = sb_("X2", [PT_, 2, TT_, C])
            csb = sb_("csb", [PT_, 2 * TT_])
            cellmax = sb_("cellmax", [PT_, N])
            overlap = sb_("overlap", [PT_, 2, N])
            Wt = sb_("Wt", [PT_, TT_, N])
            lnstat = sb_("lnstat", [PT_, NT, 6])
            lnmv = sb_("lnmv", [PT_, NT, 2])
            lnve = sb_("lnve", [PT_, NT])
            lnr = sb_("lnr", [PT_, NT])
            gstat = sb_("gstat", [PT_, NT, 6])
            gmv = sb_("gmv", [PT_, NT, 2])
            gve = sb_("gve", [PT_, NT])
            gr = sb_("gr", [PT_, NT])
            n1 = sb_("n1", [PT_, NT, C])
            n2 = sb_("n2", [PT_, NT, C])
            xnT = sb_("xnT", [128, N])
            xnThl = sb_("xnThl", [128, 2, 2, XE], F32R)
            xzero = sb_("xzero", [128, 2, 2, 2])
            tap0 = sb_("tap0", [128, 2, N])
            tap1 = sb_("tap1", [128, 2, N])
            QK = sb_("QK", [128, 2, DC, N])
            V = sb_("V", [PT_, 2, NT, D])
            P = sb_("P", [PT_, 4, 2 * N])
            nmax = sb_("nmax", [PT_, 4, NT])
            psum_ = sb_("psum_", [PT_, 4, NT])
            prec = sb_("prec", [PT_, 4, NT])
            PT = sb_("PT", [PT_, 4, 2 * N])
            OT = sb_("OT", [128, DC, N])
            row = sb_("row", [PT_, NT, ROW])
            tT = sb_("tT", [128, N])
            lg = sb_("lg", [PT_, NT, E])
            lmax = sb_("lmax", [PT_, NT])
            lsum = sb_("lsum", [PT_, NT])
            lrec = sb_("lrec", [PT_, NT])
            pTs = sb_("pTs", [E, N])

            bS, bT, bO = (bank[0], bank[1]), (bank[2], bank[3]), bank[4]
            G0, G1, G2 = bank[5], bank[6], bank[7]

            s_x2 = [sem(f"s_x2_loaded{u}") for u in range(2)]
            s_csb = sem("s_cs_of_batch")
            s_cm = sem("s_cellmax_ready")
            s_ov = sem("s_overlap_ready")
            s_wt = sem("s_pool_weights_ready")
            s_ein = sem("s_pooled_in_psum")
            s_lnd = sem("s_ln_dve_steps")
            s_lnp = sem("s_ln_rsqrt_steps")
            s_xtp = sem("s_xnT_in_psum")
            s_xt = sem("s_xnT_ready")
            s_xh = sem("s_xnT_steps")
            s_pad = sem("s_xnT_padded")
            s_qkp = sem("s_qk_in_psum")
            s_t0 = sem("s_tap0_ready")
            s_t1 = sem("s_tap1_ready")
            s_qk = sem("s_qk_ready")
            s_vp = sem("s_v_in_psum")
            s_v = sem("s_v_ready")
            s_sp = sem("s_scores_in_psum")
            s_s = sem("s_scores_ready")
            s_ex = sem("s_exp_ready")
            s_rc = sem("s_recip_ready")
            s_pn = sem("s_probs_normalised")
            s_tp = sem("s_probs_transposed_in_psum")
            s_pt0 = sem("s_probsT0_ready")
            s_pt1 = sem("s_probsT1_ready")
            s_pv = sem("s_pv_in_psum")
            s_o = sem("s_attended_ready")
            s_wo = sem("s_projected_in_psum")
            s_g = sem("s_residual_and_gate_steps")
            s_gp = sem("s_gate_ln_rsqrt_steps")
            s_ttp = sem("s_tT_in_psum")
            s_tt = sem("s_tT_ready")
            s_lp = sem("s_logits_in_psum")
            s_lm = sem("s_logits_shifted")
            s_le = sem("s_logits_exp")
            s_lf = sem("s_probabilities_steps")
            s_pp = sem("s_probsT_in_psum")
            s_pc = sem("s_probsT_copied")
            s_tab = sem("s_table_stored")
            s_tts = sem("s_tT_stored")
            s_ps = sem("s_probsT_stored")

            s_wtp = sem("s_weights_transposed_in_psum")
            s_wh = sem("s_weights_high_part")
            s_wl = sem("s_weights_low_part")

            s_on = [sem(f"s_waits_passed{n}") for n in range(2)]

            split_weights = [(wraw[:, n], WQKT[:, :, n]) for n in range(2)]
            split_weights += [(wvtap[:, a], WVT[:, :, a]) for a in range(3)]

            block = two.enter_context(nc.Block())

            def projection_step(b, h):
                return h + 2 if isinstance(b, int) and b == -1 else h

            def bodies(eng, body):
                for b in range(FIRST, LOOP0):
                    body(b, b % 2)
                with eng.Fori(LOOP0, LOOP1 - 1, 2) as i:
                    body(i, LOOP0 % 2)
                    body(i + 1, (LOOP0 + 1) % 2)
                for b in range(LOOP1, LAST + 1):
                    body(b, b % 2)

            @block.sync
            def _(sp):
                def body(b, u):
                    if valid(b + 3):
                        wait(sp, s_ein, b + 2)
                        sp.dma_start(X2[:, (u + 1) % 2], x[b + 3].rearrange("(k p) c -> p k c", p=PT_)
                                     ).then_inc(s_x2[(u + 1) % 2], 16)
                    m = b - 2
                    if valid(m):
                        sp.wait_ge(s_lf, 3 * m + 3)
                        sp.dma_start(table_b[m].rearrange("(t p) c -> p t c", p=PT_), row[:]
                                     ).then_inc(s_tab, 16)
                        sp.wait_ge(s_pc, m + 1)
                        sp.dma_start(probs_dram[m], pTs[:]).then_inc(s_ps, 16)
                    m = b - 1
                    if valid(m):
                        sp.wait_ge(s_tt, m + 1)
                        sp.dma_start(tTall[:, bass.ds(m * N, N)], tT[:]).then_inc(s_tts, 16)

                bodies(sp, body)
                sp.wait_ge(s_tab, 16 * B)
                sp.wait_ge(s_ps, 16 * B)
                sp.wait_ge(s_tts, 16 * B)

            @block.tensor
            def _(pe):
                def scores(b, h):
                    c, r = h // 2, DH * (h % 2)
                    pe.wait_ge(s_qk, 8 * b + 2 * c + 2)
                    for unit, tiles in enumerate(((2,), (0, 1))):
                        wait(pe, s_s, 3 * (8 * b + h) - 2 + 2 * unit)
                        for i in tiles:
                            w, at = (i + 1) * PT_, 0 if i != 1 else PT_
                            last = nc.tensor.matmul(bS[unit][:PT_, at:at + w],
                                                    QK[r:r + DH, 0, c, i * PT_:(i + 1) * PT_],
                                                    QK[r:r + DH, 1, c, :w], start=True, stop=True)
                        last.then_inc(s_sp, 1)

                def transpose_probs(b, h):
                    n = 8 * b + h
                    pe.wait_ge(s_pn, 3 * n + 3)
                    wait(pe, s_pt0, n)
                    for i in range(NT):
                        last = nc.tensor.transpose(bT[0][:PT_, i * PT_:(i + 1) * PT_],
                                                   P[:, h % 4, SEG[ORDER.index(i)]:SEG[ORDER.index(i)] + PT_],
                                                   ident[:PT_, :PT_])
                    last.then_inc(s_tp, 1)
                    wait(pe, s_pt1, n)
                    for at, (i, j) in enumerate(((1, 1), (2, 1), (2, 2))):
                        f = SEG[ORDER.index(i)] + j * PT_
                        last = nc.tensor.transpose(bT[1][:PT_, at * PT_:(at + 1) * PT_], P[:, h % 4, f:f + PT_],
                                                   ident[:PT_, :PT_])
                    last.then_inc(s_tp, 1)

                def attend(b, c, u):
                    pe.wait_ge(s_pt0, 8 * b + 2 * c + 2)
                    pe.wait_ge(s_pt1, 8 * b + 2 * c + 2)
                    pe.wait_ge(s_v, 3 * b + 3)
                    wait(pe, s_o, 4 * b + c)
                    for j, at in enumerate((0, N, 2 * N - PT_)):
                        for h in (2 * c, 2 * c + 1):
                            r, w = DH * (h % 2), N - j * PT_
                            last = nc.tensor.matmul(bO[r:r + DH, j * PT_:N], V[:, u, j, h * DH:(h + 1) * DH],
                                                    PT[:, h % 4, at:at + w], start=(j == 0), stop=(j == NT - 1))
                    last.then_inc(s_pv, 1)

                def project_qk(m, c, u):
                    pe.wait_ge(s_xt, m + 1)
                    for n, g in enumerate((G0, G1)):
                        if n == 0 and c > 0:
                            wait(pe, s_v, 3 * m + c)
                        elif n == 0:
                            wait(pe, s_qk, 8 * m - 1)
                        else:
                            wait(pe, s_qk, 8 * m + 2 * c)
                            if c == 0:
                                wait(pe, s_pc, m - 2)
                            if c == 3:
                                wait(pe, s_lm, 2 * (m - 1))
                        for n_, (a, x_) in enumerate(PASSES):
                            last = nc.tensor.matmul(g[:, :XE], WQKT[:, a, n, c * 128:(c + 1) * 128], xnThl[:, u, x_],
                                                    start=(n_ == 0), stop=(n_ == 2))
                        last.then_inc(s_qkp, 1)

                def project_v(m, t, u):
                    pe.wait_ge(s_qk, 8 * m + 2 * t + 1)
                    for a in range(3):
                        for n_, (x_, w_) in enumerate(PASSES):
                            last = nc.tensor.matmul(G0[:PT_, :], xnThl[:, u, x_, t * PT_ + a:(t + 1) * PT_ + a],
                                                    WVT[:, w_, a], start=(a == 0 and n_ == 0),
                                                    stop=(a == 2 and n_ == 2))
                    last.then_inc(s_vp, 1)

                def pool_tokens(m, u):
                    pe.wait_ge(s_wt, 6 * m + 6)
                    pe.wait_ge(s_x2[u], (m - u) * 8 + 16)
                    wait(pe, s_xt, m)
                    wait(pe, s_tt, m - 3)
                    for t in range(NT):
                        for k in range(TT_):
                            last = nc.tensor.matmul(G2[:PT_, t * C:(t + 1) * C], Wt[:, k, t * PT_:(t + 1) * PT_],
                                                    X2[:, u, k], start=(k == 0), stop=(k == TT_ - 1))
                    last.then_inc(s_ein, 1)

                def transpose_tokens(src, done):
                    for t in range(NT):
                        last = nc.tensor.transpose(G2[:, t * PT_:(t + 1) * PT_], src[:, t, 0:C], ident[:PT_, :PT_])
                    last.then_inc(done, 1)

                def body(b, u):
                    v_ = 1 - u
                    for h in range(HEADS):
                        if valid(b):
                            scores(b, h)
                        if h < 2 and valid(b - 1):
                            transpose_probs(b - 1, HEADS - 2 + h)
                        if h >= 2 and valid(b):
                            transpose_probs(b, h - 2)
                        if h == 0 and valid(b):
                            project_qk(b, 3, u)
                        if isinstance(b, int) and (b, h) == (-1, 0):
                            pe.wait_ge(s_wl, len(split_weights))
                            pe.wait_ge(s_wh, len(split_weights) + 1)
                            pe.wait_ge(s_pad, 3)
                        p = projection_step(b, h)
                        if p in (2, 4, 6) and valid(b + 1):
                            project_qk(b + 1, p // 2 - 1, v_)
                        if h == 1 and valid(b + 2):
                            pool_tokens(b + 2, u)
                        if h == 1 and valid(b - 2):
                            m = b - 2
                            pe.wait_ge(s_qk, cap(8 * b + 8, 8 * B))
                            pe.wait_ge(s_lf, 3 * m + 3)
                            for t in range(NT):
                                last = nc.tensor.transpose(G1[:E, t * PT_:(t + 1) * PT_], row[:, t, C:ROW],
                                                           ident[:PT_, :PT_])
                            last.then_inc(s_pp, 1)
                        if h in (0, 2) and valid(b - 1):
                            attend(b - 1, 2 + h // 2, v_)
                        if h in (4, 6) and valid(b):
                            attend(b, h // 2 - 2, u)
                        if h == 3 and valid(b - 1):
                            m = b - 1
                            pe.wait_ge(s_o, 4 * m + 4)
                            pe.wait_ge(s_lnd, cap((2 * LN + 1) * (b + 2) + 1, (2 * LN + 1) * B))
                            for t in range(NT):
                                for c in range(DC):
                                    last = nc.tensor.matmul(G2[:PT_, t * C:(t + 1) * C],
                                                            OT[:, c, t * PT_:(t + 1) * PT_], WOT[:, c],
                                                            start=(c == 0), stop=(c == DC - 1))
                            last.then_inc(s_wo, 1)
                        if p in (3, 5, 7) and valid(b + 1):
                            project_v(b + 1, (p - 3) // 2, v_)
                        if h == 4 and valid(b + 2):
                            m = b + 2
                            pe.wait_ge(s_lnd, (2 * LN + 1) * (m + 1))
                            wait(pe, s_g, (LN + 1) * (m - 3) + 1)
                            transpose_tokens(n2, s_xtp)
                        if h == 6 and valid(b - 1):
                            m = b - 1
                            pe.wait_ge(s_g, (LN + 1) * (m + 1))
                            pe.wait_ge(s_xh, cap(2 * (b + 3), 2 * B))
                            transpose_tokens(row, s_ttp)
                        if h == 7 and valid(b - 1):
                            m = b - 1
                            pe.wait_ge(s_tt, m + 1)
                            pe.wait_ge(s_qk, cap(8 * (b + 1) + 6, 8 * B))
                            wait(pe, s_pc, cap(m, B))
                            for t in range(NT):
                                last = nc.tensor.matmul(G1[:PT_, t * E:(t + 1) * E], tT[:, t * PT_:(t + 1) * PT_],
                                                        gate[:], start=True, stop=True)
                            last.then_inc(s_lp, 1)

                for n, (src, _) in enumerate(split_weights + [(woraw.rearrange("p (m d) -> p m d", m=DC), WOT)]):
                    for m in range(DC):
                        last = nc.tensor.transpose(bank[n][:, m * 128:(m + 1) * 128], src[:, m], ident[:])
                    last.then_inc(s_wtp, 1)
                bodies(pe, body)

            @block.scalar
            def _(act):
                def body(b, u):
                    for h in range(HEADS):
                        if valid(b):
                            n = 8 * b + h
                            for q, i in enumerate(ORDER):
                                w = (i + 1) * PT_
                                act.wait_ge(s_s, 3 * n + q + 1)
                                nc.scalar.activation(P[:, h % 4, SEG[q]:SEG[q] + w], P[:, h % 4, SEG[q]:SEG[q] + w],
                                                     ACT.Exp, bias=nmax[:, h % 4, q:q + 1], scale=-1.0,
                                                     accum_out=psum_[:, h % 4, q:q + 1]).then_inc(s_ex, 1)
                        p = projection_step(b, h)
                        m, c = (b, 3) if p == 0 else (b + 1, p // 2 - 1)
                        if p in (0, 2, 4, 6) and valid(m):
                            for q in range(2):
                                n = 8 * m + 2 * c + q
                                act.wait_ge(s_qkp, n + 1)
                                wait(act, s_t1, n - 1)
                                nc.scalar.activation(tap0[:, q], (G0, G1)[q][:, 0:N], ACT.Copy,
                                                     scale=qkd[:, q, c, 0:1]).then_inc(s_t0, 1)
                        m = b if h >= 2 else b - 1
                        if valid(m):
                            n, hh = 8 * m + (h - 2) % 8, (h - 2) % 4
                            wait(act, s_pv, 4 * m + ((h - 2) % 8) // 2 - 1)
                            if h % 2:
                                act.wait_ge(s_tp, 2 * n + 1)
                                nc.scalar.copy(PT[:, hh, 0:N], bT[0][:PT_, :N]).then_inc(s_pt0, 1)
                            act.wait_ge(s_tp, 2 * n + 2)
                            nc.scalar.copy(PT[:, hh, N:2 * N], bT[1][:PT_, :N]).then_inc(s_pt1, 1)
                        m, c = (b, h // 2 - 2) if h >= 4 else (b - 1, h // 2 + 2)
                        if h % 2 == 0 and valid(m):
                            act.wait_ge(s_pv, 4 * m + c + 1)
                            wait(act, s_wo, m)
                            nc.scalar.copy(OT[:, c], bO[:, :N]).then_inc(s_o, 1)
                        if p in (3, 5, 7) and valid(b + 1):
                            m, t = b + 1, (p - 3) // 2
                            act.wait_ge(s_vp, 3 * m + t + 1)
                            wait(act, s_pv, 4 * (m - 1))
                            nc.scalar.copy(V[:, 1 - u, t], G0[:PT_, :]).then_inc(s_v, 1)
                        if h == 4 and valid(b + 2):
                            m = b + 2
                            act.wait_ge(s_xtp, m + 1)
                            wait(act, s_xt, m)
                            nc.scalar.activation(xnT[:], G2[:, :N], ACT.Identity, bias=betac[:, 0:1],
                                                 scale=gammac[:, 0:1]).then_inc(s_xh, 1)
                            nc.scalar.activation(xnThl[:, u, 0, 2:XPAD], G2[:, :N], ACT.Identity,
                                                 bias=betac[:, 0:1], scale=gammac[:, 0:1]).then_inc(s_xh, 1)
                        if h == 6 and valid(b - 1):
                            m = b - 1
                            act.wait_ge(s_ttp, m + 1)
                            wait(act, s_tts, 16 * m)
                            wait(act, s_lp, m)
                            nc.scalar.copy(tT[:], G2[:, :N]).then_inc(s_tt, 1)
                        if h == 7 and valid(b - 1):
                            m = b - 1
                            act.wait_ge(s_lm, 2 * m + 2)
                            nc.scalar.activation(lg[:], lg[:], ACT.Exp).then_inc(s_le, 1)
                        m, k = (b + 3, h - 3) if h else (b + 2, TT_ - 1)
                        if h not in (1, 2) and valid(m):
                            act.wait_ge(s_ov, 6 * m + k + 1)
                            wait(act, s_ein, m)
                            nc.scalar.activation(Wt[:, k], overlap[:, k % 2], ACT.Relu).then_inc(s_wt, 1)
                        if isinstance(b, int) and (b, h) == (-2, 0):
                            for n, (_, dst) in enumerate(split_weights):
                                act.wait_ge(s_wtp, n + 1)
                                nc.scalar.copy(dst[:, 0], bank[n][:]).then_inc(s_wh, 1)
                            act.wait_ge(s_wtp, len(split_weights) + 1)
                            nc.scalar.copy(WOT[:].rearrange("p m d -> p (m d)"), bank[len(split_weights)][:]
                                           ).then_inc(s_wh, 1)

                bodies(act, body)

            @block.gpsimd
            def _(pool):
                nc.gpsimd.memset(xzero[:], 0.0).then_inc(s_pad, 1)
                pool.wait_ge(s_pad, 1)
                nc.gpsimd.tensor_copy(xnThl[:, :, :, 0:2], xzero[:]).then_inc(s_pad, 1)
                nc.gpsimd.tensor_copy(xnThl[:, :, :, XPAD], xzero[:, :, :, 0]).then_inc(s_pad, 1)

                def rsqrt(ve, r, mv, sem_, n, dve_sem, dve_n):
                    wait_apart(pool, dve_sem, dve_n, s_on[1])
                    nc.gpsimd.tensor_scalar(ve[:], mv[:, :, 1], EPS, None, ALU.add).then_inc(sem_, 1)
                    pool.wait_ge(sem_, n + 1)
                    nc.gpsimd.tensor_tensor(r[:], ve[:], mhalf[:], ALU.pow).then_inc(sem_, 1)

                def body(b, u):
                    for h in range(HEADS):
                        if valid(b + 2):
                            m, base = b + 2, (2 * LN + 1) * (b + 2)
                            if h == 1:
                                rsqrt(lnve, lnr, lnmv, s_lnp, 4 * m, s_lnd, base + 7)
                            if h == 2:
                                rsqrt(lnve, lnr, lnmv, s_lnp, 4 * m + 2, s_lnd, base + LN + 7)
                        if h == 4 and valid(b - 1):
                            m = b - 1
                            rsqrt(gve, gr, gmv, s_gp, 2 * m, s_g, (LN + 1) * m + 7)

                bodies(pool, body)

            @block.vector
            def _(dve):
                def ln_stats(src, stat, mv, s, n):
                    for t in range(NT):
                        nc.vector.bn_stats(stat[:, t], src(t)).then_inc(s, 1)
                    for t in range(NT):
                        wait_apart(dve, s, n + t + 1, s_on[0])
                        nc.vector.bn_aggr(mv[:, t], stat[:, t]).then_inc(s, 1)

                def ln_apply(dst, src, mv, r, s):
                    for t in range(NT):
                        nc.vector.tensor_scalar(dst[:, t, 0:C], src(t), mv[:, t, 0:1], r[:, t:t + 1],
                                                ALU.subtract, ALU.mult).then_inc(s, 1)

                def body(b, u):
                    for h in range(HEADS):
                        if isinstance(b, int) and (b, h) == (-2, 0):
                            for n, (_, dst) in enumerate(split_weights):
                                dve.wait_ge(s_wh, n + 1)
                                nc.vector.tensor_tensor(dst[:, 1], bank[n][:], dst[:, 0],
                                                        ALU.subtract).then_inc(s_wl, 1)
                        m = b if h else b - 1
                        if valid(m):
                            n, hh = 8 * m + (h - 1) % 8, (h - 1) % 4
                            dve.wait_ge(s_ex, 3 * n + 3)
                            nc.vector.reciprocal(prec[:, hh], psum_[:, hh]).then_inc(s_rc, 1)
                            dve.wait_ge(s_rc, n + 1)
                            for q, i in enumerate(ORDER):
                                w = (i + 1) * PT_
                                nc.vector.tensor_scalar(P[:, hh, SEG[q]:SEG[q] + w], P[:, hh, SEG[q]:SEG[q] + w],
                                                        prec[:, hh, q:q + 1], None, ALU.mult).then_inc(s_pn, 1)
                        if valid(b):
                            n = 8 * b + h
                            wait(dve, s_tp, 2 * (n - 3))
                            for q, i in enumerate(ORDER):
                                w, at = (i + 1) * PT_, 0 if i != 1 else PT_
                                if q < 2:
                                    wait_apart(dve, s_sp, 2 * n + q + 1, s_on[0])
                                nc.vector.tensor_tensor_reduce(
                                    out=P[:, h % 4, SEG[q]:SEG[q] + w], in0=bS[min(q, 1)][:PT_, at:at + w],
                                    in1=nbias[:, h, (2 - i) * PT_:N], scale=1.0, scalar=MASKED, op0=ALU.add,
                                    op1=ALU.min, accum_out=nmax[:, h % 4, q:q + 1]).then_inc(s_s, 1)
                        m = b if h >= 2 else b - 1
                        if valid(m) and h % 2 == 0:
                            n, hh = 8 * m + (h - 2) % 8, (h - 2) % 4
                            dve.wait_ge(s_tp, 2 * n + 1)
                            wait(dve, s_pv, 4 * m + ((h - 2) % 8) // 2 - 1)
                            nc.vector.tensor_copy(PT[:, hh, 0:N], bT[0][:PT_, :N]).then_inc(s_pt0, 1)
                        if h == 0 and valid(b - 2):
                            m = b - 2
                            dve.wait_ge(s_le, m + 1)
                            nc.vector.reduce_sum(lsum[:], lg[:], AX_X).then_inc(s_lf, 1)
                            dve.wait_ge(s_lf, 3 * m + 1)
                            nc.vector.reciprocal(lrec[:], lsum[:]).then_inc(s_lf, 1)
                            dve.wait_ge(s_lf, 3 * m + 2)
                            nc.vector.tensor_tensor(row[:, :, C:ROW], lg[:],
                                                    lrec[:, :, None].broadcast_to([PT_, NT, E]),
                                                    ALU.mult).then_inc(s_lf, 1)
                        if h >= 2 and valid(b + 3):
                            m, k = b + 3, h - 2
                            dve.wait_ge(s_csb, m + 1)
                            wait(dve, s_ov, 6 * m + k)
                            nc.vector.tensor_scalar(cellmax[:], grid0[:], csb[:, TT_ + k:TT_ + k + 1], None,
                                                    ALU.max).then_inc(s_cm, 1)
                            dve.wait_ge(s_cm, 6 * m + k + 1)
                            wait(dve, s_wt, 6 * m + k - 1)
                            nc.vector.scalar_tensor_tensor(out=overlap[:, k % 2], in0=grid1[:], scalar=csb[:, k:k + 1],
                                                           in1=cellmax[:], op0=ALU.min,
                                                           op1=ALU.subtract).then_inc(s_ov, 1)
                        p = projection_step(b, h)
                        m, c = (b, 3) if p == 0 else (b + 1, p // 2 - 1)
                        if p in (0, 2, 4, 6) and valid(m):
                            for q in range(2):
                                n = 8 * m + 2 * c + q
                                ps = (G0, G1)[q]
                                dve.wait_ge(s_t0, n + 1)
                                nc.vector.scalar_tensor_tensor(out=tap1[:, q], in0=ps[:, 1:N + 1],
                                                               scalar=qkd[:, q, c, 1:2], in1=tap0[:, q],
                                                               op0=ALU.mult, op1=ALU.add).then_inc(s_t1, 1)
                                dve.wait_ge(s_t1, n + 1)
                                wait(dve, s_sp, 16 * (m - 1) + 4 * c + 4)
                                nc.vector.scalar_tensor_tensor(out=QK[:, q, c], in0=ps[:, 2:N + 2],
                                                               scalar=qkd[:, q, c, 2:3], in1=tap1[:, q],
                                                               op0=ALU.mult, op1=ALU.add).then_inc(s_qk, 1)
                        if h == 1 and valid(b + 2):
                            m, base = b + 2, (2 * LN + 1) * (b + 2)
                            dve.wait_ge(s_ein, m + 1)
                            nc.vector.tensor_copy(Hall[:, m], G2[:PT_, :NT * C].rearrange("p (t c) -> p t c", c=C)
                                                  ).then_inc(s_lnd, 1)
                            wait_apart(dve, s_lnd, base + 1, s_on[0])
                            ln_stats(lambda t: Hall[:, m, t], lnstat, lnmv, s_lnd, base + 1)
                        if h == 2 and valid(b + 2):
                            m, base = b + 2, (2 * LN + 1) * (b + 2)
                            dve.wait_ge(s_lnp, 4 * m + 2)
                            ln_apply(n1, lambda t: Hall[:, m, t], lnmv, lnr, s_lnd)
                            dve.wait_ge(s_lnd, base + LN + 1)
                            ln_stats(lambda t: n1[:, t], lnstat, lnmv, s_lnd, base + LN + 1)
                        if h == 3 and valid(b + 2):
                            m, base = b + 2, (2 * LN + 1) * (b + 2)
                            dve.wait_ge(s_lnp, 4 * m + 4)
                            wait(dve, s_xtp, m)
                            ln_apply(n2, lambda t: n1[:, t], lnmv, lnr, s_lnd)
                        if h == 5 and valid(b + 2):
                            m = b + 2
                            dve.wait_ge(s_xh, 2 * m + 2)
                            nc.vector.tensor_tensor(xnThl[:, u, 1, 2:XPAD], xnT[:], xnThl[:, u, 0, 2:XPAD],
                                                    ALU.subtract).then_inc(s_xt, 1)
                        if h == 1 and valid(b - 2):
                            m = b - 2
                            dve.wait_ge(s_pp, m + 1)
                            wait(dve, s_ps, 16 * m)
                            nc.vector.tensor_copy(pTs[:], G1[:E, :N]).then_inc(s_pc, 1)
                        if h == 1 and valid(b + 3):
                            m = b + 3
                            wait(dve, s_wt, 6 * m)
                            nc.vector.tensor_copy(csb[:], csT[:, :, m]).then_inc(s_csb, 1)
                        if h == 3 and valid(b - 1):
                            m, base = b - 1, (LN + 1) * (b - 1)
                            dve.wait_ge(s_wo, m + 1)
                            nc.vector.tensor_tensor(Hall[:, m], Hall[:, m],
                                                    G2[:PT_, :NT * C].rearrange("p (t c) -> p t c", c=C),
                                                    ALU.add).then_inc(s_g, 1)
                            wait_apart(dve, s_g, base + 1, s_on[0])
                            ln_stats(lambda t: Hall[:, m, t], gstat, gmv, s_g, base + 1)
                        if h == 5 and valid(b - 1):
                            m = b - 1
                            dve.wait_ge(s_gp, 2 * m + 2)
                            wait(dve, s_tab, 16 * m)
                            wait(dve, s_ttp, m)
                            wait(dve, s_pp, m)
                            ln_apply(row, lambda t: Hall[:, m, t], gmv, gr, s_g)
                        if h == 7 and valid(b - 1):
                            m = b - 1
                            dve.wait_ge(s_lp, m + 1)
                            nc.vector.reduce_max(lmax[:], G1[:PT_, :NT * E].rearrange("p (t e) -> p t e", e=E),
                                                 AX_X).then_inc(s_lm, 1)
                            dve.wait_ge(s_lm, 2 * m + 1)
                            nc.vector.tensor_tensor(lg[:], G1[:PT_, :NT * E].rearrange("p (t e) -> p t e", e=E),
                                                    lmax[:, :, None].broadcast_to([PT_, NT, E]),
                                                    ALU.subtract).then_inc(s_lm, 1)

                bodies(dve, body)


        with ExitStack() as three:
            def sb_(name, shape, dt=F32):
                return three.enter_context(nc.sbuf_tensor(name, shape, dt))

            def sem(name):
                return three.enter_context(nc.semaphore(name))

            TOPBIT = 29
            S_BANKS = (0, 1, 5, 6)
            hS = sb_("hS", [128, 2, DC, N])
            oS = sb_("oS", [PT_, 2, NT, C])
            diff = sb_("diff", [128, 128], I32)
            step = sb_("step", [128, 2], I32)
            cand = sb_("cand", [128, 1], I32)
            grow = sb_("grow", [128, 1], I32)
            flags = sb_("flags", [128, 2 * N])

            s_c = sem("s_pool_consts2")
            s_i = sem("s_dve_consts2")
            s_h = sem("s_shared_h_in_psum")
            s_hr = sem("s_shared_h_ready")
            s_y = sem("s_shared_y_in_psum")
            s_yr = sem("s_shared_steps")
            s_out = [sem(f"s_shared_stored{u}") for u in range(2)]
            s_pl = sem("s_probsT_loaded")
            s_hb = sem("s_shared_bias_added")
            s_n = sem("s_count_ready")
            s_tot = sem("s_total_in_psum")
            s_thr = sem("s_threshold_steps")

            block = three.enter_context(nc.Block())

            @block.gpsimd
            def _(pool):
                nc.gpsimd.iota(diff[:], pattern=[[-1, 128]], base=128, channel_multiplier=1).then_inc(s_c, 1)
                pool.wait_ge(s_i, 2)
                nc.gpsimd.affine_select(out=before[:], in_=same[:], compare_op=ALU.is_gt, fill=0.0, base=0,
                                        pattern=[[1, 128]], channel_multiplier=-1).then_inc(s_c, 1)
                with pool.Fori(0, B) as b:
                    nc.gpsimd.tensor_tensor(Hall[:, b], Hall[:, b], sb2b[:, None, :].broadcast_to([PT_, NT, C]),
                                            ALU.add).then_inc(s_hb, 1)

            @block.sync
            def _(sp):
                for pair in range(B // 2):
                    sp.dma_start(probsT[pair * E:(pair + 1) * E].rearrange("e (u n) -> e u n", u=2),
                                 probs_dram[2 * pair:2 * pair + 2].rearrange("u e n -> e u n")
                                 ).then_inc(s_pl, 16)
                with sp.Fori(0, B // 2) as i:
                    for u in range(2):
                        sp.wait_ge(s_yr, 2 * i + u + 1)
                        sp.dma_start(out[2 * i + u].rearrange("(t p) c -> p t c", p=PT_), oS[:, u]
                                     ).then_inc(s_out[u], 16)
                for u in range(2):
                    sp.wait_ge(s_out[u], 16 * (B // 2))
                sp.wait_ge(s_pl, 16 * (B // 2))

            def turns(eng, turn):
                for b in range(2):
                    turn(b, b)
                with eng.Fori(1, B // 2) as i:
                    for u in range(2):
                        turn(2 * i + u, u)
                for b in range(B, B + 2):
                    turn(b, b % 2)

            @block.tensor
            def _(pe):
                def total(n):
                    pe.wait_ge(s_n, n + 1)
                    nc.tensor.matmul(bank[4][:, 0:1], same[:], cnt[:, 0:1], start=True, stop=True).then_inc(s_tot, 1)

                def turn(b, u):
                    if valid(b):
                        for m in range(DC):
                            wait(pe, s_hr, 4 * (b - 1) + m + 1)
                            nc.tensor.matmul(bank[S_BANKS[m]][:, :N], SW1[:, m * 128:(m + 1) * 128],
                                             tTall[:, bass.ds(b * N, N)], start=True, stop=True).then_inc(s_h, 1)
                        total(2 * b)
                    if valid(b - 1):
                        wait(pe, s_hr, 4 * b)
                        wait(pe, s_yr, b - 2)
                        for t in range(NT):
                            for k in range(DC):
                                last = nc.tensor.matmul(bank[3 - u][:PT_, t * C:(t + 1) * C],
                                                        hS[:, 1 - u, k, t * PT_:(t + 1) * PT_], SW2[:, k],
                                                        start=(k == 0), stop=(k == DC - 1))
                        last.then_inc(s_y, 1)
                    if valid(b):
                        total(2 * b + 1)

                pe.wait_ge(s_i, 2)
                turns(pe, turn)

            @block.scalar
            def _(act):
                def turn(b, u):
                    if valid(b):
                        for m in range(DC):
                            act.wait_ge(s_h, 4 * b + m + 1)
                            if m == 0:
                                wait(act, s_y, b - 1)
                            nc.scalar.activation(hS[:, u, m], bank[S_BANKS[m]][:, :N], ACT.Gelu_apprx_tanh,
                                                 bias=sb1c[:, m:m + 1]).then_inc(s_hr, 1)

                turns(act, turn)

            @block.vector
            def _(dve):
                def count(n):
                    nc.vector.tensor_scalar(flags[:], probsT[:], cand[:, 0:1].bitcast(F32), 0.0, ALU.is_ge, ALU.add,
                                            accum_out=cnt[:, 0:1]).then_inc(s_n, 1)

                def decide(n, k):
                    dve.wait_ge(s_tot, n + 1)
                    nc.vector.scalar_tensor_tensor(out=grow[:], in0=bank[4][:, 0:1], scalar=float(CAP),
                                                   in1=step[:, k:k + 1], op0=ALU.is_ge, op1=ALU.mult).then_inc(s_thr, 1)
                    dve.wait_ge(s_thr, 4 * n + 1)
                    nc.vector.scalar_tensor_tensor(out=cand[:], in0=grow[:], scalar=thr[:, 0:1],
                                                   in1=step[:, 1 - k:2 - k], op0=ALU.bitwise_or,
                                                   op1=ALU.bitwise_or).then_inc(s_thr, 1)
                    dve.wait_ge(s_thr, 4 * n + 2)
                    count(n + 1)
                    nc.vector.tensor_tensor(thr[:], thr[:], grow[:], ALU.bitwise_or).then_inc(s_thr, 1)
                    nc.vector.tensor_scalar(step[:, k:k + 1], step[:, 1 - k:2 - k], 1, None,
                                            ALU.logical_shift_right).then_inc(s_thr, 1)
                    dve.wait_ge(s_thr, 4 * n + 4)

                dve.wait_ge(s_c, 1)
                nc.vector.tensor_scalar(diff[:], diff[:], E - 1, None, ALU.bitwise_and).then_inc(s_i, 1)
                dve.wait_ge(s_i, 1)
                nc.vector.tensor_scalar(same[:], diff[:], 0.0, None, ALU.is_equal).then_inc(s_i, 1)
                nc.vector.memset(thr[:], 0).then_inc(s_i, 1)
                nc.vector.memset(cand[:], 1 << TOPBIT).then_inc(s_i, 1)
                nc.vector.memset(step[:, 0:1], 1 << TOPBIT).then_inc(s_i, 1)
                nc.vector.memset(step[:, 1:2], 1 << (TOPBIT - 1)).then_inc(s_i, 1)
                dve.wait_ge(s_i, 6)
                dve.wait_ge(s_pl, 16 * (B // 2))
                count(0)

                def turn(b, u):
                    if valid(b):
                        decide(2 * b, 0)
                    if valid(b - 2):
                        m = b - 2
                        dve.wait_ge(s_y, m + 1)
                        dve.wait_ge(s_hb, m + 1)
                        wait(dve, s_out[u], 16 * ((m - u) // 2) if isinstance(m, int) else 8 * (m - u))
                        nc.vector.tensor_tensor(oS[:, u], bank[2 + u][:PT_, :NT * C].rearrange(
                            "p (t c) -> p t c", c=C), Hall[:, m], ALU.add).then_inc(s_yr, 1)
                    if valid(b):
                        decide(2 * b + 1, 1)

                turns(dve, turn)

        mid.close()

        EW1 = sb("EW1", [128, 2, D])
        EW2 = sb("EW2", [128, 2, DC, C])
        EB1 = sb("EB1", [128, 2, DC])
        EB2 = sb("EB2", [PT_, 2, C])
        s_ew = [sem(f"s_expert_weights{u}") for u in range(2)]

        def load_expert(eng, e, u):
            eng.dma_start(EW1[:, u], ew1[e]).then_inc(s_ew[u], 16)
            eng.dma_start(EW2[:, u], ew2[e].rearrange("(k p) n -> p k n", p=128)).then_inc(s_ew[u], 16)
            eng.dma_start(EB1[:, u], eb1[e].rearrange("(m p) -> p m", p=128)).then_inc(s_ew[u], 16)
            eng.dma_start(EB2[:, u], eb2[e].rearrange("(o n) -> o n", o=1).broadcast_to([PT_, C])
                          ).then_inc(s_ew[u], 16)

        with ExitStack() as lst:
            def sb_(name, shape, dt=F32):
                return lst.enter_context(nc.sbuf_tensor(name, shape, dt))

            def sem(name):
                return lst.enter_context(nc.semaphore(name))

            TILES = T // PT_
            PAIRS = B // 2
            NSUB = 5
            SLOT = PT_ // NSUB
            NA = CAP // SLOT
            AW = 16
            COLS = TILES * PAIRS * E
            GE = 8
            NG = E // GE
            ROUND = 1.5 * 2.0 ** 23

            over = sb_("over", [128, 2 * N])
            tied = sb_("tied", [128, 2 * N])
            ties = sb_("ties", [128, 2 * N])
            room = sb_("room", [128, 2])
            chosen = sb_("chosen", [128, 2 * N])
            place = sb_("place", [128, 2 * N])
            ones_r = sb_("ones_r", [128, 2 * N])
            quot = sb_("quot", [PT_, COLS])
            fa = sb_("fa", [PT_, COLS], BF16)
            fb = sb_("fb", [PT_, COLS], BF16)
            pidx = sb_("pidx", [PT_, 1])
            hotA = sb_("hotA", [PT_, COLS, AW], BF16)
            hotB = sb_("hotB", [PT_, SLOT, COLS], BF16)
            diagi = sb_("diagi", [128, GE], I32)
            diag = sb_("diag", [128, GE])
            picked = sb_("picked", [128, NG, SLOT, GE])
            lists = sb_("lists", [128, NG, SLOT])
            listT = sb_("listT", [SLOT, E, AW])
            spread = sb_("spread", [SLOT, 2 * PT_ - SLOT])
            slots = sb_("slots", [128, N])
            ends = sb_("ends", [128, TILES])
            passed = sb_("passed", [128, N])
            tile_of = sb_("tile_of", [128, E])

            s_c = sem("s_pool_consts3")
            s_i = sem("s_dve_consts3")
            s_sel = sem("s_selection_steps")
            s_m = sem("s_selection_matmuls")
            s_hot = sem("s_onehot_steps")
            s_end = sem("s_passed_tiles_steps")

            HOT = 5 + NA + SLOT
            HOT_LISTS = HOT + NG + 1

            block = lst.enter_context(nc.Block())

            @block.sync
            def _(sp):
                for u in range(2):
                    load_expert(sp, u, u)

            @block.gpsimd
            def _(pool):
                nc.gpsimd.memset(ones_r[:], 1.0).then_inc(s_c, 1)
                nc.gpsimd.iota(pidx[:], pattern=[[0, 1]], base=0, channel_multiplier=1,
                               allow_small_or_imprecise_dtypes=True).then_inc(s_c, 1)
                nc.gpsimd.memset(hotA[:, :, NA:], 0.0).then_inc(s_c, 1)
                nc.gpsimd.iota(slots[:], pattern=[[1, N]], base=0, channel_multiplier=0,
                               allow_small_or_imprecise_dtypes=True).then_inc(s_c, 1)
                nc.gpsimd.iota(diagi[:], pattern=[[-AW, GE]], base=0, channel_multiplier=1).then_inc(s_c, 1)
                nc.gpsimd.memset(spread[:], 0.0).then_inc(s_c, 1)
                pool.wait_ge(s_c, 6)
                nc.gpsimd.affine_select(out=spread[:], in_=spread[:], compare_op=ALU.not_equal, fill=1.0,
                                        base=PT_ - SLOT, pattern=[[-1, 2 * PT_ - SLOT]],
                                        channel_multiplier=1).then_inc(s_c, 1)

            @block.tensor
            def _(pe):
                pe.wait_ge(s_sel, 2)
                nc.tensor.matmul(bank[5][:, 0:1], same[:], cnt[:, 1:2], start=True, stop=True)
                nc.tensor.matmul(bank[5][:, 1:2], before[:], cnt[:, 2:3], start=True, stop=True).then_inc(s_m, 1)
                pe.wait_ge(s_sel, 8)
                nc.tensor.matmul(bank[6][:, 0:1], before[:], place[:, 2 * N - 1:2 * N], start=True,
                                 stop=True).then_inc(s_m, 1)
                pe.wait_ge(s_sel, 9)
                for j in range(TILES):
                    last = nc.tensor.transpose(bank[j // 3][:PT_, (j % 3) * 128:(j % 3 + 1) * 128],
                                               chosen[:, j * PT_:(j + 1) * PT_], ident[:])
                last.then_inc(s_m, 1)
                pe.wait_ge(s_hot, HOT)
                pe.wait_ge(s_c, 3)

                def collect(j, first, final):
                    for pair in range(PAIRS):
                        for g in range(NG):
                            c0 = j * PAIRS * E + pair * E + g * GE
                            last = nc.tensor.matmul(bank[3 + g][:, 0:SLOT * GE], hotA2[:, bass.ds(c0 * AW, GE * AW)],
                                                    hotB[:, :, bass.ds(c0, GE)], start=first and pair == 0,
                                                    stop=final and pair == PAIRS - 1)
                    return last

                hotA2 = hotA[:].rearrange("p c a -> p (c a)")
                collect(0, True, False)
                with pe.Fori(1, TILES - 1) as j:
                    collect(j, False, False)
                collect(TILES - 1, False, True).then_inc(s_m, 1)
                pe.wait_ge(s_hot, HOT_LISTS)
                for g in range(NG):
                    last = nc.tensor.transpose(bank[5][:SLOT, g * 128:(g + 1) * 128], lists[:, g], ident[:])
                last.then_inc(s_m, 1)
                pe.wait_ge(s_hot, HOT_LISTS + 1)
                pe.wait_ge(s_c, 7)
                pe.wait_ge(s_i, 3)
                pe.wait_ge(s_end, TILES + 1)
                for a in range(NSUB):
                    at = PT_ - SLOT - a * SLOT
                    nc.tensor.matmul(bank[7][:PT_, :NT * E], spread[:, at:at + PT_],
                                     listT[:, :, a:NA:NSUB].rearrange("b e k -> b k e"),
                                     start=(a == 0), stop=False)
                for k in range(NT):
                    last = nc.tensor.matmul(bank[7][:PT_, k * E:(k + 1) * E], passed[:, k * PT_:(k + 1) * PT_],
                                            tile_of[:], start=False, stop=(k == NT - 1))
                last.then_inc(s_m, 1)

            @block.vector
            def _(dve):
                nc.vector.tensor_scalar(over[:], probsT[:], thr[:, 0:1].bitcast(F32), 0.0, ALU.is_gt, ALU.add,
                                        accum_out=cnt[:, 1:2]).then_inc(s_sel, 1)
                nc.vector.tensor_scalar(tied[:], probsT[:], thr[:, 0:1].bitcast(F32), 0.0, ALU.is_equal, ALU.add,
                                        accum_out=cnt[:, 2:3]).then_inc(s_sel, 1)
                dve.wait_ge(s_sel, 2)
                dve.wait_ge(s_c, 1)
                nc.vector.tensor_tensor_scan(ties[:], ones_r[:], tied[:], 0.0, ALU.mult, ALU.add).then_inc(s_sel, 1)
                dve.wait_ge(s_m, 1)
                nc.vector.tensor_scalar(room[:, 0:1], bank[5][:, 0:1], -1.0, float(CAP), ALU.mult,
                                        ALU.add).then_inc(s_sel, 1)
                dve.wait_ge(s_sel, 4)
                nc.vector.tensor_tensor(room[:, 1:2], room[:, 0:1], bank[5][:, 1:2], ALU.subtract).then_inc(s_sel, 1)
                dve.wait_ge(s_sel, 5)
                nc.vector.scalar_tensor_tensor(out=ties[:], in0=ties[:], scalar=room[:, 1:2], in1=tied[:],
                                               op0=ALU.is_le, op1=ALU.mult).then_inc(s_sel, 1)
                dve.wait_ge(s_sel, 6)
                nc.vector.tensor_tensor(chosen[:], over[:], ties[:], ALU.add).then_inc(s_sel, 1)
                dve.wait_ge(s_sel, 7)
                nc.vector.tensor_tensor_scan(place[:], ones_r[:], chosen[:], 0.0, ALU.mult, ALU.add).then_inc(s_sel, 1)
                dve.wait_ge(s_sel, 8)
                dve.wait_ge(s_m, 2)
                nc.vector.scalar_tensor_tensor(out=chosen[:], in0=place[:], scalar=bank[6][:, 0:1], in1=chosen[:],
                                               op0=ALU.add, op1=ALU.mult).then_inc(s_sel, 1)
                nc.vector.tensor_scalar(ends[:], place[:, PT_ - 1::PT_], bank[6][:, 0:1], None,
                                        ALU.add).then_inc(s_end, 1)
                dve.wait_ge(s_m, 3)
                for n in range(2):
                    nc.vector.tensor_scalar(quot[:, n * 384:(n + 1) * 384], bank[n][:PT_, :384], 1.0 / SLOT,
                                            -(1.0 + SLOT // 2) / SLOT, ALU.mult, ALU.add).then_inc(s_hot, 1)
                dve.wait_ge(s_hot, 2)
                nc.vector.tensor_scalar(fa[:], quot[:], ROUND, -ROUND, ALU.add, ALU.add).then_inc(s_hot, 1)
                dve.wait_ge(s_hot, 3)
                for n in range(2):
                    nc.vector.scalar_tensor_tensor(out=fb[:, n * 384:(n + 1) * 384], in0=fa[:, n * 384:(n + 1) * 384],
                                                   scalar=-float(SLOT), in1=bank[n][:PT_, :384], op0=ALU.mult,
                                                   op1=ALU.add).then_inc(s_hot, 1)
                dve.wait_ge(s_c, 2)
                for a in range(NA):
                    nc.vector.tensor_scalar(hotA[:, :, a], fa[:], float(a), pidx[:, 0:1], ALU.is_equal,
                                            ALU.mult).then_inc(s_hot, 1)
                dve.wait_ge(s_hot, 5)
                for b in range(SLOT):
                    nc.vector.tensor_scalar(hotB[:, b], fb[:], float(b + 1), None, ALU.is_equal).then_inc(s_hot, 1)
                dve.wait_ge(s_c, 5)
                nc.vector.tensor_scalar(diagi[:], diagi[:], 4, None, ALU.arith_shift_right).then_inc(s_i, 1)
                nc.vector.tensor_scalar(tile_of[:], same[:, 0:E], float(PT_), None, ALU.mult).then_inc(s_i, 1)
                dve.wait_ge(s_i, 1)
                nc.vector.tensor_scalar(diag[:], diagi[:], 0.0, None, ALU.is_equal).then_inc(s_i, 1)
                for j in range(TILES):
                    dve.wait_ge(s_end, j + 1)
                    if j == 0:
                        nc.vector.tensor_scalar(passed[:], slots[:], ends[:, 0:1], None, ALU.is_ge).then_inc(s_end, 1)
                    else:
                        nc.vector.scalar_tensor_tensor(out=passed[:], in0=slots[:], scalar=ends[:, j:j + 1],
                                                       in1=passed[:], op0=ALU.is_ge, op1=ALU.add).then_inc(s_end, 1)
                dve.wait_ge(s_i, 3)
                dve.wait_ge(s_m, 4)
                for g in range(NG):
                    nc.vector.tensor_tensor(picked[:, g], bank[3 + g][:, :SLOT * GE].rearrange(
                        "p (b e) -> p b e", e=GE), diag[:, None, :].broadcast_to([128, SLOT, GE]),
                        ALU.mult).then_inc(s_hot, 1)
                dve.wait_ge(s_hot, HOT_LISTS - 1)
                nc.vector.reduce_sum(lists[:].rearrange("p g b -> p (g b)"),
                                     picked[:].rearrange("p g b e -> p (g b) e"), AX_X).then_inc(s_hot, 1)
                dve.wait_ge(s_m, 5)
                nc.vector.tensor_copy(listT[:].rearrange("b e a -> b (e a)"), bank[5][:SLOT, :E * AW]
                                      ).then_inc(s_hot, 1)
                dve.wait_ge(s_m, 6)
                nc.vector.tensor_copy(idx[:].rearrange("p e k -> p k e"), bank[7][:PT_, :NT * E].rearrange(
                    "p (k e) -> p k e", e=E))

        with ExitStack() as four:
            def sb_(name, shape, dt=F32):
                return four.enter_context(nc.sbuf_tensor(name, shape, dt))

            def sem(name):
                return four.enter_context(nc.semaphore(name))

            H_BANKS = (0, 1, 4, 5)
            AHEAD = 3
            RING = 4

            ids = [[sb_(f"ids{r}_{k}", [PT_, 1], U32) for k in range(NT)] for r in range(RING)]
            tok = sb_("tok", [PT_, RING, NT, ROW])
            tokT = sb_("tokT", [128, 2, N])
            hE = sb_("hE", [128, 2, DC, N])
            score = sb_("score", [PT_, 2, NT])
            yE = sb_("yE", [PT_, 2, NT, C])

            s_id = sem("s_ids_ready")
            s_ga = [sem(f"s_tokens_gathered{r}") for r in range(RING)]
            s_tp = sem("s_tokT_in_psum")
            s_tc = sem("s_tokT_ready")
            s_scr = sem("s_scores_taken")
            s_h = sem("s_expert_h_in_psum")
            s_hr = sem("s_expert_h_ready")
            s_y = sem("s_expert_y_in_psum")
            s_yb = sem("s_expert_y_biased")
            s_ys = sem("s_expert_y_scored")
            s_sc = sem("s_scattered")
            s_on = [sem(f"s_waits_passed{n}") for n in range(2)]

            block = four.enter_context(nc.Block())

            def turns(eng, turn):
                turn(0)
                with eng.Fori(1, E // RING - 1) as i:
                    turn(i)
                turn(E // RING - 1)

            def exists(e):
                return not isinstance(e, int) or e < E

            @block.sync
            def _(sp):
                with sp.Fori(1, E // 2) as i:
                    for u in range(2):
                        sp.wait_ge(s_yb, 2 * i + u - 1)
                        load_expert(sp, 2 * i + u, u)

            @block.gpsimd
            def _(pool):
                def gather(e, r):
                    wait_apart(pool, s_id, e + 1, s_on[1])
                    for k in range(NT):
                        nc.gpsimd.indirect_dma_start(
                            out=tok[:, r, k], out_offset=None, in_=table,
                            in_offset=bass.IndirectOffsetOnAxis(ap=ids[r][k][:, 0:1], axis=0)).then_inc(s_ga[r], 16)

                def scatter(e, r):
                    pool.wait_ge(s_ys, NT * (e + 1))
                    wait_apart(pool, s_sc, 16 * NT * e, s_on[1])
                    for k in range(NT):
                        nc.gpsimd.indirect_dma_start(
                            out=out_rows, out_offset=bass.IndirectOffsetOnAxis(ap=ids[r][k][:, 0:1], axis=0),
                            in_=yE[:, r % 2, k], in_offset=None, compute_op=ALU.add,
                            bounds_check=TOK - 1, oob_is_err=True).then_inc(s_sc, 16)

                for e in range(AHEAD):
                    gather(e, e)

                def turn(i):
                    for r in range(RING):
                        e = RING * i + r
                        scatter(e, r)
                        if exists(e + AHEAD):
                            gather(e + AHEAD, (r + AHEAD) % RING)

                turns(pool, turn)
                pool.wait_ge(s_sc, 16 * NT * E)
                for r in range(RING):
                    pool.wait_ge(s_ga[r], 16 * NT * (E // RING))

            @block.tensor
            def _(pe):
                def transpose_tokens(e, r, turn):
                    pe.wait_ge(s_ga[r], 16 * NT * (turn + 1))
                    wait(pe, s_tc, e)
                    for k in range(NT):
                        last = nc.tensor.transpose(bank[6][:, k * PT_:(k + 1) * PT_], tok[:, r, k, 0:C],
                                                   ident[:PT_, :PT_])
                    last.then_inc(s_tp, 1)

                def turn(i):
                    for r in range(RING):
                        e, u = RING * i + r, r % 2
                        pe.wait_ge(s_ew[u], 16 * 4 * (2 * i + r // 2 + 1))
                        pe.wait_ge(s_tc, e + 1)
                        for m in range(DC):
                            nc.tensor.matmul(bank[H_BANKS[m]][:, :N], EW1[:, u, m * 128:(m + 1) * 128], tokT[:, u],
                                             start=True, stop=True).then_inc(s_h, 1)
                        if exists(e + 1):
                            transpose_tokens(e + 1, (r + 1) % RING, i + (r == RING - 1))
                        pe.wait_ge(s_hr, 4 * e + 4)
                        wait(pe, s_yb, e - 1)
                        for t in range(NT):
                            for k in range(DC):
                                last = nc.tensor.matmul(bank[2 + u][:PT_, t * C:(t + 1) * C],
                                                        hE[:, u, k, t * PT_:(t + 1) * PT_], EW2[:, u, k],
                                                        start=(k == 0), stop=(k == DC - 1))
                        last.then_inc(s_y, 1)

                transpose_tokens(0, 0, 0)
                turns(pe, turn)

            @block.scalar
            def _(act):
                def turn(i):
                    for r in range(RING):
                        e, u = RING * i + r, r % 2
                        for m in range(DC):
                            act.wait_ge(s_h, 4 * e + m + 1)
                            nc.scalar.activation(hE[:, u, m], bank[H_BANKS[m]][:, :N], ACT.Gelu_apprx_tanh,
                                                 bias=EB1[:, u, m:m + 1]).then_inc(s_hr, 1)

                turns(act, turn)

            @block.vector
            def _(dve):
                def take_ids(e, r):
                    for k in range(NT):
                        last = nc.vector.tensor_copy(ids[r][k][:], idx[:, e, k:k + 1])
                    last.then_inc(s_id, 1)

                def take_tokens(e, r):
                    dve.wait_ge(s_tp, e + 1)
                    nc.vector.tensor_copy(tokT[:, r % 2], bank[6][:, :N]).then_inc(s_tc, 1)
                    wait(dve, s_ys, NT * (e - 1))
                    nc.vector.tensor_copy(score[:, r % 2], tok[:, r, :, bass.ds(C + e, 1)].rearrange(
                        "p k o -> p (k o)")).then_inc(s_scr, 1)

                def turn(i):
                    for r in range(RING):
                        e, u = RING * i + r, r % 2
                        if exists(e + 1):
                            take_tokens(e + 1, (r + 1) % RING)
                        dve.wait_ge(s_y, e + 1)
                        dve.wait_ge(s_scr, e + 1)
                        wait(dve, s_sc, 16 * NT * (e - 1))
                        nc.vector.tensor_tensor(yE[:, u], bank[2 + u][:PT_, :NT * C].rearrange(
                            "p (t c) -> p t c", c=C), EB2[:, u, None, :].broadcast_to([PT_, NT, C]),
                            ALU.add).then_inc(s_yb, 1)
                        dve.wait_ge(s_yb, e + 1)
                        for k in range(NT):
                            nc.vector.tensor_scalar(yE[:, u, k], yE[:, u, k], score[:, u, k:k + 1], None,
                                                    ALU.mult).then_inc(s_ys, 1)
                        if exists(e + AHEAD):
                            wait(dve, s_sc, 16 * NT * e)
                            take_ids(e + AHEAD, (r + AHEAD) % RING)

                for e in range(AHEAD):
                    take_ids(e, e)
                take_tokens(0, 0)
                turns(dve, turn)


_INS = ['x', 'L0_tok_W1', 'L0_tok_b1', 'L0_tok_W2', 'L0_tok_b2', 'L0_tok_W3', 'L0_tok_b3', 'L0_attn_gamma',
        'L0_attn_beta', 'L0_attn_wq1', 'L0_attn_wqd', 'L0_attn_wk1', 'L0_attn_wkd', 'L0_attn_wv1', 'L0_attn_wvd',
        'L0_attn_wout', 'L0_ffn_gate_w', 'L0_ffn_w1', 'L0_ffn_b1', 'L0_ffn_w2', 'L0_ffn_b2', 'L0_ffn_sw1',
        'L0_ffn_sb1', 'L0_ffn_sw2', 'L0_ffn_sb2']
_OUTS = [((B, N, C), 'float32')]


def kernel(**inputs):
    import numpy as _np
    import concourse.bacc as _bacc
    from concourse import mybir as _mybir
    from concourse.bass_utils import run_bass_kernel_spmd as _run

    nc = _bacc.Bacc("TRN2", target_bir_lowering=False, num_devices=1)
    arrays, args = {}, []
    for name in _INS:
        a = _np.ascontiguousarray(inputs[name])
        arrays[f"in_{name}_dram"] = a
        args.append(nc.dram_tensor(f"in_{name}_dram", a.shape, _mybir.dt.from_np(a.dtype), kind="ExternalInput").ap())
    for i, (shape, dtype) in enumerate(_OUTS):
        dt = _mybir.dt.from_np(_np.dtype(dtype))
        args.append(nc.dram_tensor(f"out_{i}_dram", shape, dt, kind="ExternalOutput").ap())
    build(nc, *args)
    r = _run(nc, [arrays], core_ids=[0])
    got = tuple(r.results[0][f"out_{i}_dram"] for i in range(len(_OUTS)))
    return got[0]
```
